# Optimizing a Trainium2 kernel written in Bass

```python
import numpy as np
import jax
import jax.numpy as jnp

def _softmax(x, axis=-1):
    return jax.nn.softmax(x, axis=axis)

def _gelu(x):
    return jax.nn.gelu(x, approximate=True)

def _silu(x):
    return jax.nn.silu(x)

def _sigmoid(x):
    return jax.nn.sigmoid(x)

def _layernorm(x, axis=-1, eps=1e-05):
    m = jnp.mean(x, axis=axis, keepdims=True)
    v = jnp.var(x, axis=axis, keepdims=True)
    return (x - m) / jnp.sqrt(v + eps)

def _scatter_add(tgt, idx, src, axis=0):
    return tgt.at[idx].add(src)

def _segment_sum(src, seg, n):
    return jax.ops.segment_sum(src, seg, n)
kernel_name = 'mk_decoder_postln_d2_seqx_r8_8b4b5c'

def setup_inputs(seed: int=0):
    np.random.seed(seed)
    _w = jnp.asarray

    def _rec_inputs():
        import jax
        import jax.numpy as jnp
        _rk = jax.random.key(seed)
        x = -0.000125 + 0.9999 * jax.random.normal(jax.random.fold_in(_rk, 1), (4, 256, 256), jnp.float32)
        _lenS = 256 - jax.random.randint(jax.random.fold_in(_rk, 7), (4,), 0, max(1, 256 // 4) + 1, jnp.int32)
        _lenS2 = 64 - jax.random.randint(jax.random.fold_in(_rk, 8), (4,), 0, max(1, 64 // 4) + 1, jnp.int32)
        _ctx_2048P = jax.random.normal(jax.random.fold_in(_rk, 11), (4, 16, 256), jnp.float32)
        _ctx_2048c = jax.random.dirichlet(jax.random.fold_in(_rk, 511), 0.3 * jnp.ones((16,), jnp.float32), (4, 64))
        _ctx_2048t = jnp.einsum('bsk,bkd->bsd', _ctx_2048c, _ctx_2048P)
        _ctx_2048t = _ctx_2048t * jax.lax.rsqrt(jnp.mean(jnp.square(_ctx_2048t)) + 1e-12) * 0.953939
        ctx_2048 = 4.13588e-05 + 0.999923 * (_ctx_2048t + 0.3 * jax.random.normal(jax.random.fold_in(_rk, 611), (4, 64, 256), jnp.float32))
        return (x, ctx_2048)
    x, ctx_2048 = _rec_inputs()

    def _L0_attn_setup():
        import jax, jax.numpy as jnp
        import numpy as np
        N_HEAD = 16
        key = jax.random.key(seed)
        k1, k2, k3 = jax.random.split(key, 3)
        B, T, C = (4, 256, 256)
        x = jax.random.normal(k1, (B, T, C), dtype=jnp.float32)
        w_attn = jax.random.normal(k2, (C, 3 * C), dtype=jnp.float32) * 0.02
        b_attn = jnp.zeros((3 * C,), dtype=jnp.float32)
        w_proj = jax.random.normal(k3, (C, C), dtype=jnp.float32) * 0.02
        b_proj = jnp.zeros((C,), dtype=jnp.float32)
        return {'x': x, 'w_attn': w_attn, 'b_attn': b_attn, 'w_proj': w_proj, 'b_proj': b_proj}
    _L0_attn_all = _L0_attn_setup()
    _L0_attn_in = {k: v for k, v in _L0_attn_all.items() if k in ('w_attn', 'b_attn', 'w_proj', 'b_proj')}
    del _L0_attn_all

    def _L0_xattn_setup():
        import jax, jax.numpy as jnp
        import numpy as np
        D_MODEL = 256
        NUM_HEADS = 16
        HEAD_DIM = D_MODEL // NUM_HEADS
        key = jax.random.key(seed)
        ks = jax.random.split(key, 10)
        B, S, T = (4, 512, 128)
        s = 1.0 / np.sqrt(D_MODEL)
        inp = {'query': jax.random.normal(ks[0], (B, S, D_MODEL), jnp.float32), 'key_value': jax.random.normal(ks[1], (B, T, D_MODEL), jnp.float32), 'Wq': jax.random.normal(ks[2], (D_MODEL, D_MODEL), jnp.float32) * s, 'bq': jnp.zeros((D_MODEL,), jnp.float32), 'Wk': jax.random.normal(ks[3], (D_MODEL, D_MODEL), jnp.float32) * s, 'bk': jnp.zeros((D_MODEL,), jnp.float32), 'Wv': jax.random.normal(ks[4], (D_MODEL, D_MODEL), jnp.float32) * s, 'bv': jnp.zeros((D_MODEL,), jnp.float32), 'Wo': jax.random.normal(ks[5], (D_MODEL, D_MODEL), jnp.float32) * s, 'bo': jnp.zeros((D_MODEL,), jnp.float32)}
        return inp
    _L0_xattn_all = _L0_xattn_setup()
    _L0_xattn_in = {k: v for k, v in _L0_xattn_all.items() if k in ('Wq', 'bq', 'Wk', 'bk', 'Wv', 'bv', 'Wo', 'bo')}
    del _L0_xattn_all

    def _L0_ffn_setup():
        import jax, jax.numpy as jnp
        import numpy as np
        B, T, D = (2, 128, 256)
        E, F, K = (64, 64, 4)
        S, HS = (2, 64 * 4)
        key = jax.random.key(seed)
        ks = jax.random.split(key, 9)
        s = 0.02
        f32 = jnp.float32
        return {'x': jax.random.normal(ks[0], (B, T, D), f32), 'router_w': jax.random.normal(ks[1], (D, E), f32) * s, 'router_bias': jnp.zeros((E,), f32), 'wg': jax.random.normal(ks[2], (E, D, F), f32) * s, 'wu': jax.random.normal(ks[3], (E, D, F), f32) * s, 'wd': jax.random.normal(ks[4], (E, F, D), f32) * s, 'swg': jax.random.normal(ks[5], (S, D, HS), f32) * s, 'swu': jax.random.normal(ks[6], (S, D, HS), f32) * s, 'swd': jax.random.normal(ks[7], (S, HS, D), f32) * s}
    _L0_ffn_all = _L0_ffn_setup()
    _L0_ffn_in = {k: v for k, v in _L0_ffn_all.items() if k in ('router_w', 'router_bias', 'wg', 'wu', 'wd', 'swg', 'swu', 'swd')}
    del _L0_ffn_all

    def _L1_attn_setup():
        import jax, jax.numpy as jnp
        import numpy as np
        N_HEADS = 16
        NEG = -10000.0
        key = jax.random.key(seed)
        k1, k2, k3 = jax.random.split(key, 3)
        B, S, E = (4, 256, 256)
        x = jax.random.normal(k1, (B, S, E), dtype=jnp.float32)
        w_qkv = jax.random.normal(k2, (E, 3 * E), dtype=jnp.float32) * E ** (-0.5)
        w_out = jax.random.normal(k3, (E, E), dtype=jnp.float32) * E ** (-0.5)
        return {'x': x, 'w_qkv': w_qkv, 'w_out': w_out}
    _L1_attn_all = _L1_attn_setup()
    _L1_attn_in = {k: v for k, v in _L1_attn_all.items() if k in ('w_qkv', 'w_out')}
    del _L1_attn_all

    def _L1_xattn_setup():
        import jax, jax.numpy as jnp
        import numpy as np
        D_MODEL = 256
        NUM_HEADS = 16
        HEAD_DIM = D_MODEL // NUM_HEADS

        def _fq_sym(x, axis):
            s = jnp.max(jnp.abs(x), axis=axis, keepdims=True) / 127.0
            s = jnp.maximum(s, 1e-08)
            q = jnp.clip(jnp.round(x / s), -127.0, 127.0) * s
            return x + jax.lax.stop_gradient(q - x)

        def _fq_unsigned(x, axis):
            s = jnp.max(x, axis=axis, keepdims=True) / 255.0
            s = jnp.maximum(s, 1e-08)
            q = jnp.clip(jnp.round(x / s), 0.0, 255.0) * s
            return x + jax.lax.stop_gradient(q - x)
        key = jax.random.key(seed)
        ks = jax.random.split(key, 8)
        B, N, M, C = (2, 256, 64, D_MODEL)
        return {'x': jax.random.normal(ks[0], (B, N, C), jnp.float32), 'cond': jax.random.normal(ks[1], (B, M, C), jnp.float32), 'Wq': jax.random.normal(ks[2], (C, C), jnp.float32) * 0.02, 'bq': jnp.zeros((C,), jnp.float32), 'Wkv': jax.random.normal(ks[3], (C, 2 * C), jnp.float32) * 0.02, 'bkv': jnp.zeros((2 * C,), jnp.float32), 'Wp': jax.random.normal(ks[4], (C, C), jnp.float32) * 0.02, 'bp': jnp.zeros((C,), jnp.float32)}
    _L1_xattn_all = _L1_xattn_setup()
    _L1_xattn_in = {k: v for k, v in _L1_xattn_all.items() if k in ('Wq', 'bq', 'Wkv', 'bkv', 'Wp', 'bp')}
    del _L1_xattn_all

    def _L1_ffn_setup():
        import jax, jax.numpy as jnp
        import numpy as np
        B, S, D, M, E, K = (4, 256, 256, 512, 8, 2)

        def _routed_moe(x, gate_w, w0, w1, wo):
            T = x.shape[0]
            logits = jnp.einsum('td,de->te', x, gate_w)
            top_logits, top_idx = jax.lax.top_k(logits, K)
            top_w = jax.nn.softmax(top_logits, axis=-1)
            cw = jnp.zeros((T, E), dtype=x.dtype).at[jnp.arange(T)[:, None], top_idx].add(top_w)
            out = jnp.zeros_like(x)
            for e in range(E):
                h = jax.nn.silu(x @ w0[e]) * (x @ w1[e])
                out = out + cw[:, e:e + 1] * (h @ wo[e])
            return out
        key = jax.random.key(seed)
        ks = jax.random.split(key, 5)
        inputs = jax.random.normal(ks[0], (B, S, D), dtype=jnp.float32)
        gate_w = jax.random.normal(ks[1], (D, E), dtype=jnp.float32) * D ** (-0.5)
        w0 = jax.random.normal(ks[2], (E, D, M), dtype=jnp.float32) * D ** (-0.5)
        w1 = jax.random.normal(ks[3], (E, D, M), dtype=jnp.float32) * D ** (-0.5)
        wo = jax.random.normal(ks[4], (E, M, D), dtype=jnp.float32) * M ** (-0.5)
        decoder_segment_ids = jax.random.randint(jax.random.fold_in(key, 1), (B, S), 0, 2).astype(jnp.int32)
        decoder_positions = jnp.tile(jnp.arange(S, dtype=jnp.int32)[None, :], (B, 1))
        return {'inputs': inputs, 'gate_w': gate_w, 'w0': w0, 'w1': w1, 'wo': wo, 'decoder_segment_ids': decoder_segment_ids, 'decoder_positions': decoder_positions}
    _L1_ffn_all = _L1_ffn_setup()
    _L1_ffn_in = {k: v for k, v in _L1_ffn_all.items() if k in ('gate_w', 'w0', 'w1', 'wo', 'decoder_segment_ids', 'decoder_positions')}
    del _L1_ffn_all
    return {'x': x, 'ctx_2048': ctx_2048, 'L0_attn_w_attn': _L0_attn_in['w_attn'], 'L0_attn_b_attn': _L0_attn_in['b_attn'], 'L0_attn_w_proj': _L0_attn_in['w_proj'], 'L0_attn_b_proj': _L0_attn_in['b_proj'], 'L0_xattn_Wq': _L0_xattn_in['Wq'], 'L0_xattn_bq': _L0_xattn_in['bq'], 'L0_xattn_Wk': _L0_xattn_in['Wk'], 'L0_xattn_bk': _L0_xattn_in['bk'], 'L0_xattn_Wv': _L0_xattn_in['Wv'], 'L0_xattn_bv': _L0_xattn_in['bv'], 'L0_xattn_Wo': _L0_xattn_in['Wo'], 'L0_xattn_bo': _L0_xattn_in['bo'], 'L0_ffn_router_w': _L0_ffn_in['router_w'], 'L0_ffn_router_bias': _L0_ffn_in['router_bias'], 'L0_ffn_wg': _L0_ffn_in['wg'], 'L0_ffn_wu': _L0_ffn_in['wu'], 'L0_ffn_wd': _L0_ffn_in['wd'], 'L0_ffn_swg': _L0_ffn_in['swg'], 'L0_ffn_swu': _L0_ffn_in['swu'], 'L0_ffn_swd': _L0_ffn_in['swd'], 'L1_attn_w_qkv': _L1_attn_in['w_qkv'], 'L1_attn_w_out': _L1_attn_in['w_out'], 'L1_xattn_Wq': _L1_xattn_in['Wq'], 'L1_xattn_bq': _L1_xattn_in['bq'], 'L1_xattn_Wkv': _L1_xattn_in['Wkv'], 'L1_xattn_bkv': _L1_xattn_in['bkv'], 'L1_xattn_Wp': _L1_xattn_in['Wp'], 'L1_xattn_bp': _L1_xattn_in['bp'], 'L1_ffn_gate_w': _L1_ffn_in['gate_w'], 'L1_ffn_w0': _L1_ffn_in['w0'], 'L1_ffn_w1': _L1_ffn_in['w1'], 'L1_ffn_wo': _L1_ffn_in['wo'], 'L1_ffn_decoder_segment_ids': _L1_ffn_in['decoder_segment_ids'], 'L1_ffn_decoder_positions': _L1_ffn_in['decoder_positions']}

def reference(x, ctx_2048, L0_attn_w_attn, L0_attn_b_attn, L0_attn_w_proj, L0_attn_b_proj, L0_xattn_Wq, L0_xattn_bq, L0_xattn_Wk, L0_xattn_bk, L0_xattn_Wv, L0_xattn_bv, L0_xattn_Wo, L0_xattn_bo, L0_ffn_router_w, L0_ffn_router_bias, L0_ffn_wg, L0_ffn_wu, L0_ffn_wd, L0_ffn_swg, L0_ffn_swu, L0_ffn_swd, L1_attn_w_qkv, L1_attn_w_out, L1_xattn_Wq, L1_xattn_bq, L1_xattn_Wkv, L1_xattn_bkv, L1_xattn_Wp, L1_xattn_bp, L1_ffn_gate_w, L1_ffn_w0, L1_ffn_w1, L1_ffn_wo, L1_ffn_decoder_segment_ids, L1_ffn_decoder_positions):
    import jax
    import jax.numpy as jnp

    def _L0_attn_ref(x, w_attn, b_attn, w_proj, b_proj):
        import jax, jax.numpy as jnp
        import numpy as np
        N_HEAD = 16
        B, T, C = x.shape
        H = N_HEAD
        D = C // H
        qkv = x @ w_attn + b_attn
        q, k, v = jnp.split(qkv, 3, axis=-1)
        q = q.reshape(B, T, H, D).transpose(0, 2, 1, 3)
        k = k.reshape(B, T, H, D).transpose(0, 2, 1, 3)
        v = v.reshape(B, T, H, D).transpose(0, 2, 1, 3)
        att = jnp.einsum('bhqd,bhkd->bhqk', q, k) * (1.0 / jnp.sqrt(jnp.float32(D)))
        causal = jnp.tril(jnp.ones((T, T), dtype=bool))
        att = jnp.where(causal[None, None], att, jnp.float32(-jnp.inf))
        att = jax.nn.softmax(att, axis=-1)
        y = jnp.einsum('bhqk,bhkd->bhqd', att, v)
        y = y.transpose(0, 2, 1, 3).reshape(B, T, C)
        return y @ w_proj + b_proj

    def _L0_xattn_ref(query, key_value, Wq, bq, Wk, bk, Wv, bv, Wo, bo):
        import jax, jax.numpy as jnp
        import numpy as np
        D_MODEL = 256
        NUM_HEADS = 16
        HEAD_DIM = D_MODEL // NUM_HEADS
        B, S, _ = query.shape
        T = key_value.shape[1]
        Q = query @ Wq.T + bq
        K = key_value @ Wk.T + bk
        V = key_value @ Wv.T + bv
        Q = Q.reshape(B, S, NUM_HEADS, HEAD_DIM).transpose(0, 2, 1, 3)
        K = K.reshape(B, T, NUM_HEADS, HEAD_DIM).transpose(0, 2, 1, 3)
        V = V.reshape(B, T, NUM_HEADS, HEAD_DIM).transpose(0, 2, 1, 3)
        scale = 1.0 / np.sqrt(HEAD_DIM).astype(np.float32)
        scores = jnp.einsum('bhsd,bhtd->bhst', Q, K) * scale
        attn = jax.nn.softmax(scores, axis=-1)
        ctx = jnp.einsum('bhst,bhtd->bhsd', attn, V)
        ctx = ctx.transpose(0, 2, 1, 3).reshape(B, S, D_MODEL)
        return ctx @ Wo.T + bo

    def _L0_ffn_ref(x, router_w, router_bias, wg, wu, wd, swg, swu, swd):
        import jax, jax.numpy as jnp
        import numpy as np
        B, T, D = (2, 128, 256)
        E, F, K = (64, 64, 4)
        S, HS = (2, 64 * 4)
        b, t, d = x.shape
        flat = x.reshape(b * t, d)
        n = flat.shape[0]
        logits = flat @ router_w
        scores = jax.nn.softmax(logits, axis=-1)
        _, topk_idx = jax.lax.top_k(logits + router_bias, K)
        topk_scores = jnp.take_along_axis(scores, topk_idx, axis=-1)
        topk_scores = topk_scores / topk_scores.sum(axis=-1, keepdims=True)
        comb = jnp.zeros((n, E), dtype=flat.dtype).at[jnp.arange(n)[:, None], topk_idx].set(topk_scores)
        g = jax.nn.silu(jnp.einsum('nd,edf->nef', flat, wg))
        u = jnp.einsum('nd,edf->nef', flat, wu)
        routed = jnp.einsum('ne,nef,efd->nd', comb, g * u, wd)
        sg = jax.nn.silu(jnp.einsum('nd,sdh->nsh', flat, swg))
        su = jnp.einsum('nd,sdh->nsh', flat, swu)
        shared = jnp.einsum('nsh,shd->nd', sg * su, swd)
        return (routed + shared).reshape(b, t, d)

    def _L1_attn_ref(x, w_qkv, w_out):
        import jax, jax.numpy as jnp
        import numpy as np
        N_HEADS = 16
        NEG = -10000.0
        B, S, E = x.shape
        H = N_HEADS
        D = E // H
        qkv = x @ w_qkv
        q, k, v = jnp.split(qkv, 3, axis=-1)
        q = q.reshape(B, H, S, D)
        k = k.reshape(B, H, S, D)
        v = v.reshape(B, H, S, D)
        qk = jnp.einsum('bhqd,bhkd->bhqk', q, k) / D ** 0.5
        tri = jnp.tril(jnp.ones((S, S), dtype=bool))
        causal = jnp.where(tri, jnp.float32(1.0), jnp.float32(NEG))
        qk = qk + causal
        attn = jax.nn.softmax(qk, axis=-1)
        o = jnp.einsum('bhqk,bhkd->bhqd', attn, v)
        o = o.reshape(B, S, E)
        return o @ w_out

    def _L1_xattn_ref(x, cond, Wq, bq, Wkv, bkv, Wp, bp):
        import jax, jax.numpy as jnp
        import numpy as np
        D_MODEL = 256
        NUM_HEADS = 16
        HEAD_DIM = D_MODEL // NUM_HEADS

        def _fq_sym(x, axis):
            s = jnp.max(jnp.abs(x), axis=axis, keepdims=True) / 127.0
            s = jnp.maximum(s, 1e-08)
            q = jnp.clip(jnp.round(x / s), -127.0, 127.0) * s
            return x + jax.lax.stop_gradient(q - x)

        def _fq_unsigned(x, axis):
            s = jnp.max(x, axis=axis, keepdims=True) / 255.0
            s = jnp.maximum(s, 1e-08)
            q = jnp.clip(jnp.round(x / s), 0.0, 255.0) * s
            return x + jax.lax.stop_gradient(q - x)
        B, N, C = x.shape
        H, hd = (NUM_HEADS, HEAD_DIM)
        q = (x @ Wq + bq).reshape(1, B * N, H, hd)
        kv = (cond @ Wkv + bkv).reshape(1, -1, 2, H, hd)
        k, v = (kv[:, :, 0], kv[:, :, 1])
        scale = 1.0 / np.sqrt(hd).astype(np.float32)
        q = jnp.transpose(q * scale, (0, 2, 1, 3))
        k = jnp.transpose(k, (0, 2, 1, 3))
        v = jnp.transpose(v, (0, 2, 1, 3))
        q = _fq_sym(q, axis=-1)
        k = _fq_sym(k, axis=-1)
        v = _fq_sym(v, axis=2)
        attn = jnp.einsum('bhqd,bhkd->bhqk', q, k)
        attn = jax.nn.softmax(attn.astype(jnp.float32), axis=-1)
        attn = _fq_unsigned(attn, axis=-1)
        out = jnp.einsum('bhqk,bhkd->bhqd', attn, v)
        out = jnp.transpose(out, (0, 2, 1, 3)).reshape(B, N, C)
        return out @ Wp + bp

    def _L1_ffn_ref(inputs, gate_w, w0, w1, wo, decoder_segment_ids, decoder_positions):
        import jax, jax.numpy as jnp
        import numpy as np
        B, S, D, M, E, K = (4, 256, 256, 512, 8, 2)

        def _routed_moe(x, gate_w, w0, w1, wo):
            T = x.shape[0]
            logits = jnp.einsum('td,de->te', x, gate_w)
            top_logits, top_idx = jax.lax.top_k(logits, K)
            top_w = jax.nn.softmax(top_logits, axis=-1)
            cw = jnp.zeros((T, E), dtype=x.dtype).at[jnp.arange(T)[:, None], top_idx].add(top_w)
            out = jnp.zeros_like(x)
            for e in range(E):
                h = jax.nn.silu(x @ w0[e]) * (x @ w1[e])
                out = out + cw[:, e:e + 1] * (h @ wo[e])
            return out
        b, s, d = inputs.shape
        x = inputs.reshape(b * s, d)
        out = _routed_moe(x, gate_w, w0, w1, wo)
        return out.reshape(b, s, d)
    x = _layernorm(x + _L0_attn_ref(x, L0_attn_w_attn, L0_attn_b_attn, L0_attn_w_proj, L0_attn_b_proj), axis=-1)
    x = _layernorm(x + _L0_xattn_ref(x, ctx_2048, L0_xattn_Wq, L0_xattn_bq, L0_xattn_Wk, L0_xattn_bk, L0_xattn_Wv, L0_xattn_bv, L0_xattn_Wo, L0_xattn_bo), axis=-1)
    x = _layernorm(x + _L0_ffn_ref(x, L0_ffn_router_w, L0_ffn_router_bias, L0_ffn_wg, L0_ffn_wu, L0_ffn_wd, L0_ffn_swg, L0_ffn_swu, L0_ffn_swd), axis=-1)
    x = _layernorm(x + _L1_attn_ref(x, L1_attn_w_qkv, L1_attn_w_out), axis=-1)
    x = _layernorm(x + _L1_xattn_ref(x, ctx_2048, L1_xattn_Wq, L1_xattn_bq, L1_xattn_Wkv, L1_xattn_bkv, L1_xattn_Wp, L1_xattn_bp), axis=-1)
    x = _layernorm(x + _L1_ffn_ref(x, L1_ffn_gate_w, L1_ffn_w0, L1_ffn_w1, L1_ffn_wo, L1_ffn_decoder_segment_ids, L1_ffn_decoder_positions), axis=-1)
    return x

_drawn_inputs = setup_inputs


def setup_inputs(seed=0):
    import zlib

    import numpy as np

    out = dict(_drawn_inputs(seed))
    spreads = {'L0_attn_b_attn': (0.0, 0.1),
     'L0_attn_b_proj': (0.0, 0.1),
     'L0_xattn_bq': (0.0, 0.1),
     'L0_xattn_bk': (0.0, 2.0),
     'L0_xattn_bv': (0.0, 0.1),
     'L0_xattn_bo': (0.0, 0.1),
     'L0_ffn_router_bias': (0.0, 0.63),
     'L1_xattn_bq': (0.0, 2.0),
     'L1_xattn_bkv': (0.0, 0.1),
     'L1_xattn_bp': (0.0, 0.1)}
    factors = {'L0_ffn_router_w': 5.273, 'L0_ffn_wu': 3.059, 'L0_ffn_wd': 3.192, 'L1_xattn_Wq': 8.0}
    for name, (base, spread) in spreads.items():
        noise = np.random.default_rng([zlib.crc32(name.encode()), seed]).standard_normal(out[name].shape)
        drawn = base * np.exp(spread * noise) if base else spread * noise
        out[name] = jnp.asarray(drawn.astype(out[name].dtype))
    for name, factor in factors.items():
        out[name] = (out[name] * factor).astype(out[name].dtype)
    return out
```

```python
import concourse.bass as bass
from concourse import mybir
from contextlib import ExitStack

BATCH, SEQ, DIM = 4, 256, 256
CTX = 64
HEADS, HEAD_DIM = 16, 16
TILE = 128
TILES = BATCH * SEQ // TILE
CHUNKS = DIM // TILE
GROUPS = HEADS // 4
SCALE = HEAD_DIM ** -0.5
EPS = 1e-5
RSQRT_SEED = 1597463007.0

C_IDENT, C_CAUSAL, C_TRI, C_HEADMASK, C_PARITY, C_HALF, C_ROW, C_IOTA = 0, 128, 256, 384, 388, 390, 391, 392
C_CAUSAL1 = C_IOTA + 64
C_COLS = C_CAUSAL1 + 2 * SEQ
ROUND = 1.5 * 2 ** 23
LEVELS, PROB_LEVELS = 127.0, 255.0


class Moe:
    def __init__(self, experts, picks, hidden, stage):
        self.experts, self.picks, self.hidden, self.stage = experts, picks, hidden, stage
        self.tiles = BATCH * SEQ * picks // TILE + experts
        assert self.tiles % 4 == 0


MOE0, MOE1 = Moe(64, 4, 64, 0), Moe(8, 2, 512, 1)
SHARED_HIDDEN = 512

W_ATTN = {"L0_attn_w_attn": 0, "L0_attn_w_proj": 0, "L0_xattn_Wq": 1, "L0_xattn_Wk": 1, "L0_xattn_Wv": 1,
          "L0_xattn_Wo": 1, "L1_attn_w_qkv": 2, "L1_attn_w_out": 2,
          "L1_xattn_Wq": 3, "L1_xattn_Wkv": 3, "L1_xattn_Wp": 3}
BIAS_COL = {"L0_attn_b_attn": 0, "L0_xattn_bq": 1, "L0_xattn_bk": 1, "L0_xattn_bv": 1, "L1_xattn_bkv": 3}
BIAS_ROW = {"L0_attn_b_proj": 0, "L0_xattn_bo": 1, "L1_xattn_bq": 3, "L1_xattn_bk_row": 3, "L1_xattn_bp": 3}


def decoder_kernel(nc: bass.Bass, t: dict, out: bass.AP, stages: int = 99):
    f32, bf16, f16 = mybir.dt.float32, mybir.dt.bfloat16, mybir.dt.float16
    i32, u32 = mybir.dt.int32, mybir.dt.uint32
    ALU, ACT, AX = mybir.AluOpType, mybir.ActivationFunctionType, mybir.AxisListType

    with ExitStack() as ctx:
        def sb(name, shape, dt=f32):
            return ctx.enter_context(nc.sbuf_tensor(name, shape, dt))

        def sem(name):
            return ctx.enter_context(nc.semaphore(name))

        bank = [ctx.enter_context(nc.psum_tensor(f"bank{i}", [128, 512], f32)) for i in range(8)]
        X_BANK, Q_BANK, K_BANK, V_BANK = 0, 1, 2, 3
        S_BANKS, PT_BANKS, PV_BANK, BACK_BANK, PROJ_BANK = (4, 5, 0), (6, 7), 2, 3, 6

        class Carver:
            def __init__(self, region):
                self.region, self.at = region, 0

            def __call__(self, *shape, dt=None):
                n = 1
                for k in shape:
                    n *= k
                v = self.region[:, self.at:self.at + n]
                self.at += n
                assert self.at <= self.region.shape[1], self.at
                if dt is not None:
                    v = v.bitcast(dt)
                if len(shape) > 1:
                    names = "abcd"[:len(shape)]
                    v = v.rearrange(f"p ({' '.join(names)}) -> p {' '.join(names)}",
                                    **{k: x for k, x in zip(names[1:], shape[1:])})
                return v

        x_res = sb("x_res", [128, TILES, DIM])
        const = sb("const", [128, C_CAUSAL1])
        ident = const[:, C_IDENT:C_IDENT + 128]
        head_mask = const[:, C_HEADMASK:C_HEADMASK + 4]
        parity = const[:, C_PARITY:C_PARITY + 2]
        ident_h = sb("ident_h", [128, 128], f16)
        ident_b = sb("ident_b", [128, 128], bf16)
        causal_b = sb("causal_b", [128, 128], bf16)
        causal_h = sb("causal_h", [128, 2, SEQ], f16)
        tri_b = sb("tri_b", [128, 128], bf16)
        ones_b = sb("ones_b", [128, 128], bf16)
        ones_f = sb("ones_f", [128, 128])
        iota_e = const[:, C_IOTA:C_IOTA + 64]
        zeros = sb("zeros", [128, DIM])
        y_acc = sb("y_acc", [128, TILES, DIM])
        expert_in = sb("expert_in", [128, 16384])
        expert_out = sb("expert_out", [128, 8192])
        neg_max = sb("neg_max", [128, HEADS, 2])
        row_sum = sb("row_sum", [128, HEADS, 2])
        row_inv = sb("row_inv", [128, HEADS, 2])
        spacer = sb("spacer", [128, 1])
        stats = sb("stats", [128, TILES, 6])
        mean_var = sb("mean_var", [128, TILES, 2])
        rs_bits = sb("rs_bits", [128, TILES], i32)
        rs_y, rs_t, rs_v = sb("rs_y", [128, TILES]), sb("rs_t", [128, TILES]), sb("rs_v", [128, TILES])
        qbias = [sb(f"qbias{i}", [128, 2]) for i in range(2)]
        tile_expert = sb("tile_expert", [128, 2, 128], i32)
        tile_half = sb("tile_half", [128, 128])
        pos_f = sb("pos_f", [128, 32])
        pos = sb("pos", [128, 32], u32)
        pick_w = sb("pick_w", [128, TILES, 4])

        w_region = sb("w_region", [128, 7800])
        w_in, bias_col, bias_row = {}, {}, {}
        for layer in range(2):
            cut = Carver(w_region)
            for n in W_ATTN:
                if n.startswith(f"L{layer}"):
                    w_in[n] = cut(CHUNKS, t[n].shape[-1])
            for n in BIAS_COL:
                if n.startswith(f"L{layer}"):
                    bias_col[n] = cut(t[n].shape[1])
            for n in BIAS_ROW:
                if n.startswith(f"L{layer}"):
                    bias_row[n] = cut(t[n].shape[0])
            if layer == 0:
                shared_in = [cut(CHUNKS, SHARED_HIDDEN) for _ in range(2)]
                shared_out = cut(SHARED_HIDDEN // 128, DIM)

        work = sb("work", [128, 14400])
        cut = Carver(work)
        xb = cut(2, DIM)
        xbo = cut(2, DIM)
        xT = cut(CHUNKS, SEQ)
        qT = cut(CHUNKS, SEQ)
        kT = cut(CHUNKS, SEQ)
        kTm = cut(CHUNKS, 4, SEQ)
        v32 = cut(2, HEADS, 32)
        probs = [cut(512) for i in range(3)]
        probsT = [cut(512) for i in range(2)]
        oT4 = [cut(SEQ) for i in range(2)]
        o_tok = cut(2, DIM)
        oT = cut(CHUNKS, SEQ)
        resid = cut(2, DIM)
        dup_at = cut.at
        ctx_tok = cut(2, DIM)
        ctxT = cut(CHUNKS, BATCH * CTX)
        ctxT2 = cut(CHUNKS, BATCH, 2, CTX)
        ckT = cut(CHUNKS, BATCH * CTX)
        cv = cut(BATCH, DIM)
        cut.at = dup_at + 2 * DIM + CHUNKS * BATCH * CTX
        q_tok, k_tok, v_tok = [cut(2, DIM) for _ in range(3)]
        dup = [cut(HEADS, 2, HEAD_DIM) for _ in range(2)]
        vT = cut(CHUNKS, SEQ)
        cut.at = work.shape[1] - 512
        causal_f = cut(512)
        cut.at = dup_at + 2 * DIM + CHUNKS * BATCH * CTX
        q_int, k_int = [cut(2, DIM) for _ in range(2)]
        q_scale, k_scale = [cut(2, HEADS) for _ in range(2)]
        inv_scale = cut(2, HEADS)
        v_scale, v_inv = cut(CHUNKS), cut(CHUNKS)
        shift = cut(HEADS, 2)
        vq = cut(CHUNKS, SEQ)
        p_shifted = [cut(512)]
        probsT_b = [p[:, 0:256].bitcast(bf16) for p in probsT]
        v32_b = v32.rearrange("p i h d -> p (i h d)")[:, 0:512].bitcast(bf16)            .rearrange("p (i h d) -> p i h d", i=2, h=HEADS)
        cut.at = 0
        silu_s = [oT4[0], oT4[1]]
        hidden_s = kTm[:, 0]
        cut = Carver(work)
        logits = resid.rearrange("p i (t e) -> p (i t) e", e=64)
        biased = cut(TILES, 64)
        expw = cut(TILES, 64)
        onehot = cut(32, 64)
        product = cut(32, 64)
        slot_base = cut(TILES, 64)
        top8 = cut(TILES, 8)
        top8_i = cut(TILES, 8, dt=u32)
        top_f = cut(32)
        row_t = [cut(TILES) for _ in range(3)]
        picked = cut(TILES, 4)
        counts = [cut(64) for _ in range(5)]
        counts_i = [cut(64, dt=i32) for _ in range(2)]
        e_col = [cut(1) for _ in range(2)]
        e_diag = cut(128)
        e_par = cut(128, dt=i32)
        mask_b = cut(TILES * 32, dt=bf16).rearrange("p (i e) -> p i e", i=TILES)
        cut = Carver(work)
        xg = [cut(DIM) for _ in range(4)]
        xgT = [cut(CHUNKS, TILE) for _ in range(2)]
        silu_g = [cut(512) for _ in range(2)]
        hid = [cut(512) for _ in range(2)]
        hidT = [cut(512) for _ in range(2)]
        y_tile = [cut(DIM) for _ in range(4)]
        y_pick = [cut(DIM) for _ in range(8)]

        sorted_x = [nc.dram_tensor(f"sorted_x{m.stage}", (m.tiles * TILE, DIM), f32).ap() for m in (MOE0, MOE1)]
        sorted_y = [nc.dram_tensor(f"sorted_y{m.stage}", (m.tiles * TILE, DIM), f32).ap() for m in (MOE0, MOE1)]

        const_loaded, const_ready, x_loaded, ctx_loaded, stored = map(
            sem, ("const_loaded", "const_ready", "x_loaded", "ctx_loaded", "stored"))
        CONSTS = 6
        w_loaded = [sem(f"w_loaded{i}") for i in range(4)]
        LOADS = [16 * sum(v == i for d in (W_ATTN, BIAS_COL, BIAS_ROW) for v in d.values()) for i in range(4)]

        class Signals:
            by_dma = ("sent", "loaded", "stored", "fetched")

            def __init__(self, sems, before=None):
                self.sems = sems
                self.before = before or {n: 0 if n in self.by_dma else 1 for n in sems}

            def __getitem__(self, name):
                return self.sems[name]

            def __call__(self, name, n, buf=None):
                done = self.before[name]
                s = self.sems[name] if buf is None else self.sems[name][buf]
                return s, n + done if done else n

            def after(self, counts):
                return Signals(self.sems, {n: self.before[n] + counts.get(n, 0) for n in self.sems})

        once = ("xb_ready", "xbo_ready", "xT_psum", "xT_ready", "q_psum", "k_psum", "v_psum", "q_ready", "k_ready",
                "km_ready", "v_ready", "oT_psum", "oT_ready", "proj_psum", "x_ready")
        per_group = ("ot_ready", "back_psum", "o_ready")
        per_head = ("s_psum", "max_ready", "shift_ready", "p_ready", "pT_psum", "pT_ready", "pv_psum")

        def attention_counts(n, never):
            c = {**{k: BATCH for k in once}, **{k: BATCH * GROUPS for k in per_group}, **{k: BATCH * n for k in per_head}}
            return {k: v for k, v in c.items() if k not in never}

        SELF0 = Signals({n: sem(f"att_{n}") for n in once + per_group + per_head})
        CROSS0 = SELF0.after(attention_counts(HEADS, ("shift_ready",)))
        SELF1 = CROSS0.after(attention_counts(GROUPS, ("k_psum", "v_psum", "k_ready", "max_ready")))
        CROSS1 = SELF1.after(attention_counts(HEADS, ("shift_ready", "q_ready", "oT_psum")))

        per_batch = ("xb_ready", "xT_psum", "xT_ready", "logit_psum", "logit_ready", "y_init", "sum_psum")
        shared = ("g_psum", "silu_ready", "hid_ready")
        single = ("mask_ready", "exp_in", "exp_ready", "rank_psum", "e_ready", "e_psum", "routed", "x_ready")
        per_tile = ("t_psum", "t_ready", "gu_psum", "act_ready", "h_ready", "hT_psum", "hT_ready", "y_psum", "y_copied")
        rows0 = TILES * MOE0.picks
        moe_sems = {n: sem(f"ffn_{n}") for n in per_batch + shared + single + per_tile + ("sent", "summed")}
        moe_sems["loaded"] = [sem(f"ffn_loaded{i}") for i in range(4)]
        moe_sems["stored"] = [sem(f"ffn_stored{i}") for i in range(4)]
        moe_sems["fetched"] = [sem(f"ffn_fetched{i}") for i in range(8)]
        FFN0 = Signals(moe_sems)
        FFN1 = FFN0.after({**{n: BATCH for n in per_batch}, **{n: BATCH * SHARED_HIDDEN // 128 for n in shared},
                           **{n: 1 for n in single}, **{n: MOE0.tiles for n in per_tile},
                           "sent": 16 * rows0, "summed": rows0, "loaded": 16 * MOE0.tiles // 4,
                           "stored": 16 * MOE0.tiles // 4, "fetched": 16 * rows0 // 8})
        steps = {n: sem(f"{n}_step") for n in ("self0", "cross0", "ffn0", "self1", "kv1", "cross1", "ffn1")}
        zero_filled, shared_loaded = sem("zero_filled"), sem("shared_loaded")
        expert_loaded = [sem("expert_loaded0"), sem("expert_loaded1")]
        router_loaded = [sem("router_loaded0"), sem("router_loaded1")]
        router_w = [sb(f"router_w{m.stage}", [128, CHUNKS, m.experts]) for m in (MOE0, MOE1)]
        router_bias = sb("router_bias", [128, 64])
        QKV1 = Signals({n: sem(f"self1_{n}") for n in ("tok_ready", "qkv_ready", "vT_psum")})
        kv1_sems = {n: sem(f"kv1_{n}") for n in ("k_psum", "v_psum", "k_ready", "kT_psum", "kT_ready", "vq_ready", "vT_psum",
                                                 "v_ready", "zeroed")}
        ctx_sems = {n: sem(f"ctx_{n}") for n in ("T_psum", "T_ready", "k_psum", "v_psum", "k_ready", "v_ready", "zeroed", "step")}
        zeroed = sem("zeroed")
        LAST = (None, SELF0, CROSS0, FFN0, SELF1, CROSS1, FFN1)[min(stages, 6)]

        block = ctx.enter_context(nc.Block())

        class Steps:
            def __init__(self, eng, s, turn, steps):
                self.eng, self.s, self.steps, self.n = eng, s, steps, 0
                self.base = turn * steps if steps else 0

            def __call__(self, ins):
                self.n += 1
                ins.then_inc(self.s, 1)
                self.eng.wait_ge(self.s, self.base + self.n)

            def done(self):
                assert self.n == self.steps, self.n

        def head_rows(h):
            r = (h % 8) // 4 * 64
            return slice(r, r + 64), h // 8, h % 4

        @block.sync
        def _(sp):
            def tile_traffic(sp, moe, S):
                def load(j, u):
                    sp.dma_start(xg[u], sorted_x[moe.stage][bass.ds(j * TILE, TILE), :]).then_inc(S["loaded"][u], 16)

                def turn(j, u, load_next=True, store_last=True):
                    if load_next:
                        sp.wait_ge(*S("t_psum", j + 1))
                        load(j + 4, u)
                    if store_last:
                        v = (u + 1) % 4
                        sp.wait_ge(*S("y_copied", j - 2))
                        sp.dma_start(sorted_y[moe.stage][bass.ds((j - 3) * TILE, TILE), :], y_tile[v])\
                          .then_inc(S["stored"][v], 16)

                sp.wait_ge(*S("sent", 16 * TILES * moe.picks))
                for u in range(4):
                    load(u, u)
                for u in range(4):
                    turn(u, u, store_last=u == 3)
                with sp.Fori(1, moe.tiles // 4 - 1) as q:
                    for u in range(4):
                        turn(q * 4 + u, u)
                for j in range(moe.tiles - 4, moe.tiles + 3):
                    turn(j, j % 4, load_next=False)

            sp.dma_start(const[:], t["const"][:, 0:C_CAUSAL1]).then_inc(const_loaded, 16)
            sp.dma_start(causal_f, t["const"][:, C_CAUSAL1:C_COLS]).then_inc(const_loaded, 16)
            sp.dma_start(x_res[:], t["x"].rearrange("(i p) d -> p i d", p=128)).then_inc(x_loaded, 16)
            def attention_weights(lot):
                for n in W_ATTN:
                    if W_ATTN[n] == lot:
                        sp.dma_start(w_in[n], t[n].rearrange("(c p) n -> p c n", p=128)).then_inc(w_loaded[lot], 16)
                for n in BIAS_COL:
                    if BIAS_COL[n] == lot:
                        sp.dma_start(bias_col[n], t[n]).then_inc(w_loaded[lot], 16)
                for n in BIAS_ROW:
                    if BIAS_ROW[n] == lot:
                        sp.dma_start(bias_row[n], t[n].partition_broadcast(128)).then_inc(w_loaded[lot], 16)

            attention_weights(0)
            sp.dma_start(ctx_tok[:], t["ctx_2048"].rearrange("(i p) d -> p i d", p=128)).then_inc(ctx_loaded, 16)
            attention_weights(1)
            sp.dma_start(router_w[0][:], t["L0_ffn_router_w"].rearrange("(c p) n -> p c n", p=128)).then_inc(router_loaded[0], 16)
            sp.dma_start(router_bias[:], t["L0_ffn_router_bias"].partition_broadcast(128)).then_inc(router_loaded[0], 16)
            sp.dma_start(router_w[1][:], t["L1_ffn_gate_w"].rearrange("(c p) n -> p c n", p=128)).then_inc(router_loaded[1], 16)
            for w, n in ((shared_in[0], "L0_ffn_swg"), (shared_in[1], "L0_ffn_swu"), (shared_out, "L0_ffn_swd")):
                sp.dma_start(w, t[n].rearrange("(c p) n -> p c n", p=128)).then_inc(shared_loaded, 16)
            sp.wait_ge(zeroed, 1)
            for m in (MOE0, MOE1):
                z = sorted_x[m.stage].rearrange("(p r) d -> p r d", p=128)
                for r in range(0, m.tiles, 8):
                    sp.dma_start(z[:, r:r + 8, :], zeros[:].unsqueeze(1).to_broadcast([128, 8, DIM])).then_inc(zero_filled, 16)
            for q in range(4):
                sp.dma_start(expert_in[:, q * 4096:(q + 1) * 4096], t["expert_in0"][:, q * 4096:(q + 1) * 4096])\
                  .then_inc(expert_loaded[0], 16)
            for q in range(2):
                sp.dma_start(expert_out[:, q * 4096:(q + 1) * 4096], t["expert_out0"][:, q * 4096:(q + 1) * 4096])\
                  .then_inc(expert_loaded[0], 16)
            if stages >= 3:
                if stages >= 4:
                    sp.wait_ge(*FFN0("sum_psum", BATCH))
                    attention_weights(2)
                    attention_weights(3)
                tile_traffic(sp, MOE0, FFN0)
            if stages >= 4:
                sp.wait_ge(*FFN0("y_psum", MOE0.tiles))
                for q in range(4):
                    sp.dma_start(expert_in[:, q * 4096:(q + 1) * 4096], t["expert_in1"][:, q * 4096:(q + 1) * 4096])\
                      .then_inc(expert_loaded[1], 16)
                for q in range(2):
                    sp.dma_start(expert_out[:, q * 4096:(q + 1) * 4096], t["expert_out1"][:, q * 4096:(q + 1) * 4096])\
                      .then_inc(expert_loaded[1], 16)
            if stages >= 6:
                tile_traffic(sp, MOE1, FFN1)
            sp.wait_ge(*LAST("x_ready", 1 if LAST in (FFN0, FFN1) else BATCH))
            sp.dma_start(out.rearrange("(i p) d -> p i d", p=128), x_res[:]).then_inc(stored, 16)
            sp.wait_ge(stored, 16)

        @block.tensor
        def _(pe):
            mm, tr = nc.tensor.matmul, nc.tensor.transpose

            def transposes(dst, src):
                for kc in range(CHUNKS):
                    for i in range(2):
                        last = tr(dst[:, kc * 256 + i * 128:kc * 256 + (i + 1) * 128],
                                  src[:, i, kc * 128:(kc + 1) * 128], ident)
                return last

            def features_out(dst, w, c0, src):
                for c in range(CHUNKS):
                    for kc in range(CHUNKS):
                        last = mm(dst[:, c * 256:(c + 1) * 256], w[:, kc, c0 + c * 128:c0 + (c + 1) * 128],
                                  src[:, kc, :], start=kc == 0, stop=kc == CHUNKS - 1)
                return last

            def tokens_out(dst, src, w, c0):
                for i in range(2):
                    for kc in range(CHUNKS):
                        last = mm(dst[:, i * 256:(i + 1) * 256], src[:, kc, i * 128:(i + 1) * 128],
                                  w[:, kc, c0:c0 + DIM], start=kc == 0, stop=kc == CHUNKS - 1)
                return last

            def transpose_in(S, b):
                pe.wait_ge(*S("xb_ready", b + 1))
                transposes(bank[X_BANK], xb).then_inc(S["xT_psum"], 1)
                pe.wait_ge(*S("xT_ready", b + 1))

            def back_to_tokens(S, b, g):
                pe.wait_ge(*S("ot_ready", b * GROUPS + g + 1))
                pe.wait_ge(*S("o_ready", b * GROUPS + g))
                for i in range(2):
                    last = tr(bank[BACK_BANK][:, i * 128:(i + 1) * 128], oT4[g % 2][:, i * 128:(i + 1) * 128], ident)
                last.then_inc(S["back_psum"], 1)

            def project_out(S, b, wo):
                pe.wait_ge(*S("o_ready", (b + 1) * GROUPS))
                transposes(bank[X_BANK], o_tok).then_inc(S["oT_psum"], 1)
                pe.wait_ge(*S("oT_ready", b + 1))
                tokens_out(bank[PROJ_BANK], oT, wo, 0).then_inc(S["proj_psum"], 1)

            pe.wait_ge(const_ready, CONSTS)
            pe.wait_ge(w_loaded[0], LOADS[0])
            S = SELF0
            with pe.Fori(0, BATCH) as b:
                transpose_in(S, b)
                W = w_in["L0_attn_w_attn"]
                features_out(bank[Q_BANK], W, 0, xT).then_inc(S["q_psum"], 1)
                features_out(bank[K_BANK], W, DIM, xT).then_inc(S["k_psum"], 1)
                tokens_out(bank[V_BANK], xT, W, 2 * DIM).then_inc(S["v_psum"], 1)
                pe.wait_ge(*S("q_ready", b + 1))
                pe.wait_ge(*S("km_ready", b + 1))
                pe.wait_ge(*S("v_ready", b + 1))
                for i in range(HEADS + 4):
                    if i < HEADS:
                        rr, c, m = head_rows(i)
                        if i >= 3:
                            pe.wait_ge(*S("p_ready", b * HEADS + i - 2))
                        s = bank[S_BANKS[i % 3]]
                        mm(s[:, 0:128], qT[rr, c, 0:128], kTm[rr, c, m, 0:128], start=True, stop=False)
                        mm(s[:, 0:128], ident_b[:], causal_b[:], start=False, stop=True)
                        mm(s[:, 128:384], qT[rr, c, 128:256], kTm[rr, c, m, :], start=True, stop=False)
                        mm(s[:, 256:384], ident_b[:], causal_b[:], start=False, stop=True).then_inc(S["s_psum"], 1)
                    if 2 <= i < HEADS + 2:
                        h = i - 2
                        pe.wait_ge(*S("p_ready", b * HEADS + h + 1))
                        if h >= 2:
                            pe.wait_ge(*S("pT_ready", b * HEADS + h - 1))
                        elif h == 0:
                            pe.wait_ge(*S("x_ready", b))
                        for j in range(3):
                            last = tr(bank[PT_BANKS[h % 2]][:, j * 128:(j + 1) * 128],
                                      probs[h % 3][:, j * 128:(j + 1) * 128], ident)
                        last.then_inc(S["pT_psum"], 1)
                    if 3 <= i < HEADS + 3:
                        h = i - 3
                        if h % 4 == 0:
                            pe.wait_ge(*S("ot_ready", b * GROUPS + h // 4))
                        pe.wait_ge(*S("pT_ready", b * HEADS + h + 1))
                        o, m = bank[PV_BANK], slice(32 * (h % 4), 32 * (h % 4) + 32)
                        mm(o[m, 0:256], v32[:, 0, h, :], probsT[h % 2][:, 0:256], start=True, stop=False)
                        mm(o[m, 128:256], v32[:, 1, h, :], probsT[h % 2][:, 256:384], start=False, stop=True)\
                            .then_inc(S["pv_psum"], 1)
                    if i >= 7 and i % 4 == 3:
                        back_to_tokens(S, b, i // 4 - 1)
                project_out(S, b, w_in["L0_attn_w_proj"])
            if stages == 1:
                return

            pe.wait_ge(w_loaded[1], LOADS[1])
            pe.wait_ge(ctx_loaded, 16)
            pe.wait_ge(*SELF0("x_ready", BATCH))
            transposes(bank[X_BANK], ctx_tok).then_inc(ctx_sems["T_psum"], 1)
            pe.wait_ge(ctx_sems["T_ready"], 2)
            features_out(bank[K_BANK], w_in["L0_xattn_Wk"], 0, ctxT).then_inc(ctx_sems["k_psum"], 1)
            for bb in range(BATCH):
                for kc in range(CHUNKS):
                    last = mm(bank[4 + bb // 2][:, bb % 2 * 256:bb % 2 * 256 + 256],
                              ctxT2[:, kc, bb].rearrange("p a k -> p (a k)"), w_in["L0_xattn_Wv"][:, kc, :],
                              start=kc == 0, stop=kc == 1)
            last.then_inc(ctx_sems["v_psum"], 1)
            pe.wait_ge(ctx_sems["k_ready"], 1)
            pe.wait_ge(ctx_sems["v_ready"], 1)
            S = CROSS0
            with pe.Fori(0, BATCH) as b:
                transpose_in(S, b)
                features_out(bank[Q_BANK], w_in["L0_xattn_Wq"], 0, xT).then_inc(S["q_psum"], 1)
                pe.wait_ge(*S("q_ready", b + 1))
                pe.wait_ge(*S("km_ready", b + 1))
                pe.wait_ge(*S("v_ready", b + 1))
                for i in range(GROUPS + 4):
                    if i < GROUPS:
                        rr, c, _ = head_rows(4 * i)
                        if i == 3:
                            pe.wait_ge(*S("shift_ready", b * GROUPS + 1))
                        for j in range(2):
                            last = mm(bank[S_BANKS[i % 3]][:, j * 256:(j + 1) * 256], qT[rr, c, j * 128:(j + 1) * 128],
                                      kTm[rr, c, :, 0:CTX], start=True, stop=True)
                        last.then_inc(S["s_psum"], 1)
                    if 2 <= i < GROUPS + 2:
                        g = i - 2
                        pe.wait_ge(*S("p_ready", b * GROUPS + g + 1))
                        if g >= 2:
                            pe.wait_ge(*S("pT_ready", b * GROUPS + g - 1))
                        elif g == 0:
                            pe.wait_ge(*S("x_ready", b))
                        for pair in range(2):
                            for j in range(2):
                                last = tr(bank[PT_BANKS[g % 2]][:, pair * 256 + j * 128:pair * 256 + (j + 1) * 128],
                                          probs[g % 3][:, j * 256 + pair * 128:j * 256 + (pair + 1) * 128], ident)
                        last.then_inc(S["pT_psum"], 1)
                    if 3 <= i < GROUPS + 3:
                        g = i - 3
                        pe.wait_ge(*S("ot_ready", b * GROUPS + g))
                        pe.wait_ge(*S("pT_ready", b * GROUPS + g + 1))
                        for m in range(4):
                            last = mm(bank[PV_BANK][32 * m:32 * m + 32, 0:256], v32[:, 0, 4 * g + m, :],
                                      probsT[g % 2][:, m // 2 * 256:m // 2 * 256 + 256], start=True, stop=True)
                        last.then_inc(S["pv_psum"], 1)
                    if i >= 4:
                        back_to_tokens(S, b, i - 4)
                project_out(S, b, w_in["L0_xattn_Wo"])
            if stages == 2:
                return

            def router(S, moe, b, last_stage):
                transpose_in(S, b)
                pe.wait_ge(*S("logit_ready", b))
                for i in range(2):
                    for kc in range(CHUNKS):
                        last = mm(bank[K_BANK][:, i * 64:i * 64 + moe.experts], xT[:, kc, i * 128:(i + 1) * 128],
                                  router_w[moe.stage][:, kc, :], start=kc == 0, stop=kc == 1)
                last.then_inc(S["logit_psum"], 1)

            def count_tokens(S, moe):
                E = moe.experts
                pe.wait_ge(*S("mask_ready", 1))
                m = mask_b[:, :, 0:E]
                r = bank[0][:, 0:TILES * E].rearrange("p (i e) -> p i e", i=TILES)
                mm(r, tri_b[:], m, start=True, stop=False)
                for d in range(1, TILES):
                    mm(r[:, d:TILES], ones_b[:], m[:, 0:TILES - d], start=False, stop=d == TILES - 1)
                for i in range(TILES):
                    last = mm(bank[1][:, 0:E], ones_b[:], m[:, i], start=i == 0, stop=i == TILES - 1)
                last.then_inc(S["rank_psum"], 1)
                pe.wait_ge(*S("e_ready", 1))
                mm(bank[2][:, 0:128], ones_f[:], e_diag, start=True, stop=True).then_inc(S["e_psum"], 1)

            def expert_tiles(S, moe):
                H = moe.hidden
                small = moe is MOE0
                w_gu = expert_in[:].rearrange("p (e c n) -> p e c n", e=moe.experts, c=CHUNKS)
                w_d = expert_out[:].rearrange("p (e c n) -> p e c n", n=DIM, c=1 if small else H // 128)
                PEe = [mybir.EngineType.PE]

                def experts(row, j, n):
                    src = tile_expert[0:1, row, bass.ds(j, n)]
                    _, v = nc.values_load_multi_w_load_instructions(
                        src, engines=PEe, min_val=0, max_val=(moe.experts - 1) >> row,
                        skip_runtime_bounds_check_because="routing clamps them to the experts there are")
                    return v

                def turn(j, u, e_gu, e_d, first=True, second=True, third=True, fourth=True):
                    if first:
                        pe.wait_ge(*S("loaded", 16 * (j // 4 + 1) if isinstance(j, int) else j4_loads, u))
                        for kc in range(CHUNKS):
                            last = tr(bank[u % 2][:, kc * 128:(kc + 1) * 128], xg[u][:, kc * 128:(kc + 1) * 128], ident)
                        last.then_inc(S["t_psum"], 1)
                    if second:
                        a = (u + 1) % 2
                        pe.wait_ge(*S("t_ready", j))
                        for n in range(1 if small else 2):
                            for kc in range(CHUNKS):
                                dst = bank[2 + a + 2 * n][:, 0:(2 * H if small else H)]
                                w = w_gu[:, bass.ds(e_gu, 1), kc, :] if small else \
                                    w_gu[:, bass.ds(e_gu, 1), kc, n * H:(n + 1) * H]
                                last = mm(dst, xgT[a][:, kc, :], w, start=kc == 0, stop=kc == 1)
                        last.then_inc(S["gu_psum"], 1)
                    if third:
                        pe.wait_ge(*S("h_ready", j - 1))
                        if fourth:
                            pe.wait_ge(*S("hT_ready", j - 2))
                        for n in range(1 if small else 4):
                            last = tr(bank[6][:, n * 128:(n + 1) * 128], hid[u % 2][:, n * 128:(n + 1) * 128], ident)
                        last.then_inc(S["hT_psum"], 1)
                    if fourth:
                        a = (u + 1) % 2
                        pe.wait_ge(*S("hT_ready", j - 2))
                        pe.wait_ge(*S("y_copied", j - 3))
                        n_k = 1 if small else 4
                        for n in range(n_k):
                            last = mm(bank[7][:, 0:DIM], hidT[a][:, n * 128:(n + 1) * 128], w_d[:, bass.ds(e_d, 1), n, :],
                                      start=n == 0, stop=n == n_k - 1)
                        last.then_inc(S["y_psum"], 1)

                row_d = 1 if small else 0
                pe.wait_ge(*S("routed", 1))
                pe.wait_ge(expert_loaded[moe.stage], 16 * 6)
                ev, ed = experts(0, 0, 4), experts(row_d, 0, 4)
                for j in range(4):
                    turn(j, j, ev[j - 1] if j else None, ed[j - 3] if j == 3 else None,
                         second=j >= 1, third=j >= 2, fourth=j >= 3)
                with pe.Fori(1, moe.tiles // 4) as q:
                    j = q * 4
                    ev, ed = experts(0, j - 1, 4), experts(row_d, j - 3, 4)
                    j4_loads = j * 4 + 16
                    for u in range(4):
                        turn(j + u, u, ev[u], ed[u])
                ev, ed = experts(0, moe.tiles - 1, 1), experts(row_d, moe.tiles - 3, 3)
                for u in range(3):
                    turn(moe.tiles + u, u, ev[0], ed[u], first=False, second=u == 0, third=u <= 1)

            S = FFN0
            pe.wait_ge(router_loaded[0], 32)
            pe.wait_ge(shared_loaded, 48)
            pe.wait_ge(*CROSS0("x_ready", BATCH))
            with pe.Fori(0, BATCH) as b:
                router(S, MOE0, b, CROSS0)
                n_h = SHARED_HIDDEN // 128
                for hc in range(n_h):
                    if hc >= 2:
                        pe.wait_ge(*S("hid_ready", b * n_h + hc - 1))
                    for n in range(2):
                        for kc in range(CHUNKS):
                            last = mm(bank[4 + hc % 2][:, n * 256:(n + 1) * 256], shared_in[n][:, kc, hc * 128:(hc + 1) * 128],
                                      xT[:, kc, :], start=kc == 0, stop=kc == 1)
                    last.then_inc(S["g_psum"], 1)
                pe.wait_ge(*S("hid_ready", (b + 1) * n_h))
                pe.wait_ge(*S("y_init", b))
                for i in range(2):
                    for hc in range(n_h):
                        last = mm(bank[PROJ_BANK][:, i * 256:(i + 1) * 256], hidden_s[:, hc, i * 128:(i + 1) * 128],
                                  shared_out[:, hc, :], start=hc == 0, stop=hc == n_h - 1)
                last.then_inc(S["sum_psum"], 1)
            count_tokens(S, MOE0)
            expert_tiles(S, MOE0)
            if stages == 3:
                return

            def full_heads(S, b, quantised):
                vv, pT = (v32_b, probsT_b) if quantised else (v32, probsT)
                for i in range(HEADS + 4):
                    if i < HEADS:
                        rr, c, m = head_rows(i)
                        if i >= 3:
                            pe.wait_ge(*S("p_ready", b * HEADS + i - 2))
                        for j in range(2):
                            s = bank[S_BANKS[i % 3]][:, j * SEQ:(j + 1) * SEQ]
                            last = mm(s, qT[rr, c, j * 128:(j + 1) * 128], kTm[rr, c, m, :], start=True, stop=quantised)
                            if not quantised:
                                last = mm(s, ident_h[:], causal_h[:, j, :], start=False, stop=True)
                        last.then_inc(S["s_psum"], 1)
                    if 2 <= i < HEADS + 2:
                        h = i - 2
                        pe.wait_ge(*S("p_ready", b * HEADS + h + 1))
                        if h >= 2:
                            pe.wait_ge(*S("pT_ready", b * HEADS + h - 1))
                        elif h == 0:
                            pe.wait_ge(*S("x_ready", b))
                        for kt in range(2):
                            for j in range(2):
                                last = tr(bank[PT_BANKS[h % 2]][:, kt * SEQ + j * 128:kt * SEQ + (j + 1) * 128],
                                          probs[h % 3][:, j * SEQ + kt * 128:j * SEQ + (kt + 1) * 128], ident)
                        last.then_inc(S["pT_psum"], 1)
                    if 3 <= i < HEADS + 3:
                        h = i - 3
                        if h % 4 == 0:
                            pe.wait_ge(*S("ot_ready", b * GROUPS + h // 4))
                        pe.wait_ge(*S("pT_ready", b * HEADS + h + 1))
                        m = slice(32 * (h % 4), 32 * (h % 4) + 32)
                        for kt in range(2):
                            last = mm(bank[PV_BANK][m, 0:SEQ], vv[:, kt, h, :], pT[h % 2][:, kt * SEQ:(kt + 1) * SEQ],
                                      start=kt == 0, stop=kt == 1)
                        last.then_inc(S["pv_psum"], 1)
                    if i >= 7 and i % 4 == 3:
                        back_to_tokens(S, b, i // 4 - 1)

            pe.wait_ge(w_loaded[2], LOADS[2])
            pe.wait_ge(*FFN0("x_ready", 1))
            S = SELF1
            with pe.Fori(0, BATCH) as b:
                transpose_in(S, b)
                for n, (bk, done) in enumerate(((Q_BANK, "q_psum"), (K_BANK, "k_psum"), (V_BANK, "v_psum"))):
                    tokens_out(bank[bk], xT, w_in["L1_attn_w_qkv"], n * DIM).then_inc(S[done], 1)
                pe.wait_ge(*QKV1("qkv_ready", b * 3 + 3))
                for st in range(2):
                    for c in range(CHUNKS):
                        last = tr(bank[X_BANK][:, st * 256 + c * 128:st * 256 + (c + 1) * 128],
                                  vT[:, c, st * 128:(st + 1) * 128], ident)
                last.then_inc(QKV1["vT_psum"], 1)
                pe.wait_ge(*S("km_ready", b + 1))
                pe.wait_ge(*S("v_ready", b + 1))
                full_heads(S, b, False)
                pe.wait_ge(*S("oT_ready", b + 1))
                tokens_out(bank[PROJ_BANK], oT, w_in["L1_attn_w_out"], 0).then_inc(S["proj_psum"], 1)
            if stages == 4:
                return

            pe.wait_ge(w_loaded[3], LOADS[3])
            pe.wait_ge(*SELF1("x_ready", BATCH))
            Wkv = w_in["L1_xattn_Wkv"]
            tokens_out(bank[K_BANK], ctxT, Wkv, 0).then_inc(kv1_sems["k_psum"], 1)
            features_out(bank[V_BANK], Wkv, DIM, ctxT).then_inc(kv1_sems["v_psum"], 1)
            pe.wait_ge(kv1_sems["k_ready"], 1)
            transposes(bank[X_BANK], k_int).then_inc(kv1_sems["kT_psum"], 1)
            pe.wait_ge(kv1_sems["vq_ready"], 1)
            for st in range(2):
                for c in range(CHUNKS):
                    last = tr(bank[Q_BANK][:, st * 256 + c * 128:st * 256 + (c + 1) * 128],
                              vq[:, c, st * 128:(st + 1) * 128], ident)
            last.then_inc(kv1_sems["vT_psum"], 1)
            pe.wait_ge(kv1_sems["v_ready"], 1)
            S = CROSS1
            pe.wait_ge(*S("km_ready", 1))
            with pe.Fori(0, BATCH) as b:
                transpose_in(S, b)
                tokens_out(bank[Q_BANK], xT, w_in["L1_xattn_Wq"], 0).then_inc(S["q_psum"], 1)
                pe.wait_ge(*S("k_ready", b + 1))
                transposes(bank[K_BANK], q_int).then_inc(S["k_psum"], 1)
                pe.wait_ge(*S("q_ready", b + 1))
                full_heads(S, b, True)
                project_out(S, b, w_in["L1_xattn_Wp"])
            if stages == 5:
                return

            S = FFN1
            pe.wait_ge(*CROSS1("x_ready", BATCH))
            pe.wait_ge(router_loaded[1], 16)
            with pe.Fori(0, BATCH) as b:
                router(S, MOE1, b, CROSS1)
            count_tokens(S, MOE1)
            expert_tiles(S, MOE1)

        @block.scalar
        def _(act):
            A = nc.scalar.activation

            def copy_in(S, b):
                act.wait_ge(*S("xT_psum", b))
                act.wait_ge(*S("xbo_ready", b))
                A(xb, x_res[:, bass.ds(b * 2, 2), :], ACT.Copy).then_inc(S["xb_ready"], 1)
                act.wait_ge(*S("xT_psum", b + 1))
                A(xT[:].rearrange("p c n -> p (c n)"), bank[X_BANK][:], ACT.Copy).then_inc(S["xT_ready"], 1)

            def query_out(S, b, bias):
                act.wait_ge(*S("q_psum", b + 1))
                for c in range(CHUNKS):
                    last = A(qT[:, c, :], bank[Q_BANK][:, c * 256:(c + 1) * 256], ACT.Identity,
                             bias=bias[:, c:c + 1], scale=SCALE)
                last.then_inc(S["q_ready"], 1)

            def group_out(S, b, g, done):
                act.wait_ge(*S("pv_psum", done))
                if g >= 2:
                    act.wait_ge(*S("back_psum", b * GROUPS + g - 1))
                A(oT4[g % 2][:], bank[PV_BANK][:, 0:256], ACT.Copy).then_inc(S["ot_ready"], 1)

            def outputs_T(S, b, bias):
                act.wait_ge(*S("oT_psum", b + 1))
                for c in range(CHUNKS):
                    last = A(oT[:, c, :], bank[X_BANK][:, c * 256:(c + 1) * 256], ACT.Identity, bias=bias[:, c:c + 1])
                last.then_inc(S["oT_ready"], 1)

            act.wait_ge(x_loaded, 16)
            act.wait_ge(w_loaded[0], LOADS[0])
            act.wait_ge(const_ready, CONSTS)
            S = SELF0
            with act.Fori(0, BATCH) as b:
                copy_in(S, b)
                query_out(S, b, qbias[0])
                act.wait_ge(*S("v_psum", b + 1))
                for i in range(2):
                    last = A(v32[:, i, :, 0:HEAD_DIM],
                             bank[V_BANK][:, i * 256:(i + 1) * 256].rearrange("p (h d) -> p h d", d=HEAD_DIM), ACT.Copy)
                last.then_inc(S["v_ready"], 1)
                for h in range(HEADS + 3):
                    if h < HEADS:
                        act.wait_ge(*S("max_ready", b * HEADS + h + 1))
                        if h >= 3:
                            act.wait_ge(*S("pT_psum", b * HEADS + h - 2))
                        for i, c0, c1 in ((0, 0, 128), (1, 128, 384)):
                            last = A(probs[h % 3][:, c0:c1], bank[S_BANKS[h % 3]][:, c0:c1], ACT.Exp,
                                     bias=neg_max[:, h, i:i + 1], accum_out=row_sum[:, h, i:i + 1])
                        last.then_inc(S["p_ready"], 1)
                    if h >= 6 and h % 4 == 2:
                        group_out(S, b, h // 4 - 1, b * HEADS + h - 2)
                outputs_T(S, b, bias_col["L0_attn_b_attn"][:, 4:6])
            if stages == 1:
                return

            act.wait_ge(w_loaded[1], LOADS[1])
            act.wait_ge(*SELF0("x_ready", BATCH))
            act.wait_ge(ctx_sems["T_psum"], 1)
            A(ctxT[:].rearrange("p c n -> p (c n)"), bank[X_BANK][:], ACT.Copy).then_inc(ctx_sems["T_ready"], 1)
            for a in range(2):
                last = A(ctxT2[:, :, :, a, :], bank[X_BANK][:].rearrange("p (c b k) -> p c b k", c=2, b=4), ACT.Copy)
            last.then_inc(ctx_sems["T_ready"], 1)
            act.wait_ge(ctx_sems["k_psum"], 1)
            for c in range(CHUNKS):
                last = A(ckT[:, c, :], bank[K_BANK][:, c * 256:(c + 1) * 256], ACT.Identity,
                         bias=bias_col["L0_xattn_bk"][:, c:c + 1])
            last.then_inc(ctx_sems["k_ready"], 1)
            act.wait_ge(ctx_sems["v_psum"], 1)
            for bb in range(BATCH):
                last = A(cv[:, bb, :], bank[4 + bb // 2][:, bb % 2 * 256:bb % 2 * 256 + 256], ACT.Copy)
            last.then_inc(ctx_sems["v_ready"], 1)
            S = CROSS0
            with act.Fori(0, BATCH) as b:
                copy_in(S, b)
                query_out(S, b, qbias[1])
                for g in range(GROUPS + 3):
                    if g < GROUPS:
                        act.wait_ge(*S("shift_ready", b * GROUPS + g + 1))
                        A(probs[g % 3][:], probs[g % 3][:], ACT.Exp).then_inc(S["p_ready"], 1)
                    if g >= 3:
                        group_out(S, b, g - 3, b * GROUPS + g - 2)
                outputs_T(S, b, bias_col["L0_xattn_bv"])
            if stages == 2:
                return

            def route_exp(S, moe):
                act.wait_ge(*S("exp_in", 1))
                A(expw[:, :, 0:moe.experts], expw[:, :, 0:moe.experts], ACT.Exp).then_inc(S["exp_ready"], 1)

            def expert_tiles(S, moe):
                H = moe.hidden

                def turn(j, u, first=True, second=True, early=False):
                    if first:
                        act.wait_ge(*S("t_psum", j + 1))
                        if not early:
                            act.wait_ge(*S("gu_psum", j - 1))
                        A(xgT[u % 2].rearrange("p c n -> p (c n)"), bank[u % 2][:, 0:DIM], ACT.Copy)\
                            .then_inc(S["t_ready"], 1)
                    if second:
                        a = (u + 1) % 2
                        act.wait_ge(*S("gu_psum", j))
                        if not early:
                            act.wait_ge(*S("h_ready", j - 2))
                        A(silu_g[a][:, 0:H], bank[2 + a][:, 0:H], ACT.Silu).then_inc(S["act_ready"], 1)

                for j in range(4):
                    turn(j, j, second=j >= 1, early=j < 2)
                with act.Fori(1, moe.tiles // 4) as q:
                    for u in range(4):
                        turn(q * 4 + u, u)
                turn(moe.tiles, 0, first=False)

            S = FFN0
            act.wait_ge(*CROSS0("x_ready", BATCH))
            with act.Fori(0, BATCH) as b:
                act.wait_ge(*S("y_init", b))
                act.wait_ge(*S("sum_psum", b))
                act.wait_ge(*S("xT_psum", b))
                A(xb, x_res[:, bass.ds(b * 2, 2), :], ACT.Copy).then_inc(S["xb_ready"], 1)
                act.wait_ge(*S("xT_psum", b + 1))
                A(xT.rearrange("p c n -> p (c n)"), bank[X_BANK][:], ACT.Copy).then_inc(S["xT_ready"], 1)
                for hc in range(4):
                    act.wait_ge(*S("g_psum", b * 4 + hc + 1))
                    if hc >= 2:
                        act.wait_ge(*S("hid_ready", b * 4 + hc - 1))
                    A(silu_s[hc % 2], bank[4 + hc % 2][:, 0:256], ACT.Silu).then_inc(S["silu_ready"], 1)
            route_exp(S, MOE0)
            expert_tiles(S, MOE0)
            if stages == 3:
                return

            act.wait_ge(*FFN0("x_ready", 1))
            S = SELF1
            with act.Fori(0, BATCH) as b:
                copy_in(S, b)
                for n, (bk, psum, dst) in enumerate(((Q_BANK, "q_psum", q_tok), (K_BANK, "k_psum", k_tok),
                                                     (V_BANK, "v_psum", v_tok))):
                    act.wait_ge(*S(psum, b + 1))
                    act.wait_ge(*QKV1("qkv_ready", b * 3 + n))
                    A(dst.rearrange("p i d -> p (i d)"), bank[bk][:], ACT.Copy, scale=SCALE if n == 0 else 1.0)\
                        .then_inc(QKV1["tok_ready"], 1)
                act.wait_ge(*QKV1("vT_psum", b + 1))
                A(v32[:, :, :, 0:HEAD_DIM], bank[X_BANK][:].rearrange("p (i h d) -> p i h d", i=2, h=HEADS), ACT.Copy)\
                    .then_inc(S["v_ready"], 1)
                for h in range(HEADS + 3):
                    if h < HEADS:
                        act.wait_ge(*S("max_ready", b * HEADS + h + 1))
                        if h >= 3:
                            act.wait_ge(*S("pT_psum", b * HEADS + h - 2))
                        for i in range(2):
                            last = A(probs[h % 3][:, i * SEQ:(i + 1) * SEQ], bank[S_BANKS[h % 3]][:, i * SEQ:(i + 1) * SEQ],
                                     ACT.Exp, bias=neg_max[:, h, i:i + 1], accum_out=row_sum[:, h, i:i + 1])
                        last.then_inc(S["p_ready"], 1)
                    if h >= 6 and h % 4 == 2:
                        group_out(S, b, h // 4 - 1, b * HEADS + h - 2)
            if stages == 4:
                return

            act.wait_ge(*SELF1("x_ready", BATCH))
            act.wait_ge(kv1_sems["kT_psum"], 1)
            A(kT.rearrange("p c n -> p (c n)"), bank[X_BANK][:], ACT.Copy).then_inc(kv1_sems["kT_ready"], 1)
            act.wait_ge(kv1_sems["vT_psum"], 1)
            act.wait_ge(kv1_sems["zeroed"], 1)
            A(v32_b[:, :, :, 0:HEAD_DIM], bank[Q_BANK][:].rearrange("p (i h d) -> p i h d", i=2, h=HEADS), ACT.Copy)\
                .then_inc(kv1_sems["v_ready"], 1)
            S = CROSS1
            with act.Fori(0, BATCH) as b:
                copy_in(S, b)
                act.wait_ge(*S("k_psum", b + 1))
                A(qT.rearrange("p c n -> p (c n)"), bank[K_BANK][:], ACT.Copy).then_inc(S["q_ready"], 1)
                for h in range(HEADS + 3):
                    if h < HEADS:
                        act.wait_ge(*S("max_ready", b * HEADS + h + 1))
                        if h >= 3:
                            act.wait_ge(*S("pT_psum", b * HEADS + h - 2))
                        for i in range(2):
                            last = A(probs[h % 3][:, i * SEQ:(i + 1) * SEQ], bank[S_BANKS[h % 3]][:, i * SEQ:(i + 1) * SEQ],
                                     ACT.Exp, bias=shift[:, h, i:i + 1], scale=q_scale[:, i, h:h + 1],
                                     accum_out=row_sum[:, h, i:i + 1])
                        last.then_inc(S["p_ready"], 1)
                    if h >= 6 and h % 4 == 2:
                        group_out(S, b, h // 4 - 1, b * HEADS + h - 2)
                act.wait_ge(*S("oT_psum", b + 1))
                for c in range(CHUNKS):
                    last = A(oT[:, c, :], bank[X_BANK][:, c * 256:(c + 1) * 256], ACT.Copy, scale=v_scale[:, c:c + 1])
                last.then_inc(S["oT_ready"], 1)
            if stages == 5:
                return

            S = FFN1
            act.wait_ge(*CROSS1("x_ready", BATCH))
            with act.Fori(0, BATCH) as b:
                act.wait_ge(*S("y_init", b))
                act.wait_ge(*S("xT_psum", b))
                A(xb, x_res[:, bass.ds(b * 2, 2), :], ACT.Copy).then_inc(S["xb_ready"], 1)
                act.wait_ge(*S("xT_psum", b + 1))
                act.wait_ge(*S("logit_psum", b))
                A(xT.rearrange("p c n -> p (c n)"), bank[X_BANK][:], ACT.Copy).then_inc(S["xT_ready"], 1)
            route_exp(S, MOE1)
            expert_tiles(S, MOE1)

        @block.vector
        def _(dve):
            V = nc.vector

            def normalise_group(S, b, g):
                dve.wait_ge(*S("back_psum", b * GROUPS + g + 1))
                for i in range(2):
                    last = V.tensor_tensor(
                        o_tok[:, i, g * 64:(g + 1) * 64].rearrange("p (m d) -> p m d", m=4),
                        bank[BACK_BANK][:, i * 128:(i + 1) * 128].rearrange("p (m d) -> p m d", m=4)[:, :, 0:HEAD_DIM],
                        row_inv[:, 4 * g:4 * g + 4, i:i + 1].to_broadcast([128, 4, HEAD_DIM]), ALU.mult)
                last.then_inc(S["o_ready"], 1)

            def normalise(src, dst, n, step, done):
                for i in range(n):
                    last = V.bn_stats(stats[:, i, :], src(i))
                step(last)
                V.memset(spacer[:], 0.0)
                for i in range(n):
                    last = V.bn_aggr(mean_var[:, i, :], stats[:, i, :])
                step(last)
                v, bits, y, r = rs_v[:, 0:n], rs_bits[:, 0:n], rs_y[:, 0:n], rs_t[:, 0:n]
                step(V.tensor_scalar(v, mean_var[:, 0:n, 1], EPS, None, ALU.add))
                step(V.tensor_scalar(bits, v.bitcast(i32), 1, None, ALU.logical_shift_right))
                step(V.tensor_scalar(y.bitcast(i32), bits, -1.0, RSQRT_SEED, ALU.mult, ALU.add))
                for _ in range(4):
                    step(V.tensor_tensor(r, y, y, ALU.mult))
                    step(V.tensor_tensor(r, r, v, ALU.mult))
                    step(V.tensor_scalar(r, r, -0.5, 1.5, ALU.mult, ALU.add))
                    step(V.tensor_tensor(y, y, r, ALU.mult))
                for i in range(n):
                    last = V.tensor_scalar(dst(i), src(i), mean_var[:, i, 0:1], rs_y[:, i:i + 1],
                                           ALU.subtract, ALU.mult)
                last.then_inc(done, 1)

            def layernorm(S, b, step):
                dve.wait_ge(*S("proj_psum", b + 1))
                dve.wait_ge(*S("xbo_ready", b + 1))
                step(V.tensor_tensor(resid.rearrange("p i d -> p (i d)"), bank[PROJ_BANK][:],
                                     xbo.rearrange("p i d -> p (i d)"), ALU.add))
                normalise(lambda i: resid[:, i:i + 1, :], lambda i: x_res[:, bass.ds(b * 2 + i, 1), :], 2, step,
                          S["x_ready"])

            def layernorm_all(S, step):
                normalise(lambda i: y_acc[:, i, :], lambda i: x_res[:, i, :], TILES, step, S["x_ready"])

            LN_STEPS = 22

            dve.wait_ge(const_loaded, 32)
            V.tensor_copy(ident_b[:], ident).then_inc(const_ready, 1)
            V.tensor_copy(ident_h[:], ident).then_inc(const_ready, 1)
            V.tensor_copy(causal_b[:], const[:, C_CAUSAL:C_CAUSAL + 128]).then_inc(const_ready, 1)
            V.tensor_copy(tri_b[:], const[:, C_TRI:C_TRI + 128])
            V.tensor_copy(causal_h[:].rearrange("p i k -> p (i k)"), causal_f)
            V.memset(ones_b[:], 1.0)
            V.memset(ones_f[:], 1.0)
            V.memset(v32, 0.0).then_inc(const_ready, 1)
            V.memset(zeros[:], 0.0).then_inc(zeroed, 1)
            dve.wait_ge(w_loaded[0], LOADS[0])
            V.tensor_scalar(qbias[0][:], bias_col["L0_attn_b_attn"][:, 0:2], SCALE, None, ALU.mult).then_inc(const_ready, 1)
            dve.wait_ge(w_loaded[1], LOADS[1])
            V.tensor_scalar(qbias[1][:], bias_col["L0_xattn_bq"], SCALE, None, ALU.mult).then_inc(const_ready, 1)

            S = SELF0
            with dve.Fori(0, BATCH) as b:
                step = Steps(dve, steps["self0"], b, LN_STEPS + GROUPS)
                dve.wait_ge(*S("k_psum", b + 1))
                dve.wait_ge(*S("km_ready", b))
                for c in range(CHUNKS):
                    last = V.tensor_scalar(kT[:, c, :], bank[K_BANK][:, c * 256:(c + 1) * 256],
                                           bias_col["L0_attn_b_attn"][:, 2 + c:3 + c], None, ALU.add)
                last.then_inc(S["k_ready"], 1)
                for h in range(HEADS + 4):
                    if h < HEADS:
                        dve.wait_ge(*S("s_psum", b * HEADS + h + 1))
                        s = bank[S_BANKS[h % 3]]
                        V.tensor_reduce(neg_max[:, h, 0:1], s[:, 0:128], AX.X, ALU.max, negate=True)
                        V.tensor_reduce(neg_max[:, h, 1:2], s[:, 128:384], AX.X, ALU.max, negate=True)\
                            .then_inc(S["max_ready"], 1)
                    if 2 <= h < HEADS + 2:
                        dve.wait_ge(*S("pT_psum", b * HEADS + h - 1))
                        if h >= 4:
                            dve.wait_ge(*S("pv_psum", b * HEADS + h - 3))
                        V.tensor_copy(probsT[h % 2][:, 0:384], bank[PT_BANKS[h % 2]][:, 0:384]).then_inc(S["pT_ready"], 1)
                    if h >= 7 and h % 4 == 3:
                        g = h // 4 - 1
                        step(V.reciprocal(row_inv[:, 4 * g:4 * g + 4, :], row_sum[:, 4 * g:4 * g + 4, :]))
                        normalise_group(S, b, g)
                layernorm(S, b, step)
                step.done()
            if stages == 1:
                return

            V.memset(v32[:, 0], 0.0).then_inc(ctx_sems["zeroed"], 1)
            dve.wait_ge(ctx_sems["zeroed"], 1)
            dve.wait_ge(ctx_sems["v_ready"], 1)
            S = CROSS0
            with dve.Fori(0, BATCH) as b:
                step = Steps(dve, steps["cross0"], b, LN_STEPS + 4 * GROUPS)
                dve.wait_ge(*S("xb_ready", b + 1))
                dve.wait_ge(*S("x_ready", b))
                for a in range(2):
                    pp = slice(64 * a, 64 * a + 64)
                    last = V.tensor_copy(v32[pp, 0, a::2, 0:HEAD_DIM],
                                         cv[pp, bass.ds(b, 1), :].rearrange("p o (h a d) -> p (o h) a d", a=2, d=HEAD_DIM)[:, :, a, :])
                last.then_inc(S["v_ready"], 1)
                for i in range(GROUPS + 4):
                    if i < GROUPS:
                        dve.wait_ge(*S("s_psum", b * GROUPS + i + 1))
                        if i == 3:
                            dve.wait_ge(*S("pT_psum", b * GROUPS + 1))
                        s = bank[S_BANKS[i % 3]][:].rearrange("p (i m k) -> p i m k", i=2, m=4)
                        m = neg_max[:, 4 * i:4 * i + 4, :].rearrange("p m i -> p i m")
                        step(V.tensor_reduce(m, s, AX.X, ALU.max, negate=True))
                        V.tensor_tensor(probs[i % 3][:].rearrange("p (i m k) -> p i m k", i=2, m=4), s,
                                        m.unsqueeze(3).to_broadcast([128, 2, 4, CTX]), ALU.add)\
                            .then_inc(S["shift_ready"], 1)
                    if 2 <= i < GROUPS + 2:
                        g = i - 2
                        dve.wait_ge(*S("p_ready", b * GROUPS + g + 1))
                        r = row_sum[:, 4 * g:4 * g + 4, :].rearrange("p m i -> p i m")
                        step(V.tensor_reduce(r, probs[g % 3][:].rearrange("p (i m k) -> p i m k", i=2, m=4), AX.X, ALU.add))
                        step(V.reciprocal(row_inv[:, 4 * g:4 * g + 4, :], row_sum[:, 4 * g:4 * g + 4, :]))
                        dve.wait_ge(*S("pT_psum", b * GROUPS + g + 1))
                        if g >= 2:
                            dve.wait_ge(*S("pv_psum", b * GROUPS + g - 1))
                        step(V.tensor_copy(probsT[g % 2][:], bank[PT_BANKS[g % 2]][:]))
                        dve.sem_inc(S["pT_ready"], 1)
                    if i >= 4:
                        normalise_group(S, b, i - 4)
                layernorm(S, b, step)
                step.done()
            if stages == 2:
                return

            def route(S, moe, step):
                E, K = moe.experts, moe.picks
                TK = TILES * K
                lg, bi, ew = logits[:, :, 0:E], biased[:, :, 0:E], expw[:, :, 0:E]
                oh, pr = onehot[:, 0:TK, 0:E], product[:, 0:TK, 0:E]
                by_tile = lambda x: x.rearrange("p (i k) e -> p i k e", k=K)
                each_pick = lambda x: x.unsqueeze(2).to_broadcast([128, TILES, K, E])
                if moe is MOE0:
                    step(V.tensor_tensor(bi, lg, router_bias[:, 0:E].unsqueeze(1).to_broadcast([128, TILES, E]), ALU.add))
                else:
                    step(V.tensor_copy(bi, lg))
                for i in range(TILES):
                    last = V.max(top8[:, i, :], bi[:, i, :])
                step(last)
                for i in range(TILES):
                    last = V.max_index(top8_i[:, i, :], top8[:, i, :], bi[:, i, :])
                step(last)
                step(V.tensor_copy(top_f[:, 0:TK].rearrange("p (i k) -> p i k", k=K), top8_i[:, :, 0:K]))
                step(V.tensor_tensor(oh, iota_e[:, 0:E].unsqueeze(1).to_broadcast([128, TK, E]),
                                     top_f[:, 0:TK].unsqueeze(2).to_broadcast([128, TK, E]), ALU.is_equal))
                with nc.allow_low_precision("the mask is 0 or 1"):
                    V.tensor_reduce(mask_b[:, :, 0:E], oh.rearrange("p (i k) e -> p i e k", k=K), AX.X, ALU.add)\
                        .then_inc(S["mask_ready"], 1)
                step(V.tensor_reduce(row_t[0], lg, AX.X, ALU.max))
                V.tensor_tensor(ew, lg, row_t[0].unsqueeze(2).to_broadcast([128, TILES, E]), ALU.subtract)\
                    .then_inc(S["exp_in"], 1)
                dve.wait_ge(*S("exp_ready", 1))
                step(V.tensor_tensor(by_tile(pr), by_tile(oh), each_pick(ew), ALU.mult))
                step(V.tensor_reduce(picked[:, :, 0:K], by_tile(pr), AX.X, ALU.add))
                step(V.tensor_reduce(row_t[1], picked[:, :, 0:K], AX.X, ALU.add))
                step(V.reciprocal(row_t[2], row_t[1]))
                step(V.tensor_tensor(pick_w[:, :, 0:K], picked[:, :, 0:K],
                                     row_t[2].unsqueeze(2).to_broadcast([128, TILES, K]), ALU.mult))
                dve.wait_ge(*S("rank_psum", 1))
                cnt, tiles, upto, first, _ = [c[:, 0:E] for c in counts]
                ci, ti = [c[:, 0:E] for c in counts_i]
                step(V.tensor_scalar(ci, bank[1][:, 0:E], float(TILE - 1), None, ALU.add))
                step(V.tensor_scalar(ti, ci, TILE.bit_length() - 1, None, ALU.logical_shift_right))
                step(V.tensor_copy(tiles, ti))
                step(V.tensor_tensor_scan(upto, ones_f[:, 0:E], tiles, 0.0, ALU.mult, ALU.add))
                step(V.tensor_tensor(first, upto, tiles, ALU.subtract))
                step(V.tensor_scalar(first, first, float(TILE), None, ALU.mult))
                sb_ = slot_base[:, :, 0:E]
                step(V.tensor_tensor(sb_, bank[0][:, 0:TILES * E].rearrange("p (i e) -> p i e", i=TILES),
                                     first.unsqueeze(1).to_broadcast([128, TILES, E]), ALU.add))
                step(V.tensor_tensor(by_tile(pr), by_tile(oh), each_pick(sb_), ALU.mult))
                step(V.tensor_reduce(pos_f[:, 0:TK], pr, AX.X, ALU.add))
                step(V.tensor_copy(pos[:, 0:TK], pos_f[:, 0:TK]))
                step(V.tensor_scalar(counts[4][:, 0:E], upto, const[:, C_ROW:C_ROW + 1], None, ALU.is_le))
                step(V.tensor_reduce(e_col[0], counts[4][:, 0:E], AX.X, ALU.add))
                step(V.tensor_scalar(e_col[1], e_col[0], float(E - 1), None, ALU.min))
                V.tensor_scalar(e_diag, ident, e_col[1], None, ALU.mult).then_inc(S["e_ready"], 1)
                dve.wait_ge(*S("e_psum", 1))
                step(V.tensor_copy(tile_expert[:, 0, :], bank[2][:, 0:128]))
                step(V.tensor_scalar(tile_expert[:, 1, :], tile_expert[:, 0, :], 1, None, ALU.logical_shift_right))
                step(V.tensor_scalar(e_par, tile_expert[:, 0, :], 1, None, ALU.bitwise_and))
                step(V.tensor_scalar(tile_half[:], e_par, const[:, C_HALF:C_HALF + 1], None, ALU.is_equal))
                dve.sem_inc(S["routed"], 1)

            def expert_tiles(S, moe):
                H = moe.hidden
                small = moe is MOE0

                def turn(j, u, second=True, third=True, fourth=True, early=0, stored=None):
                    if second:
                        a = (u + 1) % 2
                        dve.wait_ge(*S("act_ready", j))
                        if early == 0 or early > 3:
                            dve.wait_ge(*S("hT_psum", j - 2))
                        if small:
                            V.tensor_tensor(hid[a][:, 0:128].rearrange("p (a n) -> p a n", a=2),
                                            silu_g[a][:, 0:H].unsqueeze(1).to_broadcast([128, 2, H]),
                                            bank[2 + a][:, H:2 * H].unsqueeze(1).to_broadcast([128, 2, H]), ALU.mult)\
                                .then_inc(S["h_ready"], 1)
                        else:
                            V.tensor_tensor(hid[a], silu_g[a], bank[4 + a][:], ALU.mult).then_inc(S["h_ready"], 1)
                    if third:
                        dve.wait_ge(*S("hT_psum", j - 1))
                        if early == 0 or early > 4:
                            dve.wait_ge(*S("y_psum", j - 3))
                        if small:
                            V.tensor_scalar(hidT[u % 2][:, 0:128], bank[6][:, 0:128], tile_half[:, bass.ds(j - 2, 1)],
                                            None, ALU.mult).then_inc(S["hT_ready"], 1)
                        else:
                            V.tensor_copy(hidT[u % 2], bank[6][:]).then_inc(S["hT_ready"], 1)
                    if fourth:
                        v = (u + 1) % 4
                        dve.wait_ge(*S("y_psum", j - 2))
                        if early == 0:
                            dve.wait_ge(*S("stored", (j - 3) // 4 * 16 if stored is None else stored, v))
                        V.tensor_copy(y_tile[v], bank[7][:, 0:DIM]).then_inc(S["y_copied"], 1)

                for j in range(1, 4):
                    turn(j, j, third=j >= 2, fourth=j >= 3, early=j)
                for j in range(4, 8):
                    turn(j, j % 4, early=j if j < 7 else 0)
                with dve.Fori(2, moe.tiles // 4) as q:
                    for u in range(4):
                        turn(q * 4 + u, u, stored=q * 16 - 16 if u < 3 else q * 16)
                for u in range(3):
                    turn(moe.tiles + u, u, second=u == 0, third=u <= 1)

            def combine(S, moe, step):
                for n in range(TILES * moe.picks):
                    i, k = n // moe.picks, n % moe.picks
                    dve.wait_ge(*S("fetched", 16 * (n // 8 + 1), n % 8))
                    ins = V.scalar_tensor_tensor(y_acc[:, i, :], y_pick[n % 8], pick_w[:, i, k:k + 1], y_acc[:, i, :],
                                                 ALU.mult, ALU.add)
                    ins.then_inc(S["summed"], 1)
                    dve.wait_ge(*S("summed", n + 1))

            S = FFN0
            with dve.Fori(0, BATCH) as b:
                dve.wait_ge(*S("logit_psum", b + 1))
                V.tensor_copy(logits[:, bass.ds(b * 2, 2), :],
                              bank[K_BANK][:, 0:128].rearrange("p (i e) -> p i e", i=2)).then_inc(S["logit_ready"], 1)
                for hc in range(4):
                    dve.wait_ge(*S("silu_ready", b * 4 + hc + 1))
                    if hc == 0:
                        dve.wait_ge(*S("sum_psum", b))
                    V.tensor_tensor(hidden_s[:, hc, :], silu_s[hc % 2], bank[4 + hc % 2][:, 256:512], ALU.mult)\
                        .then_inc(S["hid_ready"], 1)
                dve.wait_ge(*S("sum_psum", b + 1))
                V.tensor_tensor(y_acc[:, bass.ds(b * 2, 2), :], bank[PROJ_BANK][:].rearrange("p (i d) -> p i d", i=2),
                                xb, ALU.add).then_inc(S["y_init"], 1)
            dve.wait_ge(*S("logit_ready", BATCH))
            dve.wait_ge(*S("y_init", BATCH))
            dve.wait_ge(router_loaded[0], 32)
            step = Steps(dve, steps["ffn0"], 0, None)
            route(S, MOE0, step)
            expert_tiles(S, MOE0)
            combine(S, MOE0, step)
            layernorm_all(S, step)
            if stages == 3:
                return

            def by_head(src, dst, ready, step):
                for st in range(2):
                    last = V.transpose(dup[st].rearrange("p j a i -> p (j a i)"),
                                       src[:, st, :].rearrange("p (j d) -> p j d", d=HEAD_DIM).unsqueeze(2)
                                       .to_broadcast([128, HEADS, 2, HEAD_DIM]))
                step(last)
                for st in range(2):
                    last = V.tensor_scalar(dst(st), dup[st][:, :, 0, :], parity[:, 0:1], None, ALU.mult)
                step(last)
                for st in range(2):
                    last = V.scalar_tensor_tensor(dst(st), dup[st][:, :, 1, :], parity[:, 1:2], dst(st), ALU.mult, ALU.add)
                step(last)

            def full_heads(S, b, step, quantised):
                for h in range(HEADS + 4):
                    if h < HEADS:
                        dve.wait_ge(*S("s_psum", b * HEADS + h + 1))
                        ins = V.tensor_reduce(neg_max[:, h, :], bank[S_BANKS[h % 3]][:].rearrange("p (i k) -> p i k", i=2),
                                              AX.X, ALU.max, negate=True)
                        if quantised:
                            step(ins)
                            ins = V.tensor_tensor(shift[:, h, :], neg_max[:, h, :], q_scale[:, :, h], ALU.mult)
                        ins.then_inc(S["max_ready"], 1)
                    if 2 <= h < HEADS + 2:
                        dve.wait_ge(*S("pT_psum", b * HEADS + h - 1))
                        if h >= 4:
                            dve.wait_ge(*S("pv_psum", b * HEADS + h - 3))
                        if quantised:
                            step(V.tensor_scalar(p_shifted[0], bank[PT_BANKS[h % 2]][:], PROB_LEVELS, ROUND, ALU.mult, ALU.add))
                            with nc.allow_low_precision("whole numbers up to 255 are exact"):
                                step(V.tensor_scalar(probsT_b[h % 2], p_shifted[0], ROUND, None, ALU.subtract))
                            dve.sem_inc(S["pT_ready"], 1)
                        else:
                            V.tensor_copy(probsT[h % 2], bank[PT_BANKS[h % 2]][:]).then_inc(S["pT_ready"], 1)
                    if h >= 7 and h % 4 == 3:
                        g = h // 4 - 1
                        step(V.reciprocal(row_inv[:, 4 * g:4 * g + 4, :], row_sum[:, 4 * g:4 * g + 4, :]))
                        normalise_group(S, b, g)

            S = SELF1
            V.memset(v32, 0.0).then_inc(ctx_sems["zeroed"], 1)
            dve.wait_ge(ctx_sems["zeroed"], 2)
            with dve.Fori(0, BATCH) as b:
                step = Steps(dve, steps["self1"], b, 9 + GROUPS + 4 + LN_STEPS)
                by_pos = lambda a: (lambda st: a[:, st, :].rearrange("p (j i) -> p j i", i=16))
                for n, (src, dst) in enumerate(((q_tok, qT), (k_tok, kT), (v_tok, vT))):
                    dve.wait_ge(*QKV1("tok_ready", b * 3 + n + 1))
                    if n == 1:
                        dve.wait_ge(*S("km_ready", b))
                    by_head(src, by_pos(dst), None, step)
                    dve.sem_inc(QKV1["qkv_ready"], 1)
                    if n == 1:
                        dve.sem_inc(S["k_ready"], 1)
                full_heads(S, b, step, False)
                dve.wait_ge(*S("o_ready", (b + 1) * GROUPS))
                by_head(o_tok, by_pos(oT), None, step)
                step(V.tensor_copy(spacer[:], spacer[:]))
                dve.sem_inc(S["oT_ready"], 1)
                layernorm(S, b, step)
                step.done()
            if stages == 4:
                return

            S = CROSS1
            step = Steps(dve, steps["kv1"], 0, None)
            V.memset(v32_b, 0.0).then_inc(kv1_sems["zeroed"], 1)
            heads_of = lambda x: x.rearrange("p i (h d) -> p i h d", h=HEADS)

            def quantise(x, s, step):
                step(V.tensor_reduce(s, heads_of(x), AX.X, ALU.max, apply_absolute_value=True))
                step(V.tensor_scalar(s, s, 1 / LEVELS, 1e-8, ALU.mult, ALU.max))
                step(V.reciprocal(inv_scale, s))
                step(V.tensor_tensor(heads_of(x), heads_of(x), inv_scale.unsqueeze(3).to_broadcast([128, 2, HEADS, HEAD_DIM]),
                                     ALU.mult))
                step(V.tensor_scalar(x, x, ROUND, ROUND + LEVELS, ALU.add, ALU.min))
                step(V.tensor_scalar(x, x, ROUND - LEVELS, ROUND, ALU.max, ALU.subtract))

            dve.wait_ge(w_loaded[3], LOADS[3])
            dve.wait_ge(kv1_sems["k_psum"], 1)
            step(V.tensor_tensor(k_int, bank[K_BANK][:].rearrange("p (i d) -> p i d", i=2),
                                 bias_row["L1_xattn_bk_row"][:, 0:DIM].unsqueeze(1).to_broadcast([128, 2, DIM]), ALU.add))
            quantise(k_int, k_scale, step)
            step(V.tensor_tensor(heads_of(k_int), heads_of(k_int), k_scale.unsqueeze(3)
                                 .to_broadcast([128, 2, HEADS, HEAD_DIM]), ALU.mult))
            dve.sem_inc(kv1_sems["k_ready"], 1)
            dve.wait_ge(kv1_sems["v_psum"], 1)
            for c in range(CHUNKS):
                last = V.tensor_scalar(vq[:, c, :], bank[V_BANK][:, c * 256:(c + 1) * 256],
                                       bias_col["L1_xattn_bkv"][:, 2 + c:3 + c], None, ALU.add)
            step(last)
            step(V.tensor_reduce(v_scale, vq, AX.X, ALU.max, apply_absolute_value=True))
            step(V.tensor_scalar(v_scale, v_scale, 1 / LEVELS, 1e-8, ALU.mult, ALU.max))
            step(V.reciprocal(v_inv, v_scale))
            for c in range(CHUNKS):
                last = V.tensor_scalar(vq[:, c, :], vq[:, c, :], v_inv[:, c:c + 1], ROUND, ALU.mult, ALU.add)
            step(last)
            step(V.tensor_scalar(vq, vq, ROUND + LEVELS, ROUND - LEVELS, ALU.min, ALU.max))
            step(V.tensor_scalar(vq, vq, ROUND, None, ALU.subtract))
            dve.sem_inc(kv1_sems["vq_ready"], 1)
            step(V.tensor_scalar(v_scale, v_scale, 1 / PROB_LEVELS, None, ALU.mult))
            step(V.tensor_scalar(bias_row["L1_xattn_bq"], bias_row["L1_xattn_bq"], SCALE, None, ALU.mult))
            with dve.Fori(0, BATCH) as b:
                step = Steps(dve, steps["cross1"], b, 7 + 3 * HEADS + GROUPS + LN_STEPS)
                dve.wait_ge(*S("q_psum", b + 1))
                step(V.scalar_tensor_tensor(q_int, bank[Q_BANK][:].rearrange("p (i d) -> p i d", i=2), SCALE,
                                            bias_row["L1_xattn_bq"].unsqueeze(1).to_broadcast([128, 2, DIM]),
                                            ALU.mult, ALU.add))
                quantise(q_int, q_scale, step)
                dve.sem_inc(S["k_ready"], 1)
                full_heads(S, b, step, True)
                layernorm(S, b, step)
                step.done()
            if stages == 5:
                return

            S = FFN1
            with dve.Fori(0, BATCH) as b:
                dve.wait_ge(*S("xb_ready", b + 1))
                V.tensor_copy(y_acc[:, bass.ds(b * 2, 2), :], xb).then_inc(S["y_init"], 1)
                dve.wait_ge(*S("logit_psum", b + 1))
                V.tensor_copy(logits[:, bass.ds(b * 2, 2), 0:MOE1.experts],
                              bank[K_BANK][:, 0:128].rearrange("p (i e) -> p i e", i=2)[:, :, 0:MOE1.experts])\
                    .then_inc(S["logit_ready"], 1)
            dve.wait_ge(*S("logit_ready", BATCH))
            dve.wait_ge(*S("y_init", BATCH))
            step = Steps(dve, steps["ffn1"], 0, None)
            route(S, MOE1, step)
            expert_tiles(S, MOE1)
            combine(S, MOE1, step)
            layernorm_all(S, step)

        @block.gpsimd
        def _(pool):
            P = nc.gpsimd
            for signals in (SELF0, FFN0, QKV1):
                for n, s in signals.sems.items():
                    if n not in signals.by_dma:
                        pool.sem_inc(s, 1)

            def residual_rows(S, b, bias):
                pool.wait_ge(*S("xb_ready", b + 1))
                pool.wait_ge(*S("x_ready", b))
                P.tensor_tensor(xbo[:], xb[:], bias[:].unsqueeze(1).to_broadcast([128, 2, DIM]), ALU.add)\
                    .then_inc(S["xbo_ready"], 1)

            def masked_keys(S, b, src, n):
                for c in range(CHUNKS):
                    last = P.tensor_tensor(kTm[:, c, :, 0:n], src(c).to_broadcast([128, 4, n]),
                                           head_mask.unsqueeze(2).to_broadcast([128, 4, n]), ALU.mult)
                last.then_inc(S["km_ready"], 1)

            pool.wait_ge(const_loaded, 32)
            pool.wait_ge(w_loaded[0], LOADS[0])
            S = SELF0
            with pool.Fori(0, BATCH) as b:
                residual_rows(S, b, bias_row["L0_attn_b_proj"])
                pool.wait_ge(*S("k_ready", b + 1))
                masked_keys(S, b, lambda c: kT[:, c:c + 1, :], SEQ)
            if stages == 1:
                return
            pool.wait_ge(w_loaded[1], LOADS[1])
            pool.wait_ge(ctx_sems["k_ready"], 1)
            S = CROSS0
            with pool.Fori(0, BATCH) as b:
                residual_rows(S, b, bias_row["L0_xattn_bo"])
                masked_keys(S, b, lambda c: ckT[:, c:c + 1, bass.ds(b * CTX, CTX)], CTX)
            if stages == 2:
                return

            def send_rows(S, moe):
                pool.wait_ge(*S("routed", 1))
                pool.wait_ge(zero_filled, 16 * (MOE0.tiles + MOE1.tiles) // 8)
                for n in range(TILES * moe.picks):
                    P.indirect_dma_start(out=sorted_x[moe.stage],
                                         out_offset=bass.IndirectOffsetOnAxis(ap=pos[:, n:n + 1], axis=0),
                                         in_=x_res[:, n // moe.picks, :], in_offset=None).then_inc(S["sent"], 16)

            def fetch_outputs(S, moe):
                for v in range(4):
                    pool.wait_ge(*S("stored", 16 * moe.tiles // 4, v))
                for n in range(TILES * moe.picks):
                    if n >= 8:
                        pool.wait_ge(*S("summed", n - 7))
                    P.indirect_dma_start(out=y_pick[n % 8], out_offset=None, in_=sorted_y[moe.stage],
                                         in_offset=bass.IndirectOffsetOnAxis(ap=pos[:, n:n + 1], axis=0))\
                        .then_inc(S["fetched"][n % 8], 16)

            send_rows(FFN0, MOE0)
            fetch_outputs(FFN0, MOE0)
            if stages == 3:
                return
            S = SELF1
            with pool.Fori(0, BATCH) as b:
                pool.wait_ge(*S("xb_ready", b + 1))
                pool.wait_ge(*S("x_ready", b))
                P.tensor_tensor(xbo, xb, zeros[:].unsqueeze(1).to_broadcast([128, 2, DIM]), ALU.add)\
                    .then_inc(S["xbo_ready"], 1)
                pool.wait_ge(*S("k_ready", b + 1))
                masked_keys(S, b, lambda c: kT[:, c:c + 1, :], SEQ)
            if stages == 4:
                return
            S = CROSS1
            pool.wait_ge(w_loaded[3], LOADS[3])
            pool.wait_ge(kv1_sems["kT_ready"], 1)
            masked_keys(S, 0, lambda c: kT[:, c:c + 1, :], SEQ)
            with pool.Fori(0, BATCH) as b:
                residual_rows(S, b, bias_row["L1_xattn_bp"])
            if stages == 5:
                return
            send_rows(FFN1, MOE1)
            fetch_outputs(FFN1, MOE1)


_TRANSPOSED = ("L0_xattn_Wq", "L0_xattn_Wk", "L0_xattn_Wv", "L0_xattn_Wo")


def _constants(np):
    c = np.zeros((128, C_COLS), np.float32)
    p = np.arange(128)
    c[:, C_IDENT:C_IDENT + 128] = np.eye(128)
    c[:, C_CAUSAL:C_CAUSAL + 128] = np.where(p[None, :] <= p[:, None], 0.0, -1e30)
    c[:, C_TRI:C_TRI + 128] = p[:, None] < p[None, :]
    s = np.arange(256)
    s = s % 16 * 16 + s // 16
    c[:, C_CAUSAL1:C_COLS] = np.where(s[None, :] <= s[:, None], 1.0, -10000.0).reshape(2, 128, 256)\
        .transpose(1, 0, 2).reshape(128, 512)
    c[:, C_HALF] = p // 64
    c[:, C_ROW] = p
    c[:, C_IOTA:C_IOTA + 64] = np.arange(64)
    c[:, C_HEADMASK:C_HEADMASK + 4] = (p[:, None] % 64 // 16 == np.arange(4)[None, :])
    c[:, C_PARITY:C_PARITY + 2] = (p[:, None] // 16 % 2 == np.arange(2)[None, :])
    return c


def _program(nc, inputs, stages=99):
    import numpy as np

    arrays, tensors = {}, {}
    host = {n: np.asarray(a) for n, a in inputs.items() if "decoder_" not in n}
    host["x"] = host["x"].reshape(-1, DIM)
    host["ctx_2048"] = host["ctx_2048"].reshape(-1, DIM)
    for n in _TRANSPOSED:
        host[n] = host[n].T
    swg, swu, wg, wu = [host.pop(f"L0_ffn_{n}") for n in ("swg", "swu", "wg", "wu")]
    host["L0_ffn_swg"] = swg.transpose(1, 0, 2).reshape(DIM, SHARED_HIDDEN)
    host["L0_ffn_swu"] = swu.transpose(1, 0, 2).reshape(DIM, SHARED_HIDDEN)
    host["L0_ffn_swd"] = host["L0_ffn_swd"].reshape(SHARED_HIDDEN, DIM)
    gu = np.concatenate([wg, wu], axis=2)
    host["expert_in0"] = gu.reshape(64, CHUNKS, 128, 128).transpose(2, 0, 1, 3).reshape(128, -1)
    host["expert_out0"] = host.pop("L0_ffn_wd").reshape(32, 128, DIM).transpose(1, 0, 2).reshape(128, -1)
    gu = np.concatenate([host.pop("L1_ffn_w0"), host.pop("L1_ffn_w1")], axis=2)
    host["expert_in1"] = gu.reshape(8, CHUNKS, 128, 1024).transpose(2, 0, 1, 3).reshape(128, -1)
    host["expert_out1"] = host.pop("L1_ffn_wo").reshape(8, 4, 128, DIM).transpose(2, 0, 1, 3).reshape(128, -1)
    host["L1_xattn_bk_row"] = host["L1_xattn_bkv"]
    for n in BIAS_COL:
        host[n] = host[n].reshape(-1, 128).T
    host["const"] = _constants(np)
    for n, a in host.items():
        a = np.ascontiguousarray(a)
        arrays[f"in_{n}"] = a
        tensors[n] = nc.dram_tensor(f"in_{n}", a.shape, mybir.dt.from_np(a.dtype), kind="ExternalInput").ap()
    out = nc.dram_tensor("out", (BATCH * SEQ, DIM), mybir.dt.float32, kind="ExternalOutput").ap()
    decoder_kernel(nc, tensors, out, stages)
    return arrays


def kernel(**inputs):
    import concourse.bacc as bacc
    from concourse.bass_utils import run_bass_kernel_spmd

    nc = bacc.Bacc("TRN2", target_bir_lowering=False, num_devices=1)
    arrays = _program(nc, inputs)
    r = run_bass_kernel_spmd(nc, [arrays], core_ids=[0])
    return r.results[0]["out"].reshape(BATCH, SEQ, DIM)
```

```python
import concourse.bass as bass
from concourse import mybir
from contextlib import ExitStack

BATCH, SEQ, DIM = 4, 256, 256
CTX = 64
HEADS, HEAD_DIM = 16, 16
TILE = 128
TILES = BATCH * SEQ // TILE
CHUNKS = DIM // TILE
GROUPS = HEADS // 4
SCALE = HEAD_DIM ** -0.5
EPS = 1e-5
RSQRT_SEED = 1597463007.0

C_IDENT, C_CAUSAL, C_TRI, C_HEADMASK, C_PARITY, C_HALF, C_ROW, C_IOTA = 0, 128, 256, 384, 388, 390, 391, 392
C_CAUSAL1 = C_IOTA + 64
C_COLS = C_CAUSAL1 + 2 * SEQ
ROUND = 1.5 * 2 ** 23
LEVELS, PROB_LEVELS = 127.0, 255.0


class Moe:
    def __init__(self, experts, picks, hidden, stage):
        self.experts, self.picks, self.hidden, self.stage = experts, picks, hidden, stage
        self.tiles = BATCH * SEQ * picks // TILE + experts
        assert self.tiles % 4 == 0
        self.hT_banks, self.y_banks = ((6, 4), (7, 5)) if hidden < 128 else ((6, 6), (7, 7))


MOE0, MOE1 = Moe(64, 4, 64, 0), Moe(8, 2, 512, 1)
SHARED_HIDDEN = 512

W_ATTN = {"L0_attn_w_attn": 0, "L0_attn_w_proj": 0, "L0_xattn_Wq": 1, "L0_xattn_Wk": 1, "L0_xattn_Wv": 1,
          "L0_xattn_Wo": 1, "L1_attn_w_qkv": 2, "L1_attn_w_out": 2,
          "L1_xattn_Wq": 3, "L1_xattn_Wkv": 3, "L1_xattn_Wp": 3}
BIAS_COL = {"L0_attn_b_attn": 0, "L0_xattn_bq": 1, "L0_xattn_bk": 1, "L0_xattn_bv": 1, "L1_xattn_bkv": 3}
BIAS_ROW = {"L0_attn_b_proj": 0, "L0_xattn_bo": 1, "L1_xattn_bq": 3, "L1_xattn_bk_row": 3, "L1_xattn_bp": 3}


def decoder_kernel(nc: bass.Bass, t: dict, out: bass.AP, stages: int = 99):
    f32, bf16, f16 = mybir.dt.float32, mybir.dt.bfloat16, mybir.dt.float16
    i32, u32 = mybir.dt.int32, mybir.dt.uint32
    ALU, ACT, AX = mybir.AluOpType, mybir.ActivationFunctionType, mybir.AxisListType

    with ExitStack() as ctx:
        def sb(name, shape, dt=f32):
            return ctx.enter_context(nc.sbuf_tensor(name, shape, dt))

        def sem(name):
            return ctx.enter_context(nc.semaphore(name))

        bank = [ctx.enter_context(nc.psum_tensor(f"bank{i}", [128, 512], f32)) for i in range(8)]
        SX_BANK = 3
        X_BANK, Q_BANK, K_BANK, V_BANK = 0, 1, 2, 3
        S_BANKS, PT_BANKS, PV_BANK, BACK_BANK, PROJ_BANK = (4, 5, 0), (6, 7), 2, 3, 6

        class Carver:
            def __init__(self, region):
                self.region, self.at = region, 0

            def __call__(self, *shape, dt=None):
                n = 1
                for k in shape:
                    n *= k
                v = self.region[:, self.at:self.at + n]
                self.at += n
                assert self.at <= self.region.shape[1], self.at
                if dt is not None:
                    v = v.bitcast(dt)
                if len(shape) > 1:
                    names = "abcd"[:len(shape)]
                    v = v.rearrange(f"p ({' '.join(names)}) -> p {' '.join(names)}",
                                    **{k: x for k, x in zip(names[1:], shape[1:])})
                return v

        x_res = sb("x_res", [128, TILES, DIM])
        const = sb("const", [128, C_CAUSAL1])
        ident = const[:, C_IDENT:C_IDENT + 128]
        head_mask = const[:, C_HEADMASK:C_HEADMASK + 4]
        parity = const[:, C_PARITY:C_PARITY + 2]
        ident_h = sb("ident_h", [128, 128], f16)
        ident_b = sb("ident_b", [128, 128], bf16)
        causal_b = sb("causal_b", [128, 128], bf16)
        causal_h = sb("causal_h", [128, 2, SEQ], f16)
        tri_b = sb("tri_b", [128, 128], bf16)
        ones_b = sb("ones_b", [128, 128], bf16)
        ones_f = sb("ones_f", [128, 128])
        iota_e = const[:, C_IOTA:C_IOTA + 64]
        zeros = sb("zeros", [128, DIM])
        y_acc = sb("y_acc", [128, TILES, DIM])
        expert_in = sb("expert_in", [128, 16384])
        expert_out = sb("expert_out", [128, 8192])
        neg_max = sb("neg_max", [128, HEADS, 2])
        row_sum = sb("row_sum", [128, HEADS, 2])
        row_inv = sb("row_inv", [128, 2, 2, 4])
        spacer = sb("spacer", [128, 1])
        stats = sb("stats", [128, TILES, 6])
        mean_var = sb("mean_var", [128, TILES, 2])
        rs_bits = sb("rs_bits", [128, TILES], i32)
        rs_y, rs_t, rs_v = sb("rs_y", [128, TILES]), sb("rs_t", [128, TILES]), sb("rs_v", [128, TILES])
        qbias = [sb(f"qbias{i}", [128, 2]) for i in range(2)]
        tile_expert = sb("tile_expert", [128, 2, 128], i32)
        tile_half = sb("tile_half", [128, 128])
        pos_f = sb("pos_f", [128, 32])
        pos = sb("pos", [128, 32], u32)
        pick_w = sb("pick_w", [128, TILES, 4])

        w_region = sb("w_region", [128, 7800])
        w_in, bias_col, bias_row = {}, {}, {}
        for layer in range(2):
            cut = Carver(w_region)
            for n in W_ATTN:
                if n.startswith(f"L{layer}"):
                    w_in[n] = cut(CHUNKS, t[n].shape[-1])
            for n in BIAS_COL:
                if n.startswith(f"L{layer}"):
                    bias_col[n] = cut(t[n].shape[1])
            for n in BIAS_ROW:
                if n.startswith(f"L{layer}"):
                    bias_row[n] = cut(t[n].shape[0])
            if layer == 0:
                shared_in = [cut(CHUNKS, SHARED_HIDDEN) for _ in range(2)]
                shared_out = cut(SHARED_HIDDEN // 128, DIM)

        work = sb("work", [128, 14400])
        cut = Carver(work)
        xb = cut(2, DIM)
        xbo = cut(2, DIM)
        xT = cut(CHUNKS, SEQ)
        qT = cut(CHUNKS, SEQ)
        kT = cut(CHUNKS, SEQ)
        kTm = cut(CHUNKS, 4, SEQ)
        v32 = cut(2, HEADS, 32)
        probs = [cut(512) for i in range(3)]
        probsT = [cut(512) for i in range(2)]
        oT4 = [cut(SEQ) for i in range(2)]
        o_tok = cut(2, DIM)
        oT = cut(CHUNKS, SEQ)
        logits = cut(TILES, 64)
        dup_at = cut.at
        ctxT = cut(CHUNKS, BATCH * CTX)
        ctx_tok = cut(2, DIM)
        ctxT2 = cut(CHUNKS, BATCH, 2, CTX)
        ckT = cut(CHUNKS, BATCH * CTX)
        cv = cut(BATCH, DIM)
        cut.at = dup_at + CHUNKS * BATCH * CTX
        q_tok, k_tok, v_tok = [cut(2, DIM) for _ in range(3)]
        dup = [cut(HEADS, 2, HEAD_DIM) for _ in range(2)]
        vT = probs[2].rearrange("p (c n) -> p c n", c=CHUNKS)
        dup_k = [cut(HEADS, 2, HEAD_DIM) for _ in range(2)]
        cut.at = work.shape[1] - 512
        causal_f = cut(512)
        cut.at = dup_at + CHUNKS * BATCH * CTX
        q_int, k_int = [cut(2, DIM) for _ in range(2)]
        expanded = cut(1024, dt=bf16).rearrange("p (i h c d) -> p (i h) c d", i=2, h=HEADS, c=4)
        k_parts, q_parts = [kTm.rearrange("p c m n -> p (c m n)")[:, n * 1024:(n + 1) * 1024].bitcast(bf16)
                            .rearrange("p (h n) -> p h n", h=HEADS // 2) for n in range(2)]
        q_scale, k_scale = [cut(2, HEADS) for _ in range(2)]
        inv_scale = cut(2, HEADS)
        v_scale, v_inv = cut(CHUNKS), cut(CHUNKS)
        shift = cut(HEADS, 2)
        vq = qT
        p_shifted = [cut(512), cut(512)]
        EXP_BANKS = (1, 2, 3, 7)
        probsT_b = [p[:, 0:256].bitcast(bf16) for p in probsT]
        v32_b = v32.rearrange("p i h d -> p (i h d)")[:, 0:512].bitcast(bf16)            .rearrange("p (i h d) -> p i h d", i=2, h=HEADS)
        cut.at = 0
        cut.at = dup_at + CHUNKS * BATCH * CTX
        xb_s, xT_s = cut(2, DIM), cut(CHUNKS, SEQ)
        silu_s = [cut(SEQ) for _ in range(2)]
        hidden_s = cut(SHARED_HIDDEN // 128, SEQ)
        cut = Carver(work)
        biased = cut(TILES, 64)
        expw = cut(TILES, 64)
        onehot = cut(32, 64)
        product = cut(32, 64)
        slot_base = cut(TILES, 64)
        top8 = cut(TILES, 8)
        top8_i = cut(TILES, 8, dt=u32)
        top_f = cut(32)
        row_t = [cut(TILES) for _ in range(3)]
        picked = cut(TILES, 4)
        counts = [cut(64) for _ in range(5)]
        counts_i = [cut(64, dt=i32) for _ in range(2)]
        e_col = [cut(1) for _ in range(2)]
        e_diag = cut(128)
        e_par = cut(128, dt=i32)
        mask_b = cut(TILES * 32, dt=bf16).rearrange("p (i e) -> p i e", i=TILES)
        cut = Carver(work)
        xg = [cut(DIM) for _ in range(4)]
        xgT = [cut(CHUNKS, TILE) for _ in range(2)]
        silu_g = [cut(512) for _ in range(2)]
        hid = [cut(512) for _ in range(2)]
        hidT = [cut(512) for _ in range(2)]
        y_tile = [cut(DIM) for _ in range(4)]
        y_pick = [cut(DIM) for _ in range(8)]

        sorted_x = [nc.dram_tensor(f"sorted_x{m.stage}", (m.tiles * TILE, DIM), f32).ap() for m in (MOE0, MOE1)]
        sorted_y = [nc.dram_tensor(f"sorted_y{m.stage}", (m.tiles * TILE, DIM), f32).ap() for m in (MOE0, MOE1)]

        const_loaded, const_ready, x_loaded, ctx_loaded, stored = map(
            sem, ("const_loaded", "const_ready", "x_loaded", "ctx_loaded", "stored"))
        CONSTS = 6
        w_loaded = [sem(f"w_loaded{i}") for i in range(4)]
        LOADS = [16 * sum(v == i for d in (W_ATTN, BIAS_COL, BIAS_ROW) for v in d.values()) for i in range(4)]

        class Signals:
            by_dma = ("sent", "loaded", "stored", "fetched")

            def __init__(self, sems, before=None):
                self.sems = sems
                self.before = before or {n: 0 if n in self.by_dma else 1 for n in sems}

            def __getitem__(self, name):
                return self.sems[name]

            def __call__(self, name, n, buf=None):
                done = self.before[name]
                s = self.sems[name] if buf is None else self.sems[name][buf]
                return s, n + done if done else n

            def after(self, counts):
                return Signals(self.sems, {n: self.before[n] + counts.get(n, 0) for n in self.sems})

        once = ("xb_ready", "xbo_ready", "xT_psum", "xT_ready", "q_psum", "k_psum", "v_psum", "q_ready", "k_ready",
                "v_ready", "oT_psum", "oT_ready", "proj_psum", "y_ready")
        per_group = ("ot_ready", "back_psum", "o_ready")
        per_head = ("s_psum", "max_ready", "shift_ready", "p_ready", "pT_psum", "pT_ready", "pv_psum")

        def attention_counts(n, never):
            c = {**{k: BATCH for k in once}, **{k: BATCH * GROUPS for k in per_group}, **{k: BATCH * n for k in per_head},
                 "km_ready": BATCH * CHUNKS, "x_ready": 1}
            return {k: v for k, v in c.items() if k not in never}

        SELF0 = Signals({n: sem(f"att_{n}") for n in once + per_group + per_head + ("km_ready", "x_ready")})
        CROSS0 = SELF0.after(attention_counts(HEADS, ("shift_ready",)))
        SELF1 = CROSS0.after(attention_counts(GROUPS, ("k_psum", "v_psum", "k_ready", "max_ready")))
        CROSS1 = SELF1.after(attention_counts(HEADS, ("shift_ready", "q_ready", "oT_psum")))

        per_batch = ("xb_ready", "xT_psum", "xT_ready", "logit_psum", "logit_ready")
        shared_batch = ("xb_s_ready", "xT_s_psum", "xT_s_ready", "y_init", "sum_psum")
        shared = ("g_psum", "silu_ready", "hid_ready")
        single = ("mask_ready", "exp_in", "exp_ready", "rank_psum", "e_ready", "e_psum", "routed", "x_ready")
        per_tile = ("t_psum", "t_ready", "gu_psum", "act_ready", "h_ready", "hT_psum", "hT_ready", "y_psum", "y_copied")
        rows0 = TILES * MOE0.picks
        moe_sems = {n: sem(f"ffn_{n}") for n in per_batch + shared_batch + shared + single + per_tile + ("sent", "summed")}
        moe_sems["loaded"] = [sem(f"ffn_loaded{i}") for i in range(4)]
        moe_sems["stored"] = [sem(f"ffn_stored{i}") for i in range(4)]
        moe_sems["fetched"] = [sem(f"ffn_fetched{i}") for i in range(8)]
        FFN0 = Signals(moe_sems)
        FFN1 = FFN0.after({**{n: BATCH for n in per_batch + shared_batch}, **{n: BATCH * SHARED_HIDDEN // 128 for n in shared},
                           **{n: 1 for n in single}, **{n: MOE0.tiles for n in per_tile},
                           "sent": 16 * rows0, "summed": rows0, "loaded": 16 * MOE0.tiles // 4,
                           "stored": 16 * MOE0.tiles // 4, "fetched": 16 * rows0 // 8})
        steps = {n: sem(f"{n}_step") for n in (
            "self0_norm", "cross0_heads", "cross0_norm", "ffn0", "self1_out", "self1_in", "self1_norm", "kv1",
            "cross1_heads", "cross1_in", "cross1_norm", "ffn1")}
        zero_filled, shared_loaded = sem("zero_filled"), sem("shared_loaded")
        expert_loaded = [sem("expert_loaded0"), sem("expert_loaded1")]
        router_loaded = [sem("router_loaded0"), sem("router_loaded1")]
        router_w = [sb(f"router_w{m.stage}", [128, CHUNKS, m.experts]) for m in (MOE0, MOE1)]
        router_bias = sb("router_bias", [128, 64])
        QKV1 = Signals({n: sem(f"self1_{n}") for n in ("tok_ready", "qkv_ready", "vT_psum")})
        PARTS1 = Signals({n: sem(f"parts1_{n}") for n in ("psum", "ready")})
        kv1_sems = {n: sem(f"kv1_{n}") for n in ("k_psum", "v_psum", "k_ready", "vq_ready", "vT_psum",
                                                 "v_ready", "zeroed")}
        ctx_sems = {n: sem(f"ctx_{n}") for n in ("T_psum", "T_ready", "k_psum", "v_psum", "k_ready", "v_ready", "zeroed", "step")}
        zeroed = sem("zeroed")
        LAST = (None, SELF0, CROSS0, FFN0, SELF1, CROSS1, FFN1)[min(stages, 6)]

        block = ctx.enter_context(nc.Block())

        def batches(eng, before, heads, after):
            before(0)
            with eng.Fori(0, BATCH - 1) as b:
                heads(b, True)
                before(b + 1)
                after(b)
            heads(BATCH - 1, False)
            after(BATCH - 1)

        class Steps:
            def __init__(self, eng, s, turn, steps):
                self.eng, self.s, self.steps, self.n = eng, s, steps, 0
                self.base = turn * steps if steps else 0

            def __call__(self, ins):
                self.n += 1
                ins.then_inc(self.s, 1)
                self.eng.wait_ge(self.s, self.base + self.n)

            def done(self):
                assert self.n == self.steps, self.n

        def head_rows(h):
            r = (h % 8) // 4 * 64
            return slice(r, r + 64), h // 8, h % 4

        @block.sync
        def _(sp):
            def tile_traffic(sp, moe, S):
                def load(j, u):
                    sp.dma_start(xg[u], sorted_x[moe.stage][bass.ds(j * TILE, TILE), :]).then_inc(S["loaded"][u], 16)

                def turn(j, u, load_next=True, store_last=True):
                    if load_next:
                        sp.wait_ge(*S("t_psum", j + 1))
                        load(j + 4, u)
                    if store_last:
                        v = (u + 1) % 4
                        sp.wait_ge(*S("y_copied", j - 2))
                        sp.dma_start(sorted_y[moe.stage][bass.ds((j - 3) * TILE, TILE), :], y_tile[v])\
                          .then_inc(S["stored"][v], 16)

                sp.wait_ge(*S("sent", 16 * TILES * moe.picks))
                for u in range(4):
                    load(u, u)
                for u in range(4):
                    turn(u, u, store_last=u == 3)
                with sp.Fori(1, moe.tiles // 4 - 1) as q:
                    for u in range(4):
                        turn(q * 4 + u, u)
                for j in range(moe.tiles - 4, moe.tiles + 3):
                    turn(j, j % 4, load_next=False)

            sp.dma_start(const[:], t["const"][:, 0:C_CAUSAL1]).then_inc(const_loaded, 16)
            sp.dma_start(causal_f, t["const"][:, C_CAUSAL1:C_COLS]).then_inc(const_loaded, 16)
            sp.dma_start(x_res[:], t["x"].rearrange("(i p) d -> p i d", p=128)).then_inc(x_loaded, 16)
            def attention_weights(lot):
                for n in W_ATTN:
                    if W_ATTN[n] == lot:
                        sp.dma_start(w_in[n], t[n].rearrange("(c p) n -> p c n", p=128)).then_inc(w_loaded[lot], 16)
                for n in BIAS_COL:
                    if BIAS_COL[n] == lot:
                        sp.dma_start(bias_col[n], t[n]).then_inc(w_loaded[lot], 16)
                for n in BIAS_ROW:
                    if BIAS_ROW[n] == lot:
                        sp.dma_start(bias_row[n], t[n].partition_broadcast(128)).then_inc(w_loaded[lot], 16)

            attention_weights(0)
            sp.dma_start(ctx_tok[:], t["ctx_2048"].rearrange("(i p) d -> p i d", p=128)).then_inc(ctx_loaded, 16)
            attention_weights(1)
            sp.dma_start(router_w[0][:], t["L0_ffn_router_w"].rearrange("(c p) n -> p c n", p=128)).then_inc(router_loaded[0], 16)
            sp.dma_start(router_bias[:], t["L0_ffn_router_bias"].partition_broadcast(128)).then_inc(router_loaded[0], 16)
            sp.dma_start(router_w[1][:], t["L1_ffn_gate_w"].rearrange("(c p) n -> p c n", p=128)).then_inc(router_loaded[1], 16)
            for w, n in ((shared_in[0], "L0_ffn_swg"), (shared_in[1], "L0_ffn_swu"), (shared_out, "L0_ffn_swd")):
                sp.dma_start(w, t[n].rearrange("(c p) n -> p c n", p=128)).then_inc(shared_loaded, 16)
            sp.wait_ge(zeroed, 2)
            for m in (MOE0, MOE1):
                z = sorted_x[m.stage].rearrange("(p r) d -> p r d", p=128)
                for r in range(0, m.tiles, 8):
                    sp.dma_start(z[:, r:r + 8, :], zeros[:].unsqueeze(1).to_broadcast([128, 8, DIM])).then_inc(zero_filled, 16)
            for q in range(4):
                sp.dma_start(expert_in[:, q * 4096:(q + 1) * 4096], t["expert_in0"][:, q * 4096:(q + 1) * 4096])\
                  .then_inc(expert_loaded[0], 16)
            for q in range(2):
                sp.dma_start(expert_out[:, q * 4096:(q + 1) * 4096], t["expert_out0"][:, q * 4096:(q + 1) * 4096])\
                  .then_inc(expert_loaded[0], 16)
            if stages >= 3:
                if stages >= 4:
                    sp.wait_ge(*FFN0("sum_psum", BATCH))
                    attention_weights(2)
                    attention_weights(3)
                tile_traffic(sp, MOE0, FFN0)
            if stages >= 4:
                sp.wait_ge(*FFN0("y_psum", MOE0.tiles))
                for q in range(4):
                    sp.dma_start(expert_in[:, q * 4096:(q + 1) * 4096], t["expert_in1"][:, q * 4096:(q + 1) * 4096])\
                      .then_inc(expert_loaded[1], 16)
                for q in range(2):
                    sp.dma_start(expert_out[:, q * 4096:(q + 1) * 4096], t["expert_out1"][:, q * 4096:(q + 1) * 4096])\
                      .then_inc(expert_loaded[1], 16)
            if stages >= 6:
                tile_traffic(sp, MOE1, FFN1)
            sp.wait_ge(*LAST("x_ready", 1))
            sp.dma_start(out.rearrange("(i p) d -> p i d", p=128), x_res[:]).then_inc(stored, 16)
            sp.wait_ge(stored, 16)

        @block.tensor
        def _(pe):
            mm, tr = nc.tensor.matmul, nc.tensor.transpose

            def transposes(dst, src):
                for kc in range(CHUNKS):
                    for i in range(2):
                        last = tr(dst[:, kc * 256 + i * 128:kc * 256 + (i + 1) * 128],
                                  src[:, i, kc * 128:(kc + 1) * 128], ident)
                return last

            def features_out(dst, w, c0, src):
                for c in range(CHUNKS):
                    for kc in range(CHUNKS):
                        last = mm(dst[:, c * 256:(c + 1) * 256], w[:, kc, c0 + c * 128:c0 + (c + 1) * 128],
                                  src[:, kc, :], start=kc == 0, stop=kc == CHUNKS - 1)
                return last

            def tokens_out(dst, src, w, c0):
                for i in range(2):
                    for kc in range(CHUNKS):
                        last = mm(dst[:, i * 256:(i + 1) * 256], src[:, kc, i * 128:(i + 1) * 128],
                                  w[:, kc, c0:c0 + DIM], start=kc == 0, stop=kc == CHUNKS - 1)
                return last

            def transpose_in(S, b):
                pe.wait_ge(*S("xb_ready", b + 1))
                transposes(bank[X_BANK], xb).then_inc(S["xT_psum"], 1)
                pe.wait_ge(*S("xT_ready", b + 1))

            def back_to_tokens(S, b, g):
                pe.wait_ge(*S("ot_ready", b * GROUPS + g + 1))
                pe.wait_ge(*S("o_ready", b * GROUPS + g))
                for i in range(2):
                    last = tr(bank[BACK_BANK][:, i * 128:(i + 1) * 128], oT4[g % 2][:, i * 128:(i + 1) * 128], ident)
                last.then_inc(S["back_psum"], 1)

            def project_out(S, b, wo):
                pe.wait_ge(*S("o_ready", (b + 1) * GROUPS))
                transposes(bank[X_BANK], o_tok).then_inc(S["oT_psum"], 1)
                pe.wait_ge(*S("oT_ready", b + 1))
                tokens_out(bank[PROJ_BANK], oT, wo, 0).then_inc(S["proj_psum"], 1)

            pe.wait_ge(const_ready, CONSTS)
            pe.wait_ge(w_loaded[0], LOADS[0])
            S = SELF0

            def before(b):
                transpose_in(S, b)
                W = w_in["L0_attn_w_attn"]
                features_out(bank[K_BANK], W, DIM, xT).then_inc(S["k_psum"], 1)
                features_out(bank[Q_BANK], W, 0, xT).then_inc(S["q_psum"], 1)
                pe.wait_ge(*S("o_ready", b * GROUPS))
                tokens_out(bank[V_BANK], xT, W, 2 * DIM).then_inc(S["v_psum"], 1)

            def heads(b, more):
                pe.wait_ge(*S("q_ready", b + 1))
                for i in range(HEADS + 4):
                    if i < HEADS:
                        rr, c, m = head_rows(i)
                        if i % 8 == 0:
                            pe.wait_ge(*S("km_ready", b * CHUNKS + i // 8 + 1))
                        if i >= 3:
                            pe.wait_ge(*S("p_ready", b * HEADS + i - 2))
                        s = bank[S_BANKS[i % 3]]
                        mm(s[:, 0:128], qT[rr, c, 0:128], kTm[rr, c, m, 0:128], start=True, stop=False)
                        mm(s[:, 0:128], ident_b[:], causal_b[:], start=False, stop=True)
                        mm(s[:, 128:384], qT[rr, c, 128:256], kTm[rr, c, m, :], start=True, stop=False)
                        mm(s[:, 256:384], ident_b[:], causal_b[:], start=False, stop=True).then_inc(S["s_psum"], 1)
                    if 2 <= i < HEADS + 2:
                        h = i - 2
                        pe.wait_ge(*S("p_ready", b * HEADS + h + 1))
                        if h >= 2:
                            pe.wait_ge(*S("pT_ready", b * HEADS + h - 1))
                        elif h == 0:
                            pe.wait_ge(*S("y_ready", b))
                        for j in range(3):
                            last = tr(bank[PT_BANKS[h % 2]][:, j * 128:(j + 1) * 128],
                                      probs[h % 3][:, j * 128:(j + 1) * 128], ident)
                        last.then_inc(S["pT_psum"], 1)
                    if 3 <= i < HEADS + 3:
                        h = i - 3
                        if h == 0:
                            pe.wait_ge(*S("v_ready", b + 1))
                        if h % 4 == 0:
                            pe.wait_ge(*S("ot_ready", b * GROUPS + h // 4))
                        pe.wait_ge(*S("pT_ready", b * HEADS + h + 1))
                        o, m = bank[PV_BANK], slice(32 * (h % 4), 32 * (h % 4) + 32)
                        mm(o[m, 0:256], v32[:, 0, h, :], probsT[h % 2][:, 0:256], start=True, stop=False)
                        mm(o[m, 128:256], v32[:, 1, h, :], probsT[h % 2][:, 256:384], start=False, stop=True)\
                            .then_inc(S["pv_psum"], 1)
                    if i >= 7 and i % 4 == 3:
                        back_to_tokens(S, b, i // 4 - 1)

            batches(pe, before, heads, lambda b: project_out(S, b, w_in["L0_attn_w_proj"]))
            if stages == 1:
                return

            pe.wait_ge(w_loaded[1], LOADS[1])
            pe.wait_ge(ctx_loaded, 16)
            pe.wait_ge(*SELF0("x_ready", 1))
            transposes(bank[X_BANK], ctx_tok).then_inc(ctx_sems["T_psum"], 1)
            pe.wait_ge(ctx_sems["T_ready"], 2)
            features_out(bank[K_BANK], w_in["L0_xattn_Wk"], 0, ctxT).then_inc(ctx_sems["k_psum"], 1)
            for bb in range(BATCH):
                for kc in range(CHUNKS):
                    last = mm(bank[4 + bb // 2][:, bb % 2 * 256:bb % 2 * 256 + 256],
                              ctxT2[:, kc, bb].rearrange("p a k -> p (a k)"), w_in["L0_xattn_Wv"][:, kc, :],
                              start=kc == 0, stop=kc == 1)
            last.then_inc(ctx_sems["v_psum"], 1)
            pe.wait_ge(ctx_sems["k_ready"], 1)
            pe.wait_ge(ctx_sems["v_ready"], 1)
            S = CROSS0

            def before(b):
                transpose_in(S, b)
                features_out(bank[Q_BANK], w_in["L0_xattn_Wq"], 0, xT).then_inc(S["q_psum"], 1)

            def heads(b, more):
                pe.wait_ge(*S("q_ready", b + 1))
                pe.wait_ge(*S("km_ready", (b + 1) * CHUNKS))
                for i in range(GROUPS + 4):
                    if i < GROUPS:
                        rr, c, _ = head_rows(4 * i)
                        if i == 3:
                            pe.wait_ge(*S("shift_ready", b * GROUPS + 1))
                        for j in range(2):
                            last = mm(bank[S_BANKS[i % 3]][:, j * 256:(j + 1) * 256], qT[rr, c, j * 128:(j + 1) * 128],
                                      kTm[rr, c, :, 0:CTX], start=True, stop=True)
                        last.then_inc(S["s_psum"], 1)
                    if 2 <= i < GROUPS + 2:
                        g = i - 2
                        pe.wait_ge(*S("p_ready", b * GROUPS + g + 1))
                        if g >= 2:
                            pe.wait_ge(*S("pT_ready", b * GROUPS + g - 1))
                        elif g == 0:
                            pe.wait_ge(*S("y_ready", b))
                        for pair in range(2):
                            for j in range(2):
                                last = tr(bank[PT_BANKS[g % 2]][:, pair * 256 + j * 128:pair * 256 + (j + 1) * 128],
                                          probs[g % 3][:, j * 256 + pair * 128:j * 256 + (pair + 1) * 128], ident)
                        last.then_inc(S["pT_psum"], 1)
                    if 3 <= i < GROUPS + 3:
                        g = i - 3
                        if g == 0:
                            pe.wait_ge(*S("v_ready", b + 1))
                        pe.wait_ge(*S("ot_ready", b * GROUPS + g))
                        pe.wait_ge(*S("pT_ready", b * GROUPS + g + 1))
                        for m in range(4):
                            last = mm(bank[PV_BANK][32 * m:32 * m + 32, 0:256], v32[:, 0, 4 * g + m, :],
                                      probsT[g % 2][:, m // 2 * 256:m // 2 * 256 + 256], start=True, stop=True)
                        last.then_inc(S["pv_psum"], 1)
                    if i >= 4:
                        back_to_tokens(S, b, i - 4)

            batches(pe, before, heads, lambda b: project_out(S, b, w_in["L0_xattn_Wo"]))
            if stages == 2:
                return

            def router(S, moe, b):
                transpose_in(S, b)
                pe.wait_ge(*S("logit_ready", b))
                for i in range(2):
                    for kc in range(CHUNKS):
                        last = mm(bank[K_BANK][:, i * 64:i * 64 + moe.experts], xT[:, kc, i * 128:(i + 1) * 128],
                                  router_w[moe.stage][:, kc, :], start=kc == 0, stop=kc == 1)
                last.then_inc(S["logit_psum"], 1)

            def count_tokens(S, moe):
                E = moe.experts
                pe.wait_ge(*S("mask_ready", 1))
                m = mask_b[:, :, 0:E]
                r = bank[0][:, 0:TILES * E].rearrange("p (i e) -> p i e", i=TILES)
                mm(r, tri_b[:], m, start=True, stop=False)
                for d in range(1, TILES):
                    mm(r[:, d:TILES], ones_b[:], m[:, 0:TILES - d], start=False, stop=d == TILES - 1)
                for i in range(TILES):
                    last = mm(bank[1][:, 0:E], ones_b[:], m[:, i], start=i == 0, stop=i == TILES - 1)
                last.then_inc(S["rank_psum"], 1)
                pe.wait_ge(*S("e_ready", 1))
                mm(bank[2][:, 0:128], ones_f[:], e_diag, start=True, stop=True).then_inc(S["e_psum"], 1)

            def expert_tiles(S, moe):
                H = moe.hidden
                small = moe is MOE0
                w_gu = expert_in[:].rearrange("p (e c n) -> p e c n", e=moe.experts, c=CHUNKS)
                w_d = expert_out[:].rearrange("p (e c n) -> p e c n", n=DIM, c=1 if small else H // 128)
                PEe = [mybir.EngineType.PE]

                def experts(row, j, n):
                    src = tile_expert[0:1, row, bass.ds(j, n)]
                    _, v = nc.values_load_multi_w_load_instructions(
                        src, engines=PEe, min_val=0, max_val=(moe.experts - 1) >> row,
                        skip_runtime_bounds_check_because="routing clamps them to the experts there are")
                    return v

                def turn(j, u, e_gu, e_d, first=True, second=True, third=True, fourth=True):
                    if first:
                        pe.wait_ge(*S("loaded", 16 * (j // 4 + 1) if isinstance(j, int) else j4_loads, u))
                        for kc in range(CHUNKS):
                            last = tr(bank[u % 2][:, kc * 128:(kc + 1) * 128], xg[u][:, kc * 128:(kc + 1) * 128], ident)
                        last.then_inc(S["t_psum"], 1)
                    if second:
                        a = (u + 1) % 2
                        pe.wait_ge(*S("t_ready", j))
                        for n in range(1 if small else 2):
                            for kc in range(CHUNKS):
                                dst = bank[2 + a + 2 * n][:, 0:(2 * H if small else H)]
                                w = w_gu[:, bass.ds(e_gu, 1), kc, :] if small else \
                                    w_gu[:, bass.ds(e_gu, 1), kc, n * H:(n + 1) * H]
                                last = mm(dst, xgT[a][:, kc, :], w, start=kc == 0, stop=kc == 1)
                        last.then_inc(S["gu_psum"], 1)
                    if third:
                        pe.wait_ge(*S("h_ready", j - 1))
                        if fourth:
                            pe.wait_ge(*S("hT_ready", j - 3 if small else j - 2))
                        for n in range(1 if small else 4):
                            last = tr(bank[moe.hT_banks[u % 2]][:, n * 128:(n + 1) * 128], hid[u % 2][:, n * 128:(n + 1) * 128], ident)
                        last.then_inc(S["hT_psum"], 1)
                    if fourth:
                        a = (u + 1) % 2
                        pe.wait_ge(*S("hT_ready", j - 2))
                        if not small or not isinstance(j, int) or j > 3:
                            pe.wait_ge(*S("y_copied", j - 4 if small else j - 3))
                        n_k = 1 if small else 4
                        for n in range(n_k):
                            last = mm(bank[moe.y_banks[a]][:, 0:DIM], hidT[a][:, n * 128:(n + 1) * 128], w_d[:, bass.ds(e_d, 1), n, :],
                                      start=n == 0, stop=n == n_k - 1)
                        last.then_inc(S["y_psum"], 1)

                row_d = 1 if small else 0
                pe.wait_ge(*S("routed", 1))
                pe.wait_ge(expert_loaded[moe.stage], 16 * 6)
                ev, ed = experts(0, 0, 4), experts(row_d, 0, 4)
                for j in range(4):
                    turn(j, j, ev[j - 1] if j else None, ed[j - 3] if j == 3 else None,
                         second=j >= 1, third=j >= 2, fourth=j >= 3)
                with pe.Fori(1, moe.tiles // 4) as q:
                    j = q * 4
                    ev, ed = experts(0, j - 1, 4), experts(row_d, j - 3, 4)
                    j4_loads = j * 4 + 16
                    for u in range(4):
                        turn(j + u, u, ev[u], ed[u])
                ev, ed = experts(0, moe.tiles - 1, 1), experts(row_d, moe.tiles - 3, 3)
                for u in range(3):
                    turn(moe.tiles + u, u, ev[0], ed[u], first=False, second=u == 0, third=u <= 1)

            S = FFN0
            pe.wait_ge(router_loaded[0], 32)
            pe.wait_ge(shared_loaded, 48)
            pe.wait_ge(*CROSS0("x_ready", 1))
            with pe.Fori(0, BATCH) as b:
                router(S, MOE0, b)
            count_tokens(S, MOE0)
            with pe.Fori(0, BATCH) as b:
                n_h = SHARED_HIDDEN // 128
                pe.wait_ge(*S("xb_s_ready", b + 1))
                transposes(bank[SX_BANK], xb_s).then_inc(S["xT_s_psum"], 1)
                pe.wait_ge(*S("xT_s_ready", b + 1))
                for hc in range(n_h):
                    pe.wait_ge(*S("hid_ready", b * n_h + max(hc - 1, 0)))
                    for n in range(2):
                        for kc in range(CHUNKS):
                            last = mm(bank[4 + hc % 2][:, n * 256:(n + 1) * 256], shared_in[n][:, kc, hc * 128:(hc + 1) * 128],
                                      xT_s[:, kc, :], start=kc == 0, stop=kc == 1)
                    last.then_inc(S["g_psum"], 1)
                pe.wait_ge(*S("y_init", b))
                for hc in range(n_h):
                    pe.wait_ge(*S("hid_ready", b * n_h + hc + 1))
                    for i in range(2):
                        last = mm(bank[6 + i][:, 0:256], hidden_s[:, hc, i * 128:(i + 1) * 128],
                                  shared_out[:, hc, :], start=hc == 0, stop=hc == n_h - 1)
                last.then_inc(S["sum_psum"], 1)
            pe.wait_ge(*S("y_init", BATCH))
            expert_tiles(S, MOE0)
            if stages == 3:
                return

            def full_heads(S, b, quantised):
                vv, pT = (v32_b, probsT_b) if quantised else (v32, probsT)
                for i in range(HEADS + 4):
                    if i < HEADS:
                        rr, c, m = head_rows(i)
                        if not quantised and i % 8 == 0:
                            pe.wait_ge(*S("km_ready", b * CHUNKS + i // 8 + 1))
                        if quantised and i in (0, 3):
                            pe.wait_ge(*PARTS1("ready", b * 4 + 5 + i))
                        if i >= 3:
                            pe.wait_ge(*S("p_ready", b * HEADS + i - 2))
                        for j in range(2):
                            s = bank[S_BANKS[i % 3]][:, j * SEQ:(j + 1) * SEQ]
                            if quantised:
                                half = slice(i % 2 * 64, i % 2 * 64 + 64)
                                last = mm(s, q_parts[half, i // 2, j * 128:(j + 1) * 128], k_parts[half, i // 2, :],
                                          start=True, stop=True)
                            else:
                                mm(s, qT[rr, c, j * 128:(j + 1) * 128], kTm[rr, c, m, :], start=True, stop=False)
                                last = mm(s, ident_h[:], causal_h[:, j, :], start=False, stop=True)
                        last.then_inc(S["s_psum"], 1)
                    if i == 1 and not quantised:
                        pe.wait_ge(*QKV1("qkv_ready", b * 3 + 3))
                        for st in range(2):
                            for c in range(CHUNKS):
                                last = tr(bank[Q_BANK][:, st * 256 + c * 128:st * 256 + (c + 1) * 128],
                                          vT[:, c, st * 128:(st + 1) * 128], ident)
                        last.then_inc(QKV1["vT_psum"], 1)
                    if 2 <= i < HEADS + 2:
                        h = i - 2
                        pe.wait_ge(*S("p_ready", b * HEADS + h + 1))
                        if h >= 2:
                            pe.wait_ge(*S("pT_ready", b * HEADS + h - 1))
                        elif h == 0:
                            pe.wait_ge(*S("y_ready", b))
                        for kt in range(2):
                            for j in range(2):
                                last = tr(bank[PT_BANKS[h % 2]][:, kt * SEQ + j * 128:kt * SEQ + (j + 1) * 128],
                                          probs[h % 3][:, j * SEQ + kt * 128:j * SEQ + (kt + 1) * 128], ident)
                        last.then_inc(S["pT_psum"], 1)
                    if 3 <= i < HEADS + 3:
                        h = i - 3
                        if h == 0 and not quantised:
                            pe.wait_ge(*S("v_ready", b + 1))
                        if h % 4 == 0:
                            pe.wait_ge(*S("ot_ready", b * GROUPS + h // 4))
                        pe.wait_ge(*S("pT_ready", b * HEADS + h + 1))
                        m = slice(32 * (h % 4), 32 * (h % 4) + 32)
                        for kt in range(2):
                            last = mm(bank[PV_BANK][m, 0:SEQ], vv[:, kt, h, :], pT[h % 2][:, kt * SEQ:(kt + 1) * SEQ],
                                      start=kt == 0, stop=kt == 1)
                        last.then_inc(S["pv_psum"], 1)
                    if i >= 7 and i % 4 == 3:
                        back_to_tokens(S, b, i // 4 - 1)

            pe.wait_ge(w_loaded[2], LOADS[2])
            pe.wait_ge(*FFN0("x_ready", 1))
            S = SELF1

            def before(b):
                transpose_in(S, b)
                for n, bk, done in ((1, K_BANK, "k_psum"), (0, Q_BANK, "q_psum"), (2, V_BANK, "v_psum")):
                    if n == 2:
                        pe.wait_ge(*S("o_ready", b * GROUPS))
                    tokens_out(bank[bk], xT, w_in["L1_attn_w_qkv"], n * DIM).then_inc(S[done], 1)

            def heads(b, more):
                pe.wait_ge(*QKV1("qkv_ready", b * 3 + 2))
                full_heads(S, b, False)

            def after(b):
                pe.wait_ge(*S("oT_ready", b + 1))
                tokens_out(bank[PROJ_BANK], oT, w_in["L1_attn_w_out"], 0).then_inc(S["proj_psum"], 1)

            batches(pe, before, heads, after)
            if stages == 4:
                return

            pe.wait_ge(w_loaded[3], LOADS[3])
            pe.wait_ge(*SELF1("x_ready", 1))
            Wkv = w_in["L1_xattn_Wkv"]
            tokens_out(bank[K_BANK], ctxT, Wkv, 0).then_inc(kv1_sems["k_psum"], 1)
            features_out(bank[V_BANK], Wkv, DIM, ctxT).then_inc(kv1_sems["v_psum"], 1)
            def parts_T():
                flat = expanded.rearrange("p (i h) c d -> p i (h c d)", i=2)
                for n, bk in enumerate(EXP_BANKS):
                    for pair in range(2):
                        c0 = (2 * n + pair) * 128
                        for i in range(2):
                            last = mm(bank[bk][:, pair * 256 + i * 128:pair * 256 + (i + 1) * 128],
                                      flat[:, i, c0:c0 + 128], ident_b[:], start=True, stop=True)
                    last.then_inc(PARTS1["psum"], 1)

            pe.wait_ge(kv1_sems["vq_ready"], 1)
            for st in range(2):
                for c in range(CHUNKS):
                    last = tr(bank[Q_BANK][:, st * 256 + c * 128:st * 256 + (c + 1) * 128],
                              vq[:, c, st * 128:(st + 1) * 128], ident)
            last.then_inc(kv1_sems["vT_psum"], 1)
            pe.wait_ge(kv1_sems["v_ready"], 1)
            pe.wait_ge(kv1_sems["k_ready"], 1)
            parts_T()
            pe.wait_ge(*PARTS1("ready", 4))
            S = CROSS1

            def before(b):
                transpose_in(S, b)
                tokens_out(bank[Q_BANK], xT, w_in["L1_xattn_Wq"], 0).then_inc(S["q_psum"], 1)

            def heads(b, more):
                pe.wait_ge(*S("k_ready", b + 1))
                pe.wait_ge(*S("o_ready", b * GROUPS))
                parts_T()
                full_heads(S, b, True)

            batches(pe, before, heads, lambda b: project_out(S, b, w_in["L1_xattn_Wp"]))
            if stages == 5:
                return

            S = FFN1
            pe.wait_ge(*CROSS1("x_ready", 1))
            pe.wait_ge(router_loaded[1], 16)
            with pe.Fori(0, BATCH) as b:
                router(S, MOE1, b)
            count_tokens(S, MOE1)
            expert_tiles(S, MOE1)

        @block.scalar
        def _(act):
            A = nc.scalar.activation

            def rows_in(S, b):
                act.wait_ge(*S("xT_psum", b))
                act.wait_ge(*S("xbo_ready", b))
                A(xb, x_res[:, bass.ds(b * 2, 2), :], ACT.Copy).then_inc(S["xb_ready"], 1)

            def rows_T(S, b):
                act.wait_ge(*S("xT_psum", b + 1))
                A(xT[:].rearrange("p c n -> p (c n)"), bank[X_BANK][:], ACT.Copy).then_inc(S["xT_ready"], 1)

            def query_out(S, b, bias):
                act.wait_ge(*S("q_psum", b + 1))
                for c in range(CHUNKS):
                    last = A(qT[:, c, :], bank[Q_BANK][:, c * 256:(c + 1) * 256], ACT.Identity,
                             bias=bias[:, c:c + 1], scale=SCALE)
                last.then_inc(S["q_ready"], 1)

            def group_out(S, b, g, done):
                act.wait_ge(*S("pv_psum", done))
                if g >= 2:
                    act.wait_ge(*S("back_psum", b * GROUPS + g - 1))
                A(oT4[g % 2][:], bank[PV_BANK][:, 0:256], ACT.Copy).then_inc(S["ot_ready"], 1)

            def outputs_T(S, b, bias):
                act.wait_ge(*S("oT_psum", b + 1))
                for c in range(CHUNKS):
                    last = A(oT[:, c, :], bank[X_BANK][:, c * 256:(c + 1) * 256], ACT.Identity, bias=bias[:, c:c + 1])
                last.then_inc(S["oT_ready"], 1)

            act.wait_ge(x_loaded, 16)
            act.wait_ge(w_loaded[0], LOADS[0])
            act.wait_ge(const_ready, CONSTS)
            S = SELF0

            def before(b):
                rows_T(S, b)
                query_out(S, b, qbias[0])
                act.wait_ge(*S("v_psum", b + 1))
                for i in range(2):
                    last = A(v32[:, i, :, 0:HEAD_DIM],
                             bank[V_BANK][:, i * 256:(i + 1) * 256].rearrange("p (h d) -> p h d", d=HEAD_DIM), ACT.Copy)
                last.then_inc(S["v_ready"], 1)

            def heads(b, more):
                for h in range(HEADS + 3):
                    if h < HEADS:
                        act.wait_ge(*S("max_ready", b * HEADS + h + 1))
                        if h >= 3:
                            act.wait_ge(*S("pT_psum", b * HEADS + h - 2))
                        for i, c0, c1 in ((0, 0, 128), (1, 128, 384)):
                            last = A(probs[h % 3][:, c0:c1], bank[S_BANKS[h % 3]][:, c0:c1], ACT.Exp,
                                     bias=neg_max[:, h, i:i + 1])
                        last.then_inc(S["p_ready"], 1)
                    if more and h == 8:
                        rows_in(S, b + 1)
                    if h >= 6 and h % 4 == 2:
                        group_out(S, b, h // 4 - 1, b * HEADS + h - 2)

            rows_in(S, 0)
            batches(act, before, heads, lambda b: outputs_T(S, b, bias_col["L0_attn_b_attn"][:, 4:6]))
            if stages == 1:
                return

            act.wait_ge(w_loaded[1], LOADS[1])
            act.wait_ge(*SELF0("x_ready", 1))
            act.wait_ge(ctx_sems["T_psum"], 1)
            A(ctxT[:].rearrange("p c n -> p (c n)"), bank[X_BANK][:], ACT.Copy).then_inc(ctx_sems["T_ready"], 1)
            for a in range(2):
                last = A(ctxT2[:, :, :, a, :], bank[X_BANK][:].rearrange("p (c b k) -> p c b k", c=2, b=4), ACT.Copy)
            last.then_inc(ctx_sems["T_ready"], 1)
            act.wait_ge(ctx_sems["k_psum"], 1)
            for c in range(CHUNKS):
                last = A(ckT[:, c, :], bank[K_BANK][:, c * 256:(c + 1) * 256], ACT.Identity,
                         bias=bias_col["L0_xattn_bk"][:, c:c + 1])
            last.then_inc(ctx_sems["k_ready"], 1)
            act.wait_ge(ctx_sems["v_psum"], 1)
            for bb in range(BATCH):
                last = A(cv[:, bb, :], bank[4 + bb // 2][:, bb % 2 * 256:bb % 2 * 256 + 256], ACT.Copy)
            last.then_inc(ctx_sems["v_ready"], 1)
            S = CROSS0

            def before(b):
                rows_T(S, b)
                query_out(S, b, qbias[1])

            def heads(b, more):
                for g in range(GROUPS + 3):
                    if g < GROUPS:
                        act.wait_ge(*S("shift_ready", b * GROUPS + g + 1))
                        A(probs[g % 3][:], probs[g % 3][:], ACT.Exp).then_inc(S["p_ready"], 1)
                    if 2 <= g < GROUPS + 2:
                        act.wait_ge(*S("pT_psum", b * GROUPS + g - 1))
                        if g >= 4:
                            act.wait_ge(*S("pv_psum", b * GROUPS + g - 3))
                        A(probsT[g % 2], bank[PT_BANKS[g % 2]][:], ACT.Copy).then_inc(S["pT_ready"], 1)
                    if more and g == 2:
                        rows_in(S, b + 1)
                    if g >= 3:
                        group_out(S, b, g - 3, b * GROUPS + g - 2)

            rows_in(S, 0)
            batches(act, before, heads, lambda b: outputs_T(S, b, bias_col["L0_xattn_bv"]))
            if stages == 2:
                return

            def route_exp(S, moe):
                act.wait_ge(*S("exp_in", 1))
                A(expw[:, :, 0:moe.experts], expw[:, :, 0:moe.experts], ACT.Exp).then_inc(S["exp_ready"], 1)

            def expert_tiles(S, moe):
                H = moe.hidden

                def turn(j, u, first=True, second=True, early=False):
                    if first:
                        act.wait_ge(*S("t_psum", j + 1))
                        if not early:
                            act.wait_ge(*S("gu_psum", j - 1))
                        A(xgT[u % 2].rearrange("p c n -> p (c n)"), bank[u % 2][:, 0:DIM], ACT.Copy)\
                            .then_inc(S["t_ready"], 1)
                    if second:
                        a = (u + 1) % 2
                        act.wait_ge(*S("gu_psum", j))
                        if not early:
                            act.wait_ge(*S("h_ready", j - 2))
                        A(silu_g[a][:, 0:H], bank[2 + a][:, 0:H], ACT.Silu).then_inc(S["act_ready"], 1)

                for j in range(4):
                    turn(j, j, second=j >= 1, early=j < 2)
                with act.Fori(1, moe.tiles // 4) as q:
                    for u in range(4):
                        turn(q * 4 + u, u)
                turn(moe.tiles, 0, first=False)

            def router_rows(S):
                with act.Fori(0, BATCH) as b:
                    act.wait_ge(*S("xT_psum", b))
                    A(xb, x_res[:, bass.ds(b * 2, 2), :], ACT.Copy).then_inc(S["xb_ready"], 1)
                    act.wait_ge(*S("xT_psum", b + 1))
                    act.wait_ge(*S("logit_psum", b))
                    A(xT.rearrange("p c n -> p (c n)"), bank[X_BANK][:], ACT.Copy).then_inc(S["xT_ready"], 1)

            S = FFN0
            act.wait_ge(*CROSS0("x_ready", 1))
            router_rows(S)
            route_exp(S, MOE0)
            with act.Fori(0, BATCH) as b:
                act.wait_ge(*S("y_init", b))
                A(xb_s, x_res[:, bass.ds(b * 2, 2), :], ACT.Copy).then_inc(S["xb_s_ready"], 1)
                act.wait_ge(*S("xT_s_psum", b + 1))
                A(xT_s.rearrange("p c n -> p (c n)"), bank[SX_BANK][:], ACT.Copy).then_inc(S["xT_s_ready"], 1)
                for hc in range(4):
                    act.wait_ge(*S("g_psum", b * 4 + hc + 1))
                    act.wait_ge(*S("hid_ready", b * 4 + max(hc - 1, 0)))
                    A(silu_s[hc % 2], bank[4 + hc % 2][:, 0:256], ACT.Silu).then_inc(S["silu_ready"], 1)
            expert_tiles(S, MOE0)
            if stages == 3:
                return

            act.wait_ge(*FFN0("x_ready", 1))
            S = SELF1

            def before(b):
                rows_T(S, b)
                for n, (bk, psum, dst) in enumerate(((K_BANK, "k_psum", k_tok), (Q_BANK, "q_psum", q_tok),
                                                     (V_BANK, "v_psum", v_tok))):
                    act.wait_ge(*S(psum, b + 1))
                    act.wait_ge(*QKV1("qkv_ready", b * 3))
                    A(dst.rearrange("p i d -> p (i d)"), bank[bk][:], ACT.Copy, scale=SCALE if n == 1 else 1.0)\
                        .then_inc(QKV1["tok_ready"], 1)

            def heads(b, more):
                for h in range(HEADS + 3):
                    if h == 1:
                        act.wait_ge(*QKV1("vT_psum", b + 1))
                        A(v32[:, :, :, 0:HEAD_DIM], bank[Q_BANK][:].rearrange("p (i h d) -> p i h d", i=2, h=HEADS),
                          ACT.Copy).then_inc(S["v_ready"], 1)
                    if h < HEADS:
                        act.wait_ge(*S("max_ready", b * HEADS + h + 1))
                        if h >= 3:
                            act.wait_ge(*S("pT_psum", b * HEADS + h - 2))
                        for i in range(2):
                            last = A(probs[h % 3][:, i * SEQ:(i + 1) * SEQ], bank[S_BANKS[h % 3]][:, i * SEQ:(i + 1) * SEQ],
                                     ACT.Exp, bias=neg_max[:, h, i:i + 1])
                        last.then_inc(S["p_ready"], 1)
                    if more and h == 8:
                        rows_in(S, b + 1)
                    if h >= 6 and h % 4 == 2:
                        group_out(S, b, h // 4 - 1, b * HEADS + h - 2)

            rows_in(S, 0)
            batches(act, before, heads, lambda b: None)
            if stages == 4:
                return

            act.wait_ge(*SELF1("x_ready", 1))
            def parts_out(dst, lot, first, last):
                for n in range(first, last):
                    act.wait_ge(*PARTS1("psum", lot * 4 + n + 1))
                    A(dst[:, 2 * n:2 * n + 2, :].rearrange("p h n -> p (h n)"), bank[EXP_BANKS[n]][:], ACT.Copy)\
                        .then_inc(PARTS1["ready"], 1)

            act.wait_ge(kv1_sems["vT_psum"], 1)
            act.wait_ge(kv1_sems["zeroed"], 1)
            A(v32_b[:, :, :, 0:HEAD_DIM], bank[Q_BANK][:].rearrange("p (i h d) -> p i h d", i=2, h=HEADS), ACT.Copy)\
                .then_inc(kv1_sems["v_ready"], 1)
            parts_out(k_parts, 0, 0, 4)
            S = CROSS1

            def heads(b, more):
                parts_out(q_parts, b + 1, 0, 4)
                for h in range(HEADS + 3):
                    if 2 <= h < HEADS + 2:
                        act.wait_ge(*S("pT_psum", b * HEADS + h - 1))
                        if h >= 4:
                            act.wait_ge(*S("pT_ready", b * HEADS + h - 3))
                        A(p_shifted[h % 2], bank[PT_BANKS[h % 2]][:], ACT.Copy, scale=PROB_LEVELS, bias=ROUND)\
                            .then_inc(S["shift_ready"], 1)
                    if h < HEADS:
                        act.wait_ge(*S("max_ready", b * HEADS + h + 1))
                        if h >= 3:
                            act.wait_ge(*S("pT_psum", b * HEADS + h - 2))
                        for i in range(2):
                            last = A(probs[h % 3][:, i * SEQ:(i + 1) * SEQ], bank[S_BANKS[h % 3]][:, i * SEQ:(i + 1) * SEQ],
                                     ACT.Exp, bias=shift[:, h, i:i + 1], scale=q_scale[:, i, h:h + 1],
                                     accum_out=row_sum[:, h, i:i + 1])
                        last.then_inc(S["p_ready"], 1)
                    if more and h == 8:
                        rows_in(S, b + 1)
                    if h >= 6 and h % 4 == 2:
                        group_out(S, b, h // 4 - 1, b * HEADS + h - 2)

            def after(b):
                act.wait_ge(*S("oT_psum", b + 1))
                for c in range(CHUNKS):
                    last = A(oT[:, c, :], bank[X_BANK][:, c * 256:(c + 1) * 256], ACT.Copy, scale=v_scale[:, c:c + 1])
                last.then_inc(S["oT_ready"], 1)

            rows_in(S, 0)
            batches(act, lambda b: rows_T(S, b), heads, after)
            if stages == 5:
                return

            S = FFN1
            act.wait_ge(*CROSS1("x_ready", 1))
            router_rows(S)
            route_exp(S, MOE1)
            expert_tiles(S, MOE1)

        @block.vector
        def _(dve):
            V = nc.vector

            def normalise_group(S, b, g, step, summed=False):
                dve.wait_ge(*S("back_psum", b * GROUPS + g + 1))
                o = bank[BACK_BANK][:, 0:256].rearrange("p (i m d) -> p i m d", i=2, m=4)
                inv = row_inv[:, g % 2]
                if summed:
                    step(V.reciprocal(inv, row_sum[:, 4 * g:4 * g + 4, :].rearrange("p m i -> p i m")))
                else:
                    step(V.reciprocal(inv, o[:, :, :, HEAD_DIM]))
                V.tensor_tensor(o_tok[:, :, g * 64:(g + 1) * 64].rearrange("p i (m d) -> p i m d", m=4),
                                o[:, :, :, 0:HEAD_DIM], inv.unsqueeze(3).to_broadcast([128, 2, 4, HEAD_DIM]), ALU.mult)\
                    .then_inc(S["o_ready"], 1)

            def normalise(src, dst, n, step, done):
                for i in range(n):
                    last = V.bn_stats(stats[:, i, :], src(i))
                step(last)
                V.memset(spacer[:], 0.0)
                for i in range(n):
                    last = V.bn_aggr(mean_var[:, i, :], stats[:, i, :])
                step(last)
                v, bits, y, r = rs_v[:, 0:n], rs_bits[:, 0:n], rs_y[:, 0:n], rs_t[:, 0:n]
                step(V.tensor_scalar(v, mean_var[:, 0:n, 1], EPS, None, ALU.add))
                step(V.tensor_scalar(bits, v.bitcast(i32), 1, None, ALU.logical_shift_right))
                step(V.tensor_scalar(y.bitcast(i32), bits, -1.0, RSQRT_SEED, ALU.mult, ALU.add))
                for _ in range(4):
                    step(V.tensor_tensor(r, y, y, ALU.mult))
                    step(V.tensor_tensor(r, r, v, ALU.mult))
                    step(V.tensor_scalar(r, r, -0.5, 1.5, ALU.mult, ALU.add))
                    step(V.tensor_tensor(y, y, r, ALU.mult))
                for i in range(n):
                    last = V.tensor_scalar(dst(i), src(i), mean_var[:, i, 0:1], rs_y[:, i:i + 1],
                                           ALU.subtract, ALU.mult)
                last.then_inc(done, 1)

            def add_rows(S, b):
                dve.wait_ge(*S("proj_psum", b + 1))
                dve.wait_ge(*S("xbo_ready", b + 1))
                V.tensor_tensor(y_acc[:, bass.ds(b * 2, 2), :], bank[PROJ_BANK][:].rearrange("p (i d) -> p i d", i=2),
                                xbo, ALU.add).then_inc(S["y_ready"], 1)

            def layernorm_all(S, step):
                normalise(lambda i: y_acc[:, i, :], lambda i: x_res[:, i, :], TILES, step, S["x_ready"])


            dve.wait_ge(const_loaded, 32)
            V.tensor_copy(ident_b[:], ident).then_inc(const_ready, 1)
            V.tensor_copy(ident_h[:], ident).then_inc(const_ready, 1)
            V.tensor_copy(causal_b[:], const[:, C_CAUSAL:C_CAUSAL + 128]).then_inc(const_ready, 1)
            V.tensor_copy(tri_b[:], const[:, C_TRI:C_TRI + 128])
            V.tensor_copy(causal_h[:].rearrange("p i k -> p (i k)"), causal_f)
            V.memset(ones_b[:], 1.0)
            V.memset(ones_f[:], 1.0)
            V.memset(v32, 0.0).then_inc(zeroed, 1)
            dve.wait_ge(zeroed, 1)
            V.memset(v32[:, :, :, HEAD_DIM], 1.0).then_inc(const_ready, 1)
            V.memset(zeros[:], 0.0).then_inc(zeroed, 1)
            dve.wait_ge(w_loaded[0], LOADS[0])
            V.tensor_scalar(qbias[0][:], bias_col["L0_attn_b_attn"][:, 0:2], SCALE, None, ALU.mult).then_inc(const_ready, 1)
            dve.wait_ge(w_loaded[1], LOADS[1])
            V.tensor_scalar(qbias[1][:], bias_col["L0_xattn_bq"], SCALE, None, ALU.mult).then_inc(const_ready, 1)

            S = SELF0

            def before(b):
                dve.wait_ge(*S("k_psum", b + 1))
                dve.wait_ge(*S("km_ready", b * CHUNKS))
                for c in range(CHUNKS):
                    last = V.tensor_scalar(kT[:, c, :], bank[K_BANK][:, c * 256:(c + 1) * 256],
                                           bias_col["L0_attn_b_attn"][:, 2 + c:3 + c], None, ALU.add)
                last.then_inc(S["k_ready"], 1)

            def heads(b, more):
                step = Steps(dve, steps["self0_norm"], b, GROUPS)
                for h in range(HEADS + 4):
                    if h < HEADS:
                        dve.wait_ge(*S("s_psum", b * HEADS + h + 1))
                        s = bank[S_BANKS[h % 3]]
                        V.tensor_reduce(neg_max[:, h, 0:1], s[:, 0:128], AX.X, ALU.max, negate=True)
                        V.tensor_reduce(neg_max[:, h, 1:2], s[:, 128:384], AX.X, ALU.max, negate=True)\
                            .then_inc(S["max_ready"], 1)
                    if 2 <= h < HEADS + 2:
                        dve.wait_ge(*S("pT_psum", b * HEADS + h - 1))
                        if h >= 4:
                            dve.wait_ge(*S("pv_psum", b * HEADS + h - 3))
                        V.tensor_copy(probsT[h % 2][:, 0:384], bank[PT_BANKS[h % 2]][:, 0:384]).then_inc(S["pT_ready"], 1)
                    if h >= 7 and h % 4 == 3:
                        normalise_group(S, b, h // 4 - 1, step)
                step.done()

            batches(dve, before, heads, lambda b: add_rows(S, b))
            dve.wait_ge(*S("y_ready", BATCH))
            layernorm_all(S, Steps(dve, steps["self0_norm"], 1, BATCH * GROUPS))
            if stages == 1:
                return

            V.memset(v32[:, 0], 0.0).then_inc(ctx_sems["zeroed"], 1)
            dve.wait_ge(ctx_sems["zeroed"], 1)
            for a in range(2):
                last = V.memset(v32[64 * a:64 * a + 64, 0, a::2, HEAD_DIM], 1.0)
            last.then_inc(ctx_sems["zeroed"], 1)
            dve.wait_ge(ctx_sems["zeroed"], 2)
            dve.wait_ge(ctx_sems["v_ready"], 1)
            S = CROSS0

            def before(b):
                for a in range(2):
                    pp = slice(64 * a, 64 * a + 64)
                    last = V.tensor_copy(v32[pp, 0, a::2, 0:HEAD_DIM],
                                         cv[pp, bass.ds(b, 1), :].rearrange("p o (h a d) -> p (o h) a d", a=2, d=HEAD_DIM)[:, :, a, :])
                last.then_inc(S["v_ready"], 1)

            def heads(b, more):
                step = Steps(dve, steps["cross0_heads"], b, 2 * GROUPS)
                for i in range(GROUPS + 4):
                    if i < GROUPS:
                        dve.wait_ge(*S("s_psum", b * GROUPS + i + 1))
                        if i == 3:
                            dve.wait_ge(*S("pT_psum", b * GROUPS + 1))
                        s = bank[S_BANKS[i % 3]][:].rearrange("p (i m k) -> p i m k", i=2, m=4)
                        m = neg_max[:, 4 * i:4 * i + 4, :].rearrange("p m i -> p i m")
                        step(V.tensor_reduce(m, s, AX.X, ALU.max, negate=True))
                        V.tensor_tensor(probs[i % 3][:].rearrange("p (i m k) -> p i m k", i=2, m=4), s,
                                        m.unsqueeze(3).to_broadcast([128, 2, 4, CTX]), ALU.add)\
                            .then_inc(S["shift_ready"], 1)
                    if i >= 4:
                        normalise_group(S, b, i - 4, step)
                step.done()

            batches(dve, before, heads, lambda b: add_rows(S, b))
            dve.wait_ge(*S("y_ready", BATCH))
            layernorm_all(S, Steps(dve, steps["cross0_norm"], 0, None))
            if stages == 2:
                return

            def route(S, moe, step):
                E, K = moe.experts, moe.picks
                TK = TILES * K
                lg, bi, ew = logits[:, :, 0:E], biased[:, :, 0:E], expw[:, :, 0:E]
                oh, pr = onehot[:, 0:TK, 0:E], product[:, 0:TK, 0:E]
                by_tile = lambda x: x.rearrange("p (i k) e -> p i k e", k=K)
                each_pick = lambda x: x.unsqueeze(2).to_broadcast([128, TILES, K, E])
                if moe is MOE0:
                    step(V.tensor_tensor(bi, lg, router_bias[:, 0:E].unsqueeze(1).to_broadcast([128, TILES, E]), ALU.add))
                else:
                    step(V.tensor_copy(bi, lg))
                for i in range(TILES):
                    last = V.max(top8[:, i, :], bi[:, i, :])
                step(last)
                for i in range(TILES):
                    last = V.max_index(top8_i[:, i, :], top8[:, i, :], bi[:, i, :])
                step(last)
                step(V.tensor_copy(top_f[:, 0:TK].rearrange("p (i k) -> p i k", k=K), top8_i[:, :, 0:K]))
                step(V.tensor_tensor(oh, iota_e[:, 0:E].unsqueeze(1).to_broadcast([128, TK, E]),
                                     top_f[:, 0:TK].unsqueeze(2).to_broadcast([128, TK, E]), ALU.is_equal))
                with nc.allow_low_precision("the mask is 0 or 1"):
                    V.tensor_reduce(mask_b[:, :, 0:E], oh.rearrange("p (i k) e -> p i e k", k=K), AX.X, ALU.add)\
                        .then_inc(S["mask_ready"], 1)
                step(V.tensor_reduce(row_t[0], lg, AX.X, ALU.max))
                V.tensor_tensor(ew, lg, row_t[0].unsqueeze(2).to_broadcast([128, TILES, E]), ALU.subtract)\
                    .then_inc(S["exp_in"], 1)
                dve.wait_ge(*S("exp_ready", 1))
                step(V.tensor_tensor(by_tile(pr), by_tile(oh), each_pick(ew), ALU.mult))
                step(V.tensor_reduce(picked[:, :, 0:K], by_tile(pr), AX.X, ALU.add))
                step(V.tensor_reduce(row_t[1], picked[:, :, 0:K], AX.X, ALU.add))
                step(V.reciprocal(row_t[2], row_t[1]))
                step(V.tensor_tensor(pick_w[:, :, 0:K], picked[:, :, 0:K],
                                     row_t[2].unsqueeze(2).to_broadcast([128, TILES, K]), ALU.mult))
                dve.wait_ge(*S("rank_psum", 1))
                cnt, tiles, upto, first, _ = [c[:, 0:E] for c in counts]
                ci, ti = [c[:, 0:E] for c in counts_i]
                step(V.tensor_scalar(ci, bank[1][:, 0:E], float(TILE - 1), None, ALU.add))
                step(V.tensor_scalar(ti, ci, TILE.bit_length() - 1, None, ALU.logical_shift_right))
                step(V.tensor_copy(tiles, ti))
                step(V.tensor_tensor_scan(upto, ones_f[:, 0:E], tiles, 0.0, ALU.mult, ALU.add))
                step(V.tensor_tensor(first, upto, tiles, ALU.subtract))
                step(V.tensor_scalar(first, first, float(TILE), None, ALU.mult))
                sb_ = slot_base[:, :, 0:E]
                step(V.tensor_tensor(sb_, bank[0][:, 0:TILES * E].rearrange("p (i e) -> p i e", i=TILES),
                                     first.unsqueeze(1).to_broadcast([128, TILES, E]), ALU.add))
                step(V.tensor_tensor(by_tile(pr), by_tile(oh), each_pick(sb_), ALU.mult))
                step(V.tensor_reduce(pos_f[:, 0:TK], pr, AX.X, ALU.add))
                step(V.tensor_copy(pos[:, 0:TK], pos_f[:, 0:TK]))
                step(V.tensor_scalar(counts[4][:, 0:E], upto, const[:, C_ROW:C_ROW + 1], None, ALU.is_le))
                step(V.tensor_reduce(e_col[0], counts[4][:, 0:E], AX.X, ALU.add))
                step(V.tensor_scalar(e_col[1], e_col[0], float(E - 1), None, ALU.min))
                V.tensor_scalar(e_diag, ident, e_col[1], None, ALU.mult).then_inc(S["e_ready"], 1)
                dve.wait_ge(*S("e_psum", 1))
                step(V.tensor_copy(tile_expert[:, 0, :], bank[2][:, 0:128]))
                step(V.tensor_scalar(tile_expert[:, 1, :], tile_expert[:, 0, :], 1, None, ALU.logical_shift_right))
                step(V.tensor_scalar(e_par, tile_expert[:, 0, :], 1, None, ALU.bitwise_and))
                step(V.tensor_scalar(tile_half[:], e_par, const[:, C_HALF:C_HALF + 1], None, ALU.is_equal))
                dve.sem_inc(S["routed"], 1)

            def expert_tiles(S, moe):
                H = moe.hidden
                small = moe is MOE0

                def turn(j, u, second=True, third=True, fourth=True, early=0, stored=None):
                    if second:
                        a = (u + 1) % 2
                        dve.wait_ge(*S("act_ready", j))
                        if early == 0 or early > 3:
                            dve.wait_ge(*S("hT_psum", j - 2))
                        if small:
                            V.tensor_tensor(hid[a][:, 0:128].rearrange("p (a n) -> p a n", a=2),
                                            silu_g[a][:, 0:H].unsqueeze(1).to_broadcast([128, 2, H]),
                                            bank[2 + a][:, H:2 * H].unsqueeze(1).to_broadcast([128, 2, H]), ALU.mult)\
                                .then_inc(S["h_ready"], 1)
                        else:
                            V.tensor_tensor(hid[a], silu_g[a], bank[4 + a][:], ALU.mult).then_inc(S["h_ready"], 1)
                    if third:
                        dve.wait_ge(*S("hT_psum", j - 1))
                        if early == 0 or early > 4:
                            dve.wait_ge(*S("y_psum", j - 3))
                        if small:
                            V.tensor_scalar(hidT[u % 2][:, 0:128], bank[moe.hT_banks[u % 2]][:, 0:128], tile_half[:, bass.ds(j - 2, 1)],
                                            None, ALU.mult).then_inc(S["hT_ready"], 1)
                        else:
                            V.tensor_copy(hidT[u % 2], bank[moe.hT_banks[0]][:]).then_inc(S["hT_ready"], 1)
                    if fourth:
                        v = (u + 1) % 4
                        dve.wait_ge(*S("y_psum", j - 2))
                        if early == 0:
                            dve.wait_ge(*S("stored", (j - 3) // 4 * 16 if stored is None else stored, v))
                        V.tensor_copy(y_tile[v], bank[moe.y_banks[(u + 1) % 2]][:, 0:DIM]).then_inc(S["y_copied"], 1)

                for j in range(1, 4):
                    turn(j, j, third=j >= 2, fourth=j >= 3, early=j)
                for j in range(4, 8):
                    turn(j, j % 4, early=j if j < 7 else 0)
                with dve.Fori(2, moe.tiles // 4) as q:
                    for u in range(4):
                        turn(q * 4 + u, u, stored=q * 16 - 16 if u < 3 else q * 16)
                for u in range(3):
                    turn(moe.tiles + u, u, second=u == 0, third=u <= 1)

            def combine(S, moe, step):
                for n in range(TILES * moe.picks):
                    i, k = n // moe.picks, n % moe.picks
                    dve.wait_ge(*S("fetched", 16 * (n // 8 + 1), n % 8))
                    ins = V.scalar_tensor_tensor(y_acc[:, i, :], y_pick[n % 8], pick_w[:, i, k:k + 1], y_acc[:, i, :],
                                                 ALU.mult, ALU.add)
                    ins.then_inc(S["summed"], 1)
                    dve.wait_ge(*S("summed", n + 1))

            def collect_logits(S, moe):
                with dve.Fori(0, BATCH) as b:
                    dve.wait_ge(*S("logit_psum", b + 1))
                    V.tensor_copy(logits[:, bass.ds(b * 2, 2), 0:moe.experts],
                                  bank[K_BANK][:, 0:128].rearrange("p (i e) -> p i e", i=2)[:, :, 0:moe.experts])\
                        .then_inc(S["logit_ready"], 1)
                dve.wait_ge(*S("logit_ready", BATCH))

            S = FFN0
            collect_logits(S, MOE0)
            dve.wait_ge(router_loaded[0], 32)
            step = Steps(dve, steps["ffn0"], 0, None)
            route(S, MOE0, step)
            with dve.Fori(0, BATCH) as b:
                for hc in range(4):
                    dve.wait_ge(*S("silu_ready", b * 4 + hc + 1))
                    if hc == 0:
                        dve.wait_ge(*S("sum_psum", b))
                    V.tensor_tensor(hidden_s[:, hc, :], silu_s[hc % 2], bank[4 + hc % 2][:, 256:512], ALU.mult)\
                        .then_inc(S["hid_ready"], 1)
                dve.wait_ge(*S("sum_psum", b + 1))
                for i in range(2):
                    last = V.tensor_tensor(y_acc[:, bass.ds(b * 2 + i, 1), :], bank[6 + i][:, 0:256].unsqueeze(1),
                                           xb_s[:, i:i + 1, :], ALU.add)
                last.then_inc(S["y_init"], 1)
            expert_tiles(S, MOE0)
            dve.wait_ge(*S("y_init", BATCH))
            combine(S, MOE0, step)
            layernorm_all(S, step)
            if stages == 3:
                return

            def blocks_T(src, dst):
                for st in range(2):
                    last = V.transpose(dst[st].rearrange("p j a i -> p (j a i)"),
                                       src[:, st, :].rearrange("p (j d) -> p j d", d=HEAD_DIM).unsqueeze(2)
                                       .to_broadcast([128, HEADS, 2, HEAD_DIM]))
                return last

            def by_head(src, dst, step):
                step(blocks_T(src, dup))
                for st in range(2):
                    last = V.tensor_scalar(dst(st), dup[st][:, :, 0, :], parity[:, 0:1], None, ALU.mult)
                step(last)
                for st in range(2):
                    last = V.scalar_tensor_tensor(dst(st), dup[st][:, :, 1, :], parity[:, 1:2], dst(st), ALU.mult, ALU.add)
                step(last)

            def full_heads(S, b, step, quantised):
                for h in range(HEADS + 4):
                    if h < HEADS:
                        dve.wait_ge(*S("s_psum", b * HEADS + h + 1))
                        ins = V.tensor_reduce(neg_max[:, h, :], bank[S_BANKS[h % 3]][:].rearrange("p (i k) -> p i k", i=2),
                                              AX.X, ALU.max, negate=True)
                        if quantised:
                            step(ins)
                            ins = V.tensor_tensor(shift[:, h, :], neg_max[:, h, :], q_scale[:, :, h], ALU.mult)
                        ins.then_inc(S["max_ready"], 1)
                    if 2 <= h < HEADS + 2:
                        if quantised:
                            dve.wait_ge(*S("shift_ready", b * HEADS + h - 1))
                        else:
                            dve.wait_ge(*S("pT_psum", b * HEADS + h - 1))
                        if h >= 4:
                            dve.wait_ge(*S("pv_psum", b * HEADS + h - 3))
                        if quantised:
                            with nc.allow_low_precision("whole numbers up to 255 are exact"):
                                V.tensor_scalar(probsT_b[h % 2], p_shifted[h % 2], ROUND, None, ALU.subtract)\
                                    .then_inc(S["pT_ready"], 1)
                        else:
                            V.tensor_copy(probsT[h % 2], bank[PT_BANKS[h % 2]][:]).then_inc(S["pT_ready"], 1)
                    if h >= 7 and h % 4 == 3:
                        normalise_group(S, b, h // 4 - 1, step, summed=quantised)

            S = SELF1
            V.memset(v32, 0.0).then_inc(ctx_sems["zeroed"], 1)
            dve.wait_ge(ctx_sems["zeroed"], 3)
            V.memset(v32[:, :, :, HEAD_DIM], 1.0).then_inc(ctx_sems["zeroed"], 1)
            dve.wait_ge(ctx_sems["zeroed"], 4)
            by_pos = lambda a: (lambda st: a[:, st, :].rearrange("p (j i) -> p j i", i=16))

            def before(b):
                step = Steps(dve, steps["self1_in"], b, 1 + 2 * 3)
                dve.wait_ge(*QKV1("tok_ready", b * 3 + 1))
                dve.wait_ge(*S("km_ready", b * CHUNKS))
                step(blocks_T(k_tok, dup_k))
                dve.sem_inc(QKV1["qkv_ready"], 1)
                dve.sem_inc(S["k_ready"], 1)
                for n, src, dst in ((1, q_tok, qT), (2, v_tok, vT)):
                    dve.wait_ge(*QKV1("tok_ready", b * 3 + n + 1))
                    by_head(src, by_pos(dst), step)
                    dve.sem_inc(QKV1["qkv_ready"], 1)
                step.done()

            def heads(b, more):
                step = Steps(dve, steps["self1_norm"], b, GROUPS)
                full_heads(S, b, step, False)
                step.done()
                dve.wait_ge(*S("o_ready", (b + 1) * GROUPS))
                step = Steps(dve, steps["self1_out"], b, 3)
                by_head(o_tok, by_pos(oT), step)
                dve.sem_inc(S["oT_ready"], 1)
                step.done()

            batches(dve, before, heads, lambda b: add_rows(S, b))
            dve.wait_ge(*S("y_ready", BATCH))
            layernorm_all(S, Steps(dve, steps["self1_norm"], 1, BATCH * GROUPS))
            if stages == 4:
                return

            S = CROSS1
            step = Steps(dve, steps["kv1"], 0, None)
            V.memset(v32_b, 0.0).then_inc(kv1_sems["zeroed"], 1)
            heads_of = lambda x: x.rearrange("p i (h d) -> p i h d", h=HEADS)

            def quantise(x, s, step):
                step(V.tensor_reduce(s, heads_of(x), AX.X, ALU.max, apply_absolute_value=True))
                step(V.tensor_scalar(s, s, 1 / LEVELS, 1e-8, ALU.mult, ALU.max))
                step(V.reciprocal(inv_scale, s))
                step(V.tensor_tensor(heads_of(x), heads_of(x), inv_scale.unsqueeze(3).to_broadcast([128, 2, HEADS, HEAD_DIM]),
                                     ALU.mult))
                step(V.tensor_scalar(x, x, ROUND, ROUND + LEVELS, ALU.add, ALU.min))

            dve.wait_ge(w_loaded[3], LOADS[3])
            dve.wait_ge(kv1_sems["k_psum"], 1)
            step(V.tensor_tensor(k_int, bank[K_BANK][:].rearrange("p (i d) -> p i d", i=2),
                                 bias_row["L1_xattn_bk_row"][:, 0:DIM].unsqueeze(1).to_broadcast([128, 2, DIM]), ALU.add))
            quantise(k_int, k_scale, step)
            step(V.tensor_scalar(k_int, k_int, ROUND - LEVELS, ROUND, ALU.max, ALU.subtract))
            step(V.tensor_tensor(heads_of(k_int), heads_of(k_int), k_scale.unsqueeze(3)
                                 .to_broadcast([128, 2, HEADS, HEAD_DIM]), ALU.mult))
            rows = k_int.rearrange("p i (h d) -> p (i h) d", h=HEADS)
            with nc.allow_low_precision("the parts add up to the whole float32"):
                step(V.tensor_copy(expanded[:, :, 0, :], rows))
                step(V.tensor_tensor(rows, rows, expanded[:, :, 0, :], ALU.subtract))
                step(V.tensor_copy(expanded[:, :, 1, :], rows))
                step(V.tensor_tensor(rows, rows, expanded[:, :, 1, :], ALU.subtract))
                step(V.tensor_copy(expanded[:, :, 2, :], rows))
                step(V.memset(expanded[:, :, 3, :], 0.0))
            dve.sem_inc(kv1_sems["k_ready"], 1)
            dve.wait_ge(kv1_sems["v_psum"], 1)
            for c in range(CHUNKS):
                last = V.tensor_scalar(vq[:, c, :], bank[V_BANK][:, c * 256:(c + 1) * 256],
                                       bias_col["L1_xattn_bkv"][:, 2 + c:3 + c], None, ALU.add)
            step(last)
            step(V.tensor_reduce(v_scale, vq, AX.X, ALU.max, apply_absolute_value=True))
            step(V.tensor_scalar(v_scale, v_scale, 1 / LEVELS, 1e-8, ALU.mult, ALU.max))
            step(V.reciprocal(v_inv, v_scale))
            for c in range(CHUNKS):
                last = V.tensor_scalar(vq[:, c, :], vq[:, c, :], v_inv[:, c:c + 1], ROUND, ALU.mult, ALU.add)
            step(last)
            step(V.tensor_scalar(vq, vq, ROUND + LEVELS, ROUND - LEVELS, ALU.min, ALU.max))
            step(V.tensor_scalar(vq, vq, ROUND, None, ALU.subtract))
            dve.sem_inc(kv1_sems["vq_ready"], 1)
            step(V.tensor_scalar(v_scale, v_scale, 1 / PROB_LEVELS, None, ALU.mult))
            step(V.tensor_scalar(bias_row["L1_xattn_bq"], bias_row["L1_xattn_bq"], SCALE, None, ALU.mult))

            def before(b):
                step = Steps(dve, steps["cross1_in"], b, 7)
                dve.wait_ge(*PARTS1("psum", b * 4 + 4))
                dve.wait_ge(*S("q_psum", b + 1))
                step(V.scalar_tensor_tensor(q_int, bank[Q_BANK][:].rearrange("p (i d) -> p i d", i=2), SCALE,
                                            bias_row["L1_xattn_bq"].unsqueeze(1).to_broadcast([128, 2, DIM]),
                                            ALU.mult, ALU.add))
                quantise(q_int, q_scale, step)
                with nc.allow_low_precision("whole numbers up to 127 are exact"):
                    step(V.tensor_scalar(expanded, q_int.rearrange("p i (h d) -> p (i h) d", h=HEADS).unsqueeze(2)
                                         .to_broadcast([128, 2 * HEADS, 4, HEAD_DIM]), ROUND - LEVELS, ROUND,
                                         ALU.max, ALU.subtract))
                dve.sem_inc(S["k_ready"], 1)
                step.done()

            def heads(b, more):
                step = Steps(dve, steps["cross1_heads"], b, HEADS + GROUPS)
                full_heads(S, b, step, True)
                step.done()

            batches(dve, before, heads, lambda b: add_rows(S, b))
            dve.wait_ge(*S("y_ready", BATCH))
            layernorm_all(S, Steps(dve, steps["cross1_norm"], 0, None))
            if stages == 5:
                return

            S = FFN1
            collect_logits(S, MOE1)
            V.tensor_copy(y_acc[:], x_res[:]).then_inc(S["y_init"], 1)
            step = Steps(dve, steps["ffn1"], 0, None)
            route(S, MOE1, step)
            expert_tiles(S, MOE1)
            dve.wait_ge(*S("y_init", 1))
            combine(S, MOE1, step)
            layernorm_all(S, step)

        @block.gpsimd
        def _(pool):
            P = nc.gpsimd
            for signals in (SELF0, FFN0, QKV1, PARTS1):
                for n, s in signals.sems.items():
                    if n not in signals.by_dma:
                        pool.sem_inc(s, 1)

            def residual_rows(S, b, bias):
                pool.wait_ge(*S("xb_ready", b + 1))
                pool.wait_ge(*S("y_ready", b))
                P.tensor_tensor(xbo[:], xb[:], bias[:].unsqueeze(1).to_broadcast([128, 2, DIM]), ALU.add)\
                    .then_inc(S["xbo_ready"], 1)

            def masked_keys(S, b, src, n):
                for c in range(CHUNKS):
                    P.tensor_tensor(kTm[:, c, :, 0:n], src(c).to_broadcast([128, 4, n]),
                                    head_mask.unsqueeze(2).to_broadcast([128, 4, n]), ALU.mult)\
                        .then_inc(S["km_ready"], 1)

            pool.wait_ge(const_loaded, 32)
            pool.wait_ge(w_loaded[0], LOADS[0])
            S = SELF0
            with pool.Fori(0, BATCH) as b:
                pool.wait_ge(*S("k_ready", b + 1))
                masked_keys(S, b, lambda c: kT[:, c:c + 1, :], SEQ)
                residual_rows(S, b, bias_row["L0_attn_b_proj"])
            if stages == 1:
                return
            pool.wait_ge(w_loaded[1], LOADS[1])
            pool.wait_ge(ctx_sems["k_ready"], 1)
            S = CROSS0
            with pool.Fori(0, BATCH) as b:
                pool.wait_ge(*S("s_psum", b * GROUPS))
                masked_keys(S, b, lambda c: ckT[:, c:c + 1, bass.ds(b * CTX, CTX)], CTX)
                residual_rows(S, b, bias_row["L0_xattn_bo"])
            if stages == 2:
                return

            def send_rows(S, moe):
                pool.wait_ge(*S("routed", 1))
                pool.wait_ge(zero_filled, 16 * (MOE0.tiles + MOE1.tiles) // 8)
                for n in range(TILES * moe.picks):
                    P.indirect_dma_start(out=sorted_x[moe.stage],
                                         out_offset=bass.IndirectOffsetOnAxis(ap=pos[:, n:n + 1], axis=0),
                                         in_=x_res[:, n // moe.picks, :], in_offset=None).then_inc(S["sent"], 16)

            def fetch_outputs(S, moe):
                for v in range(4):
                    pool.wait_ge(*S("stored", 16 * moe.tiles // 4, v))
                for n in range(TILES * moe.picks):
                    if n >= 8:
                        pool.wait_ge(*S("summed", n - 7))
                    P.indirect_dma_start(out=y_pick[n % 8], out_offset=None, in_=sorted_y[moe.stage],
                                         in_offset=bass.IndirectOffsetOnAxis(ap=pos[:, n:n + 1], axis=0))\
                        .then_inc(S["fetched"][n % 8], 16)

            send_rows(FFN0, MOE0)
            fetch_outputs(FFN0, MOE0)
            if stages == 3:
                return
            S = SELF1
            with pool.Fori(0, BATCH) as b:
                pool.wait_ge(*S("k_ready", b + 1))
                for st in range(2):
                    for a in range(2):
                        last = P.tensor_tensor(
                            kTm[:, st, 2 * a:2 * a + 2, :].rearrange("p e (j i) -> p e j i", i=16),
                            dup_k[st].rearrange("p j e i -> p e j i"),
                            head_mask[:, 2 * a:2 * a + 2].unsqueeze(2).unsqueeze(3).to_broadcast([128, 2, 16, 16]), ALU.mult)
                    last.then_inc(S["km_ready"], 1)
                residual_rows(S, b, zeros[:])
            if stages == 4:
                return
            S = CROSS1
            pool.wait_ge(w_loaded[3], LOADS[3])
            with pool.Fori(0, BATCH) as b:
                residual_rows(S, b, bias_row["L1_xattn_bp"])
            if stages == 5:
                return
            send_rows(FFN1, MOE1)
            fetch_outputs(FFN1, MOE1)


_TRANSPOSED = ("L0_xattn_Wq", "L0_xattn_Wk", "L0_xattn_Wv", "L0_xattn_Wo")


def _constants(np):
    c = np.zeros((128, C_COLS), np.float32)
    p = np.arange(128)
    c[:, C_IDENT:C_IDENT + 128] = np.eye(128)
    c[:, C_CAUSAL:C_CAUSAL + 128] = np.where(p[None, :] <= p[:, None], 0.0, -1e30)
    c[:, C_TRI:C_TRI + 128] = p[:, None] < p[None, :]
    s = np.arange(256)
    s = s % 16 * 16 + s // 16
    c[:, C_CAUSAL1:C_COLS] = np.where(s[None, :] <= s[:, None], 1.0, -10000.0).reshape(2, 128, 256)\
        .transpose(1, 0, 2).reshape(128, 512)
    c[:, C_HALF] = p // 64
    c[:, C_ROW] = p
    c[:, C_IOTA:C_IOTA + 64] = np.arange(64)
    c[:, C_HEADMASK:C_HEADMASK + 4] = (p[:, None] % 64 // 16 == np.arange(4)[None, :])
    c[:, C_PARITY:C_PARITY + 2] = (p[:, None] // 16 % 2 == np.arange(2)[None, :])
    return c


def _program(nc, inputs, stages=99):
    import numpy as np

    arrays, tensors = {}, {}
    host = {n: np.asarray(a) for n, a in inputs.items() if "decoder_" not in n}
    host["x"] = host["x"].reshape(-1, DIM)
    host["ctx_2048"] = host["ctx_2048"].reshape(-1, DIM)
    for n in _TRANSPOSED:
        host[n] = host[n].T
    swg, swu, wg, wu = [host.pop(f"L0_ffn_{n}") for n in ("swg", "swu", "wg", "wu")]
    host["L0_ffn_swg"] = swg.transpose(1, 0, 2).reshape(DIM, SHARED_HIDDEN)
    host["L0_ffn_swu"] = swu.transpose(1, 0, 2).reshape(DIM, SHARED_HIDDEN)
    host["L0_ffn_swd"] = host["L0_ffn_swd"].reshape(SHARED_HIDDEN, DIM)
    gu = np.concatenate([wg, wu], axis=2)
    host["expert_in0"] = gu.reshape(64, CHUNKS, 128, 128).transpose(2, 0, 1, 3).reshape(128, -1)
    host["expert_out0"] = host.pop("L0_ffn_wd").reshape(32, 128, DIM).transpose(1, 0, 2).reshape(128, -1)
    gu = np.concatenate([host.pop("L1_ffn_w0"), host.pop("L1_ffn_w1")], axis=2)
    host["expert_in1"] = gu.reshape(8, CHUNKS, 128, 1024).transpose(2, 0, 1, 3).reshape(128, -1)
    host["expert_out1"] = host.pop("L1_ffn_wo").reshape(8, 4, 128, DIM).transpose(2, 0, 1, 3).reshape(128, -1)
    host["L1_xattn_bk_row"] = host["L1_xattn_bkv"]
    for n in BIAS_COL:
        host[n] = host[n].reshape(-1, 128).T
    host["const"] = _constants(np)
    for n, a in host.items():
        a = np.ascontiguousarray(a)
        arrays[f"in_{n}"] = a
        tensors[n] = nc.dram_tensor(f"in_{n}", a.shape, mybir.dt.from_np(a.dtype), kind="ExternalInput").ap()
    out = nc.dram_tensor("out", (BATCH * SEQ, DIM), mybir.dt.float32, kind="ExternalOutput").ap()
    decoder_kernel(nc, tensors, out, stages)
    return arrays


def kernel(**inputs):
    import concourse.bacc as bacc
    from concourse.bass_utils import run_bass_kernel_spmd

    nc = bacc.Bacc("TRN2", target_bir_lowering=False, num_devices=1)
    arrays = _program(nc, inputs)
    r = run_bass_kernel_spmd(nc, [arrays], core_ids=[0])
    return r.results[0]["out"].reshape(BATCH, SEQ, DIM)
```

```python
import concourse.bass as bass
from concourse import mybir
from contextlib import ExitStack

BATCH, SEQ, DIM = 4, 256, 256
CTX = 64
HEADS, HEAD_DIM = 16, 16
TILE = 128
TILES = BATCH * SEQ // TILE
CHUNKS = DIM // TILE
GROUPS = HEADS // 4
SCALE = HEAD_DIM ** -0.5
EPS = 1e-5
RSQRT_SEED = 1597463007.0

C_IDENT, C_CAUSAL, C_TRI, C_HEADMASK, C_PARITY, C_HALF, C_ROW, C_IOTA = 0, 128, 256, 384, 388, 390, 391, 392
C_CAUSAL1 = C_IOTA + 64
C_COLS = C_CAUSAL1 + 2 * SEQ
ROUND = 1.5 * 2 ** 23
LEVELS, PROB_LEVELS = 127.0, 255.0


class Moe:
    def __init__(self, experts, picks, hidden, stage):
        self.experts, self.picks, self.hidden, self.stage = experts, picks, hidden, stage
        self.tiles = BATCH * SEQ * picks // TILE + experts
        assert self.tiles % 4 == 0
        self.hT_banks, self.y_banks = ((6, 4), (7, 5)) if hidden < 128 else ((6, 6), (7, 7))


MOE0, MOE1 = Moe(64, 4, 64, 0), Moe(8, 2, 512, 1)
SHARED_HIDDEN = 512

W_ATTN = {"L0_attn_w_attn": 0, "L0_attn_w_proj": 0, "L0_xattn_Wq": 1, "L0_xattn_Wk": 1, "L0_xattn_Wv": 1,
          "L0_xattn_Wo": 1, "L1_attn_w_qkv": 2, "L1_attn_w_out": 2,
          "L1_xattn_Wq": 3, "L1_xattn_Wkv": 3, "L1_xattn_Wp": 3}
BIAS_COL = {"L0_attn_b_attn": 0, "L0_xattn_bq": 1, "L0_xattn_bk": 1, "L0_xattn_bv": 1, "L1_xattn_bkv": 3}
BIAS_ROW = {"L0_attn_b_proj": 0, "L0_xattn_bo": 1, "L1_xattn_bq": 3, "L1_xattn_bk_row": 3, "L1_xattn_bp": 3}


def decoder_kernel(nc: bass.Bass, t: dict, out: bass.AP):
    f32, bf16, f16 = mybir.dt.float32, mybir.dt.bfloat16, mybir.dt.float16
    i32, u32 = mybir.dt.int32, mybir.dt.uint32
    ALU, ACT, AX = mybir.AluOpType, mybir.ActivationFunctionType, mybir.AxisListType

    with ExitStack() as ctx:
        def sb(name, shape, dt=f32):
            return ctx.enter_context(nc.sbuf_tensor(name, shape, dt))

        def sem(name):
            return ctx.enter_context(nc.semaphore(name))

        bank = [ctx.enter_context(nc.psum_tensor(f"bank{i}", [128, 512], f32)) for i in range(8)]
        SX_BANK, V_BANKS = 3, (1, 2)
        X_BANK, Q_BANK, K_BANK, V_BANK = 0, 1, 2, 3
        S_BANKS, PT_BANKS, PV_BANKS, BACK_BANK, PROJ_BANK = (4, 5, 0), (6, 7), (2, 1), 3, 6

        class Carver:
            def __init__(self, region):
                self.region, self.at = region, 0

            def __call__(self, *shape, dt=None):
                n = 1
                for k in shape:
                    n *= k
                v = self.region[:, self.at:self.at + n]
                self.at += n
                assert self.at <= self.region.shape[1], self.at
                if dt is not None:
                    v = v.bitcast(dt)
                if len(shape) > 1:
                    names = "abcd"[:len(shape)]
                    v = v.rearrange(f"p ({' '.join(names)}) -> p {' '.join(names)}",
                                    **{k: x for k, x in zip(names[1:], shape[1:])})
                return v

        x_res = sb("x_res", [128, TILES, DIM])
        const = sb("const", [128, C_CAUSAL1])
        ident = const[:, C_IDENT:C_IDENT + 128]
        head_mask = const[:, C_HEADMASK:C_HEADMASK + 4]
        parity = const[:, C_PARITY:C_PARITY + 2]
        ident_h = sb("ident_h", [128, 128], f16)
        ident_b = sb("ident_b", [128, 128], bf16)
        causal_b = sb("causal_b", [128, 128], bf16)
        causal_h = sb("causal_h", [128, 2, SEQ], f16)
        tri_b = sb("tri_b", [128, 128], bf16)
        ones_b = sb("ones_b", [128, 128], bf16)
        ones_f = sb("ones_f", [128, 128])
        iota_e = const[:, C_IOTA:C_IOTA + 64]
        zeros = sb("zeros", [128, DIM])
        y_acc = sb("y_acc", [128, TILES, DIM])
        expert_in = sb("expert_in", [128, 16384])
        expert_out = sb("expert_out", [128, 8192])
        neg_max = sb("neg_max", [128, HEADS, 2])
        row_sum = sb("row_sum", [128, HEADS, 2])
        row_inv = sb("row_inv", [128, 2, 2, 4])
        spacer = sb("spacer", [128, 1])
        stats = sb("stats", [128, TILES, 6])
        mean_var = sb("mean_var", [128, TILES, 2])
        rs_bits = sb("rs_bits", [128, TILES], i32)
        rs_y, rs_t, rs_v = sb("rs_y", [128, TILES]), sb("rs_t", [128, TILES]), sb("rs_v", [128, TILES])
        qbias = [sb(f"qbias{i}", [128, 2]) for i in range(2)]
        tile_expert = sb("tile_expert", [128, 2, 128], i32)
        turn_experts = sb("turn_experts", [128, MOE0.tiles // 4, 8], i32)
        tile_half = sb("tile_half", [128, 128])
        pos = sb("pos", [128, 32], u32)
        pick_w = sb("pick_w", [128, TILES, 4])

        w_region = sb("w_region", [128, 7700])
        w_in, bias_col, bias_row = {}, {}, {}
        for layer in range(2):
            cut = Carver(w_region)
            for n in W_ATTN:
                if n.startswith(f"L{layer}"):
                    w_in[n] = cut(CHUNKS, t[n].shape[-1])
            for n in BIAS_COL:
                if n.startswith(f"L{layer}"):
                    bias_col[n] = cut(t[n].shape[1])
            for n in BIAS_ROW:
                if n.startswith(f"L{layer}"):
                    bias_row[n] = cut(t[n].shape[0])
            if layer == 0:
                shared_in = [cut(CHUNKS, SHARED_HIDDEN) for _ in range(2)]
                shared_out = cut(SHARED_HIDDEN // 128, DIM)

        work = sb("work", [128, 14340])
        cut = Carver(work)
        xb = cut(2, DIM)
        xbo = cut(2, DIM)
        xT = cut(CHUNKS, SEQ)
        qT = cut(CHUNKS, SEQ)
        kT = cut(CHUNKS, SEQ)
        kTm = cut(CHUNKS, 4, SEQ)
        v32 = cut(2, HEADS, 32)
        probs = [cut(512) for i in range(3)]
        probsT = [cut(512) for i in range(2)]
        oT4 = [cut(SEQ) for i in range(2)]
        o_tok = cut(2, DIM)
        oT = cut(CHUNKS, SEQ)
        logits = cut(TILES, 64)
        dup_at = cut.at
        ctxT = cut(CHUNKS, BATCH * CTX)
        ctx_tok = cut(2, DIM)
        ctxT2 = cut(CHUNKS, BATCH, 2, CTX)
        ckT = cut(CHUNKS, BATCH * CTX)
        cv = cut(BATCH, DIM)
        cut.at = dup_at + CHUNKS * BATCH * CTX
        q_tok, k_tok, v_tok = [cut(2, DIM) for _ in range(3)]
        dup = [cut(2, HEADS, HEAD_DIM) for _ in range(2)]
        dup_v = [probs[n].rearrange("p (a j i) -> p a j i", a=2, i=16) for n in (1, 2)]
        dup_k = [cut(2, HEADS, HEAD_DIM) for _ in range(2)]
        cut.at = work.shape[1] - 512
        causal_f = cut(512)
        cut.at = dup_at + CHUNKS * BATCH * CTX
        q_int, k_int = [cut(2, DIM) for _ in range(2)]
        expanded = cut(1024, dt=bf16).rearrange("p (i h c d) -> p (i h) c d", i=2, h=HEADS, c=4)
        k_parts, q_parts = [kTm.rearrange("p c m n -> p (c m n)")[:, n * 1024:(n + 1) * 1024].bitcast(bf16)
                            .rearrange("p (h n) -> p h n", h=HEADS // 2) for n in range(2)]
        q_scale, k_scale = [cut(2, HEADS) for _ in range(2)]
        inv_scale = cut(2, HEADS)
        v_scale, v_inv = cut(CHUNKS), cut(CHUNKS)
        shift = cut(HEADS, 2)
        vq = qT
        p_shifted = [cut(512), cut(512)]
        EXP_BANKS = (1, 2, 3, 7)
        KEY_BANKS, VT_BANK = (4, 5, 2, 3), 7
        probsT_b = [p[:, 0:256].bitcast(bf16) for p in probsT]
        v32_b = v32.rearrange("p i h d -> p (i h d)")[:, 0:512].bitcast(bf16)\
            .rearrange("p (i h d) -> p i h d", i=2, h=HEADS)
        cut.at = dup_at + CHUNKS * BATCH * CTX
        xb_s, xT_s = cut(2, DIM), cut(CHUNKS, SEQ)
        silu_s = [cut(SEQ) for _ in range(2)]
        hidden_s = cut(SHARED_HIDDEN // 128, SEQ)
        cut = Carver(work)
        biased = cut(TILES, 64)
        expw = cut(TILES, 64)
        onehot = cut(32, 64)
        product = cut(32, 64)
        slot_base = cut(TILES, 64)
        top8 = cut(TILES, 8)
        top8_i = cut(TILES, 8, dt=u32)
        top_f = cut(32)
        row_t = [cut(TILES) for _ in range(3)]
        pos_f = cut(TILES * 4)
        picked = cut(TILES, 4)
        counts = [cut(64) for _ in range(5)]
        counts_i = [cut(64, dt=i32) for _ in range(2)]
        e_col = [cut(1) for _ in range(2)]
        e_diag = cut(128)
        e_par = cut(128, dt=i32)
        mask_b = cut(TILES * 32, dt=bf16).rearrange("p (i e) -> p i e", i=TILES)
        cut = Carver(work)
        xg = [cut(DIM) for _ in range(4)]
        xgT = [cut(CHUNKS, TILE) for _ in range(2)]
        silu_g = [cut(512) for _ in range(2)]
        hid = [cut(512) for _ in range(2)]
        hidT = [cut(512) for _ in range(2)]
        y_tile = [cut(DIM) for _ in range(4)]
        y_pick = [cut(DIM) for _ in range(8)]

        sorted_x = [nc.dram_tensor(f"sorted_x{m.stage}", (m.tiles * TILE, DIM), f32).ap() for m in (MOE0, MOE1)]
        sorted_y = [nc.dram_tensor(f"sorted_y{m.stage}", (m.tiles * TILE, DIM), f32).ap() for m in (MOE0, MOE1)]

        const_loaded, const_ready, x_loaded, ctx_loaded, stored = map(
            sem, ("const_loaded", "const_ready", "x_loaded", "ctx_loaded", "stored"))
        CONSTS = 5
        w_loaded = [sem(f"w_loaded{i}") for i in range(4)]
        LOADS = [16 * sum(v == i for d in (W_ATTN, BIAS_COL, BIAS_ROW) for v in d.values()) for i in range(4)]

        class Signals:
            by_dma = ("sent", "loaded", "stored", "fetched")

            def __init__(self, sems, before=None):
                self.sems = sems
                self.before = before or {n: 0 if n in self.by_dma else 1 for n in sems}

            def __getitem__(self, name):
                return self.sems[name]

            def __call__(self, name, n, buf=None):
                done = self.before[name]
                s = self.sems[name] if buf is None else self.sems[name][buf]
                return s, n + done if done else n

            def after(self, counts):
                return Signals(self.sems, {n: self.before[n] + counts.get(n, 0) for n in self.sems})

        once = ("xb_ready", "xbo_ready", "xT_psum", "xT_ready", "q_psum", "k_psum", "v_psum", "q_ready", "k_ready",
                "v_ready", "oT_psum", "oT_ready", "proj_psum", "y_ready")
        per_group = ("ot_ready", "back_psum", "o_ready")
        per_head = ("s_psum", "max_ready", "shift_ready", "p_ready", "pT_psum", "pT_ready", "pv_psum")

        def attention_counts(n, never):
            c = {**{k: BATCH for k in once}, **{k: BATCH * GROUPS for k in per_group}, **{k: BATCH * n for k in per_head},
                 "km_ready": BATCH * CHUNKS, "x_ready": 2}
            return {k: v for k, v in c.items() if k not in never}

        SELF0 = Signals({n: sem(f"att_{n}") for n in once + per_group + per_head + ("km_ready", "x_ready")})
        CROSS0 = SELF0.after(attention_counts(HEADS, ("shift_ready",)))
        SELF1 = CROSS0.after(attention_counts(GROUPS, ("k_psum", "v_psum", "k_ready", "max_ready")))
        CROSS1 = SELF1.after(attention_counts(HEADS, ("shift_ready", "q_ready", "oT_psum")))

        per_batch = ("xb_ready", "xT_psum", "xT_ready", "logit_psum", "logit_ready")
        shared_batch = ("xb_s_ready", "xT_s_psum", "xT_s_ready", "y_init", "sum_psum")
        shared = ("g_psum", "silu_ready", "hid_ready")
        single = ("mask_ready", "exp_in", "exp_ready", "rank_psum", "e_ready", "e_psum", "routed", "x_ready", "placed")
        per_tile = ("t_psum", "t_ready", "gu_psum", "act_ready", "h_ready", "hT_psum", "hT_ready", "y_psum", "y_copied")
        rows0 = TILES * MOE0.picks
        moe_sems = {n: sem(f"ffn_{n}") for n in per_batch + shared_batch + shared + single + per_tile + ("sent", "summed")}
        moe_sems["loaded"] = [sem(f"ffn_loaded{i}") for i in range(4)]
        moe_sems["stored"] = [sem(f"ffn_stored{i}") for i in range(4)]
        moe_sems["fetched"] = [sem(f"ffn_fetched{i}") for i in range(8)]
        FFN0 = Signals(moe_sems)
        FFN1 = FFN0.after({**{n: BATCH for n in per_batch + shared_batch}, **{n: BATCH * SHARED_HIDDEN // 128 for n in shared},
                           **{n: 1 for n in single}, "x_ready": 2, **{n: MOE0.tiles for n in per_tile},
                           "sent": 16 * rows0, "summed": rows0, "loaded": 16 * MOE0.tiles // 4,
                           "stored": 16 * MOE0.tiles // 4, "fetched": 16 * rows0 // 8})
        steps = {n: sem(f"{n}_step") for n in (
            "self0_norm", "cross0_heads", "ffn0", "self1_out", "self1_in", "self1_norm", "kv1",
            "cross1_heads", "cross1_in", "ffn1", "ln", "early_ln")}
        zero_filled, shared_loaded = sem("zero_filled"), sem("shared_loaded")
        expert_loaded = [sem("expert_loaded0"), sem("expert_loaded1")]
        router_loaded = [sem("router_loaded0"), sem("router_loaded1")]
        router_w = [sb(f"router_w{m.stage}", [128, CHUNKS, m.experts]) for m in (MOE0, MOE1)]
        router_bias = sb("router_bias", [128, 64])
        QKV1 = Signals({n: sem(f"self1_{n}") for n in ("tok_ready", "qkv_ready", "vT_psum")})
        PARTS1 = Signals({n: sem(f"parts1_{n}") for n in ("psum", "ready")})
        kv1_sems = {n: sem(f"kv1_{n}") for n in ("k_psum", "v_psum", "k_ready", "vq_ready", "vT_psum",
                                                 "v_ready", "zeroed")}
        ctx_sems = {n: sem(f"ctx_{n}") for n in ("T_psum", "T_ready", "k_psum", "v_psum", "k_ready", "v_ready", "zeroed", "step")}
        zeroed, qbias1_ready = sem("zeroed"), sem("qbias1_ready")

        block = ctx.enter_context(nc.Block())

        def batches(eng, before, heads, after, first=lambda: None, last=lambda: None, start=None):
            (start or before)(0)
            first()
            with eng.Fori(0, BATCH - 1) as b:
                heads(b, True)
                before(b + 1)
                after(b)
            heads(BATCH - 1, False)
            last()
            after(BATCH - 1)

        def shifted_by_act(h):
            return h + 1 - sum(by_dve(k) for k in range(h + 1))

        def by_dve(h):
            return h % 4 == 0

        class Steps:
            def __init__(self, eng, s, turn, steps):
                self.eng, self.s, self.steps, self.n = eng, s, steps, 0
                self.base = turn * steps if steps else 0

            def __call__(self, ins):
                self.n += 1
                ins.then_inc(self.s, 1)
                self.eng.wait_ge(self.s, self.base + self.n)

            def done(self):
                assert self.n == self.steps, self.n

        def head_rows(h):
            r = (h % 8) // 4 * 64
            return slice(r, r + 64), h // 8, h % 4

        @block.sync
        def _(sp):
            def tile_traffic(sp, moe, S):
                def load(j, u):
                    sp.dma_start(xg[u], sorted_x[moe.stage][bass.ds(j * TILE, TILE), :]).then_inc(S["loaded"][u], 16)

                def turn(j, u, load_next=True, store_last=True):
                    if load_next:
                        sp.wait_ge(*S("t_psum", j + 1))
                        load(j + 4, u)
                    if store_last:
                        v = (u + 1) % 4
                        sp.wait_ge(*S("y_copied", j - 2))
                        sp.dma_start(sorted_y[moe.stage][bass.ds((j - 3) * TILE, TILE), :], y_tile[v])\
                          .then_inc(S["stored"][v], 16)

                sp.wait_ge(*S("sent", 16 * TILES * moe.picks))
                for u in range(4):
                    load(u, u)
                for u in range(4):
                    turn(u, u, store_last=u == 3)
                with sp.Fori(1, moe.tiles // 4 - 1) as q:
                    for u in range(4):
                        turn(q * 4 + u, u)
                for j in range(moe.tiles - 4, moe.tiles + 3):
                    turn(j, j % 4, load_next=False)

            sp.dma_start(const[:], t["const"][:, 0:C_CAUSAL1]).then_inc(const_loaded, 16)
            sp.dma_start(causal_f, t["const"][:, C_CAUSAL1:C_COLS]).then_inc(const_loaded, 16)
            sp.dma_start(x_res[:], t["x"].rearrange("(i p) d -> p i d", p=128)).then_inc(x_loaded, 16)

            def attention_weights(lot):
                for n in W_ATTN:
                    if W_ATTN[n] == lot:
                        sp.dma_start(w_in[n], t[n].rearrange("(c p) n -> p c n", p=128)).then_inc(w_loaded[lot], 16)
                for n in BIAS_COL:
                    if BIAS_COL[n] == lot:
                        sp.dma_start(bias_col[n], t[n]).then_inc(w_loaded[lot], 16)
                for n in BIAS_ROW:
                    if BIAS_ROW[n] == lot:
                        sp.dma_start(bias_row[n], t[n].partition_broadcast(128)).then_inc(w_loaded[lot], 16)

            attention_weights(0)
            sp.dma_start(ctx_tok[:], t["ctx_2048"].rearrange("(i p) d -> p i d", p=128)).then_inc(ctx_loaded, 16)
            attention_weights(1)
            sp.dma_start(router_w[0][:], t["L0_ffn_router_w"].rearrange("(c p) n -> p c n", p=128)).then_inc(router_loaded[0], 16)
            sp.dma_start(router_bias[:], t["L0_ffn_router_bias"].partition_broadcast(128)).then_inc(router_loaded[0], 16)
            sp.dma_start(router_w[1][:], t["L1_ffn_gate_w"].rearrange("(c p) n -> p c n", p=128)).then_inc(router_loaded[1], 16)
            for w, n in ((shared_in[0], "L0_ffn_swg"), (shared_in[1], "L0_ffn_swu"), (shared_out, "L0_ffn_swd")):
                sp.dma_start(w, t[n].rearrange("(c p) n -> p c n", p=128)).then_inc(shared_loaded, 16)
            sp.wait_ge(zeroed, 2)
            for m in (MOE0, MOE1):
                z = sorted_x[m.stage].rearrange("(p r) d -> p r d", p=128)
                for r in range(0, m.tiles, 8):
                    sp.dma_start(z[:, r:r + 8, :], zeros[:].unsqueeze(1).to_broadcast([128, 8, DIM])).then_inc(zero_filled, 16)

            def experts(layer):
                for dst, src in ((expert_in, t[f"expert_in{layer}"]), (expert_out, t[f"expert_out{layer}"])):
                    for q in range(0, dst.shape[1], 4096):
                        sp.dma_start(dst[:, q:q + 4096], src[:, q:q + 4096]).then_inc(expert_loaded[layer], 16)

            experts(0)
            sp.wait_ge(*FFN0("sum_psum", BATCH))
            attention_weights(2)
            attention_weights(3)
            tile_traffic(sp, MOE0, FFN0)
            sp.wait_ge(*FFN0("y_psum", MOE0.tiles))
            sp.wait_ge(*FFN0("summed", rows0))
            experts(1)
            tile_traffic(sp, MOE1, FFN1)
            rows_out, early = out.rearrange("(i p) d -> p i d", p=128), TILES - 2
            sp.wait_ge(*FFN1("x_ready", 1))
            sp.dma_start(rows_out[:, 0:early], x_res[:, 0:early]).then_inc(stored, 16)
            sp.wait_ge(*FFN1("x_ready", 2))
            sp.dma_start(rows_out[:, early:TILES], x_res[:, early:TILES]).then_inc(stored, 16)
            sp.wait_ge(stored, 32)

        @block.tensor
        def _(pe):
            mm, tr = nc.tensor.matmul, nc.tensor.transpose

            def transposes(dst, src):
                for kc in range(CHUNKS):
                    for i in range(2):
                        last = tr(dst[:, kc * 256 + i * 128:kc * 256 + (i + 1) * 128],
                                  src[:, i, kc * 128:(kc + 1) * 128], ident)
                return last

            def features_out(dst, w, c0, src):
                for c in range(CHUNKS):
                    for kc in range(CHUNKS):
                        last = mm(dst[:, c * 256:(c + 1) * 256], w[:, kc, c0 + c * 128:c0 + (c + 1) * 128],
                                  src[:, kc, :], start=kc == 0, stop=kc == CHUNKS - 1)
                return last

            def tokens_out(dst, src, w, c0):
                for i in range(2):
                    for kc in range(CHUNKS):
                        last = mm(dst[:, i * 256:(i + 1) * 256], src[:, kc, i * 128:(i + 1) * 128],
                                  w[:, kc, c0:c0 + DIM], start=kc == 0, stop=kc == CHUNKS - 1)
                return last

            def transpose_in(S, b):
                pe.wait_ge(*S("xb_ready", b + 1))
                transposes(bank[X_BANK], xb).then_inc(S["xT_psum"], 1)
                pe.wait_ge(*S("xT_ready", b + 1))

            def back_to_tokens(S, b, g):
                pe.wait_ge(*S("ot_ready", b * GROUPS + g + 1))
                pe.wait_ge(*S("o_ready", b * GROUPS + g))
                for i in range(2):
                    last = tr(bank[BACK_BANK][:, i * 128:(i + 1) * 128], oT4[g % 2][:, i * 128:(i + 1) * 128], ident)
                last.then_inc(S["back_psum"], 1)

            def project_out(S, b, wo):
                pe.wait_ge(*S("o_ready", (b + 1) * GROUPS))
                transposes(bank[X_BANK], o_tok).then_inc(S["oT_psum"], 1)
                pe.wait_ge(*S("oT_ready", b + 1))
                tokens_out(bank[PROJ_BANK], oT, wo, 0).then_inc(S["proj_psum"], 1)

            pe.wait_ge(const_ready, CONSTS)
            pe.wait_ge(w_loaded[0], LOADS[0])
            S = SELF0

            def before(b):
                transpose_in(S, b)
                W = w_in["L0_attn_w_attn"]
                features_out(bank[K_BANK], W, DIM, xT).then_inc(S["k_psum"], 1)
                features_out(bank[Q_BANK], W, 0, xT).then_inc(S["q_psum"], 1)
                pe.wait_ge(*S("o_ready", b * GROUPS))
                tokens_out(bank[V_BANK], xT, W, 2 * DIM).then_inc(S["v_psum"], 1)

            def heads(b, more):
                pe.wait_ge(*S("q_ready", b + 1))
                for i in range(HEADS + 5):
                    if i < HEADS:
                        rr, c, m = head_rows(i)
                        if i % 8 == 0:
                            pe.wait_ge(*S("km_ready", b * CHUNKS + i // 8 + 1))
                        if i >= 3:
                            pe.wait_ge(*S("p_ready", b * HEADS + i - 2))
                        s = bank[S_BANKS[i % 3]]
                        mm(s[:, 0:128], qT[rr, c, 0:128], kTm[rr, c, m, 0:128], start=True, stop=False)
                        mm(s[:, 0:128], ident_b[:], causal_b[:], start=False, stop=True)
                        mm(s[:, 128:384], qT[rr, c, 128:256], kTm[rr, c, m, :], start=True, stop=False)
                        mm(s[:, 256:384], ident_b[:], causal_b[:], start=False, stop=True).then_inc(S["s_psum"], 1)
                    if 2 <= i < HEADS + 2:
                        h = i - 2
                        pe.wait_ge(*S("p_ready", b * HEADS + h + 1))
                        if h >= 2:
                            pe.wait_ge(*S("pT_ready", b * HEADS + h - 1))
                        elif h == 0:
                            pe.wait_ge(*S("y_ready", b))
                        for j in range(3):
                            last = tr(bank[PT_BANKS[h % 2]][:, j * 128:(j + 1) * 128],
                                      probs[h % 3][:, j * 128:(j + 1) * 128], ident)
                        last.then_inc(S["pT_psum"], 1)
                    if 3 <= i < HEADS + 3:
                        h = i - 3
                        if h == 0:
                            pe.wait_ge(*S("v_ready", b + 1))
                        if h % 4 == 0:
                            pe.wait_ge(*S("ot_ready", b * GROUPS + max(h // 4 - 1, 0)))
                        pe.wait_ge(*S("pT_ready", b * HEADS + h + 1))
                        o, m = bank[PV_BANKS[h // 4 % 2]], slice(32 * (h % 4), 32 * (h % 4) + 32)
                        mm(o[m, 0:256], v32[:, 0, h, :], probsT[h % 2][:, 0:256], start=True, stop=False)
                        mm(o[m, 128:256], v32[:, 1, h, :], probsT[h % 2][:, 256:384], start=False, stop=True)\
                            .then_inc(S["pv_psum"], 1)
                    if i >= 8 and i % 4 == 0:
                        back_to_tokens(S, b, i // 4 - 2)

            batches(pe, before, heads, lambda b: project_out(S, b, w_in["L0_attn_w_proj"]))

            pe.wait_ge(w_loaded[1], LOADS[1])
            pe.wait_ge(ctx_loaded, 16)
            pe.wait_ge(*SELF0("x_ready", 1))
            transposes(bank[X_BANK], ctx_tok).then_inc(ctx_sems["T_psum"], 1)
            pe.wait_ge(ctx_sems["T_ready"], 2)
            features_out(bank[K_BANK], w_in["L0_xattn_Wk"], 0, ctxT).then_inc(ctx_sems["k_psum"], 1)
            for bb in range(BATCH):
                for kc in range(CHUNKS):
                    last = mm(bank[4 + bb // 2][:, bb % 2 * 256:bb % 2 * 256 + 256],
                              ctxT2[:, kc, bb].rearrange("p a k -> p (a k)"), w_in["L0_xattn_Wv"][:, kc, :],
                              start=kc == 0, stop=kc == 1)
            last.then_inc(ctx_sems["v_psum"], 1)
            pe.wait_ge(ctx_sems["k_ready"], 1)
            pe.wait_ge(ctx_sems["v_ready"], 1)
            S = CROSS0

            def before(b):
                transpose_in(S, b)
                features_out(bank[Q_BANK], w_in["L0_xattn_Wq"], 0, xT).then_inc(S["q_psum"], 1)

            def heads(b, more):
                pe.wait_ge(*S("q_ready", b + 1))
                pe.wait_ge(*S("km_ready", (b + 1) * CHUNKS))
                for i in range(GROUPS + 4):
                    if i < GROUPS:
                        rr, c, _ = head_rows(4 * i)
                        if i == 3:
                            pe.wait_ge(*S("shift_ready", b * GROUPS + 1))
                        for j in range(2):
                            last = mm(bank[S_BANKS[i % 3]][:, j * 256:(j + 1) * 256], qT[rr, c, j * 128:(j + 1) * 128],
                                      kTm[rr, c, :, 0:CTX], start=True, stop=True)
                        last.then_inc(S["s_psum"], 1)
                    if 2 <= i < GROUPS + 2:
                        g = i - 2
                        pe.wait_ge(*S("p_ready", b * GROUPS + g + 1))
                        if g >= 2:
                            pe.wait_ge(*S("pT_ready", b * GROUPS + g - 1))
                        elif g == 0:
                            pe.wait_ge(*S("y_ready", b))
                        for pair in range(2):
                            for j in range(2):
                                last = tr(bank[PT_BANKS[g % 2]][:, pair * 256 + j * 128:pair * 256 + (j + 1) * 128],
                                          probs[g % 3][:, j * 256 + pair * 128:j * 256 + (pair + 1) * 128], ident)
                        last.then_inc(S["pT_psum"], 1)
                    if 3 <= i < GROUPS + 3:
                        g = i - 3
                        if g == 0:
                            pe.wait_ge(*S("v_ready", b + 1))
                        pe.wait_ge(*S("ot_ready", b * GROUPS + max(g - 1, 0)))
                        pe.wait_ge(*S("pT_ready", b * GROUPS + g + 1))
                        for m in range(4):
                            last = mm(bank[PV_BANKS[g % 2]][32 * m:32 * m + 32, 0:256], v32[:, 0, 4 * g + m, :],
                                      probsT[g % 2][:, m // 2 * 256:m // 2 * 256 + 256], start=True, stop=True)
                        last.then_inc(S["pv_psum"], 1)
                    if i >= 4:
                        back_to_tokens(S, b, i - 4)

            batches(pe, before, heads, lambda b: project_out(S, b, w_in["L0_xattn_Wo"]))

            def router(S, moe):
                def before(b):
                    pe.wait_ge(*S("xb_ready", b + 1))
                    transposes(bank[X_BANK], xb).then_inc(S["xT_psum"], 1)

                def logits_of(b, more):
                    pe.wait_ge(*S("xT_ready", b + 1))
                    pe.wait_ge(*S("logit_ready", b))
                    for i in range(2):
                        for kc in range(CHUNKS):
                            last = mm(bank[K_BANK][:, i * 64:i * 64 + moe.experts], xT[:, kc, i * 128:(i + 1) * 128],
                                      router_w[moe.stage][:, kc, :], start=kc == 0, stop=kc == 1)
                    last.then_inc(S["logit_psum"], 1)

                batches(pe, before, logits_of, lambda b: None)

            def count_tokens(S, moe):
                E = moe.experts
                pe.wait_ge(*S("mask_ready", 1))
                m = mask_b[:, :, 0:E]
                r = bank[0][:, 0:TILES * E].rearrange("p (i e) -> p i e", i=TILES)
                mm(r, tri_b[:], m, start=True, stop=False)
                for d in range(1, TILES):
                    mm(r[:, d:TILES], ones_b[:], m[:, 0:TILES - d], start=False, stop=d == TILES - 1)
                for i in range(TILES):
                    last = mm(bank[1][:, 0:E], ones_b[:], m[:, i], start=i == 0, stop=i == TILES - 1)
                last.then_inc(S["rank_psum"], 1)

            def spread_experts(S):
                pe.wait_ge(*S("e_ready", 1))
                mm(bank[2][:, 0:128], ones_f[:], e_diag, start=True, stop=True).then_inc(S["e_psum"], 1)

            def expert_tiles(S, moe):
                H = moe.hidden
                small = moe is MOE0
                w_gu = expert_in[:].rearrange("p (e c n) -> p e c n", e=moe.experts, c=CHUNKS)
                w_d = expert_out[:].rearrange("p (e c n) -> p e c n", n=DIM, c=1 if small else H // 128)
                PEe = [mybir.EngineType.PE]

                def experts(row, j, n):
                    src = tile_expert[0:1, row, bass.ds(j, n)]
                    _, v = nc.values_load_multi_w_load_instructions(
                        src, engines=PEe, min_val=0, max_val=(moe.experts - 1) >> row,
                        skip_runtime_bounds_check_because="routing clamps them to the experts there are")
                    return v

                def turn(j, u, e_gu, e_d, first=True, second=True, third=True, fourth=True):
                    if first:
                        pe.wait_ge(*S("loaded", 16 * (j // 4 + 1) if isinstance(j, int) else j4_loads, u))
                        for kc in range(CHUNKS):
                            last = tr(bank[u % 2][:, kc * 128:(kc + 1) * 128], xg[u][:, kc * 128:(kc + 1) * 128], ident)
                        last.then_inc(S["t_psum"], 1)
                    if second:
                        a = (u + 1) % 2
                        pe.wait_ge(*S("t_ready", j))
                        for n in range(1 if small else 2):
                            for kc in range(CHUNKS):
                                dst = bank[2 + a + 2 * n][:, 0:(2 * H if small else H)]
                                w = w_gu[:, bass.ds(e_gu, 1), kc, :] if small else \
                                    w_gu[:, bass.ds(e_gu, 1), kc, n * H:(n + 1) * H]
                                last = mm(dst, xgT[a][:, kc, :], w, start=kc == 0, stop=kc == 1)
                        last.then_inc(S["gu_psum"], 1)
                    if third:
                        pe.wait_ge(*S("h_ready", j - 1))
                        if fourth:
                            pe.wait_ge(*S("hT_ready", j - 3 if small else j - 2))
                        for n in range(1 if small else 4):
                            last = tr(bank[moe.hT_banks[u % 2]][:, n * 128:(n + 1) * 128], hid[u % 2][:, n * 128:(n + 1) * 128], ident)
                        last.then_inc(S["hT_psum"], 1)
                    if fourth:
                        a = (u + 1) % 2
                        pe.wait_ge(*S("hT_ready", j - 2))
                        if not small or not isinstance(j, int) or j > 3:
                            pe.wait_ge(*S("y_copied", j - 4 if small else j - 3))
                        n_k = 1 if small else 4
                        for n in range(n_k):
                            last = mm(bank[moe.y_banks[a]][:, 0:DIM], hidT[a][:, n * 128:(n + 1) * 128], w_d[:, bass.ds(e_d, 1), n, :],
                                      start=n == 0, stop=n == n_k - 1)
                        last.then_inc(S["y_psum"], 1)

                row_d = 1 if small else 0
                pe.wait_ge(*S("routed", 1))
                pe.wait_ge(expert_loaded[moe.stage], 16 * 6)
                ev, ed = experts(0, 0, 4), experts(row_d, 0, 4)
                for j in range(4):
                    turn(j, j, ev[j - 1] if j else None, ed[j - 3] if j == 3 else None,
                         second=j >= 1, third=j >= 2, fourth=j >= 3)
                with pe.Fori(1, moe.tiles // 4) as q:
                    j = q * 4
                    _, e = nc.values_load_multi_w_load_instructions(
                        turn_experts[0:1].rearrange("p q u -> p (q u)")[:, bass.ds(q * 8, 8)], engines=PEe, min_val=0,
                        max_val=moe.experts - 1, skip_runtime_bounds_check_because="routing clamps them")
                    ev = e[0:4]
                    ed = [nc.s_assert_within(v, 0, (moe.experts - 1) >> row_d, skip_runtime_bounds_check_because=
                                             "they are halves of those experts") for v in e[4:8]]
                    j4_loads = j * 4 + 16
                    for u in range(4):
                        turn(j + u, u, ev[u], ed[u])
                ev, ed = experts(0, moe.tiles - 1, 1), experts(row_d, moe.tiles - 3, 3)
                for u in range(3):
                    turn(moe.tiles + u, u, ev[0], ed[u], first=False, second=u == 0, third=u <= 1)

            S = FFN0
            pe.wait_ge(router_loaded[0], 32)
            pe.wait_ge(shared_loaded, 48)
            pe.wait_ge(*CROSS0("x_ready", 1))
            router(S, MOE0)
            n_h = SHARED_HIDDEN // 128

            def before(b):
                pe.wait_ge(*S("xb_s_ready", b + 1))
                transposes(bank[SX_BANK], xb_s).then_inc(S["xT_s_psum"], 1)

            def hidden(b, more):
                pe.wait_ge(*S("xT_s_ready", b + 1))
                for hc in range(n_h):
                    pe.wait_ge(*S("hid_ready", b * n_h + max(hc - 1, 0)))
                    for n in range(2):
                        for kc in range(CHUNKS):
                            last = mm(bank[4 + hc % 2][:, n * 256:(n + 1) * 256], shared_in[n][:, kc, hc * 128:(hc + 1) * 128],
                                      xT_s[:, kc, :], start=kc == 0, stop=kc == 1)
                    last.then_inc(S["g_psum"], 1)

            def down(b):
                pe.wait_ge(*S("y_init", b))
                for hc in range(n_h):
                    pe.wait_ge(*S("hid_ready", b * n_h + hc + 1))
                    for i in range(2):
                        last = mm(bank[6 + i][:, 0:256], hidden_s[:, hc, i * 128:(i + 1) * 128],
                                  shared_out[:, hc, :], start=hc == 0, stop=hc == n_h - 1)
                last.then_inc(S["sum_psum"], 1)

            before(0)
            for b in range(BATCH):
                hidden(b, b < BATCH - 1)
                if b < BATCH - 1:
                    before(b + 1)
                down(b)
                if b == 0:
                    count_tokens(S, MOE0)
                if b == 1:
                    spread_experts(S)
            pe.wait_ge(*S("y_init", BATCH))
            expert_tiles(S, MOE0)

            def full_heads(S, b, quantised):
                vv, pT = (v32_b, probsT_b) if quantised else (v32, probsT)
                for i in range(HEADS + 5):
                    if i < HEADS:
                        rr, c, m = head_rows(i)
                        if not quantised and i % 8 == 0:
                            pe.wait_ge(*S("km_ready", b * CHUNKS + i // 8 + 1))
                        if quantised and i in (0, 3):
                            pe.wait_ge(*PARTS1("ready", b * 4 + 5 + i))
                        if i >= 3:
                            pe.wait_ge(*S("p_ready", b * HEADS + i - 2))
                        for j in range(2):
                            s = bank[S_BANKS[i % 3]][:, j * SEQ:(j + 1) * SEQ]
                            if quantised:
                                half = slice(i % 2 * 64, i % 2 * 64 + 64)
                                last = mm(s, q_parts[half, i // 2, j * 128:(j + 1) * 128], k_parts[half, i // 2, :],
                                          start=True, stop=True)
                            else:
                                mm(s, dup[c][rr, m % 2, j * 8:(j + 1) * 8, :], kTm[rr, c, m, :], start=True, stop=False)
                                last = mm(s, ident_h[:], causal_h[:, j, :], start=False, stop=True)
                        last.then_inc(S["s_psum"], 1)
                    if i == 1 and not quantised:
                        pe.wait_ge(*QKV1("qkv_ready", b * 3 + 3))
                        for e in range(2):
                            for kt in range(2):
                                for st in range(2):
                                    last = tr(bank[V_BANKS[e]][:, (kt * 2 + st) * 128:(kt * 2 + st + 1) * 128],
                                              dup_v[st][:, e, kt * 8:(kt + 1) * 8, :], ident)
                        last.then_inc(QKV1["vT_psum"], 1)
                    if 2 <= i < HEADS + 2:
                        h = i - 2
                        pe.wait_ge(*S("p_ready", b * HEADS + h + 1))
                        if h >= 2:
                            pe.wait_ge(*S("pT_ready", b * HEADS + h - 1))
                        elif h == 0:
                            pe.wait_ge(*S("y_ready", b))
                        for kt in range(2):
                            for j in range(2):
                                last = tr(bank[PT_BANKS[h % 2]][:, kt * SEQ + j * 128:kt * SEQ + (j + 1) * 128],
                                          probs[h % 3][:, j * SEQ + kt * 128:j * SEQ + (kt + 1) * 128], ident)
                        last.then_inc(S["pT_psum"], 1)
                    if 3 <= i < HEADS + 3:
                        h = i - 3
                        if h == 0 and not quantised:
                            pe.wait_ge(*S("v_ready", b + 1))
                        if h % 4 == 0:
                            pe.wait_ge(*S("ot_ready", b * GROUPS + max(h // 4 - 1, 0)))
                        pe.wait_ge(*S("pT_ready", b * HEADS + h + 1))
                        m = slice(32 * (h % 4), 32 * (h % 4) + 32)
                        for kt in range(2):
                            last = mm(bank[PV_BANKS[h // 4 % 2]][m, 0:SEQ], vv[:, kt, h, :], pT[h % 2][:, kt * SEQ:(kt + 1) * SEQ],
                                      start=kt == 0, stop=kt == 1)
                        last.then_inc(S["pv_psum"], 1)
                    if i >= 8 and i % 4 == 0:
                        back_to_tokens(S, b, i // 4 - 2)

            pe.wait_ge(w_loaded[2], LOADS[2])
            pe.wait_ge(*FFN0("x_ready", 1))
            S = SELF1

            def before(b):
                transpose_in(S, b)
                for n, bk, done in ((1, K_BANK, "k_psum"), (0, Q_BANK, "q_psum"), (2, V_BANK, "v_psum")):
                    if n == 2:
                        pe.wait_ge(*S("o_ready", b * GROUPS))
                    tokens_out(bank[bk], xT, w_in["L1_attn_w_qkv"], n * DIM).then_inc(S[done], 1)

            def heads(b, more):
                pe.wait_ge(*QKV1("qkv_ready", b * 3 + 2))
                full_heads(S, b, False)

            def after(b):
                pe.wait_ge(*S("oT_ready", b + 1))
                tokens_out(bank[PROJ_BANK], oT, w_in["L1_attn_w_out"], 0).then_inc(S["proj_psum"], 1)

            def context_kv():
                pe.wait_ge(w_loaded[3], LOADS[3])
                pe.wait_ge(*S("o_ready", BATCH * GROUPS))
                tokens_out(bank[K_BANK], ctxT, w_in["L1_xattn_Wkv"], 0).then_inc(kv1_sems["k_psum"], 1)
                features_out(bank[V_BANK], w_in["L1_xattn_Wkv"], DIM, ctxT).then_inc(kv1_sems["v_psum"], 1)

            batches(pe, before, heads, after, last=context_kv)

            S = CROSS1

            def before(b):
                transpose_in(S, b)
                tokens_out(bank[Q_BANK], xT, w_in["L1_xattn_Wq"], 0).then_inc(S["q_psum"], 1)

            def heads(b, more):
                pe.wait_ge(*S("k_ready", b + 1))
                pe.wait_ge(*S("o_ready", b * GROUPS))
                parts_T(EXP_BANKS)
                full_heads(S, b, True)

            def parts_T(banks):
                flat = expanded.rearrange("p (i h) c d -> p i (h c d)", i=2)
                for n, bk in enumerate(banks):
                    for pair in range(2):
                        c0 = (2 * n + pair) * 128
                        for i in range(2):
                            last = mm(bank[bk][:, pair * 256 + i * 128:pair * 256 + (i + 1) * 128],
                                      flat[:, i, c0:c0 + 128], ident_b[:], start=True, stop=True)
                    last.then_inc(PARTS1["psum"], 1)

            def keys_and_values():
                pe.wait_ge(kv1_sems["k_ready"], 1)
                pe.wait_ge(kv1_sems["vq_ready"], 1)
                for st in range(2):
                    for c in range(CHUNKS):
                        last = tr(bank[VT_BANK][:, st * 256 + c * 128:st * 256 + (c + 1) * 128],
                                  vq[:, c, st * 128:(st + 1) * 128], ident)
                last.then_inc(kv1_sems["vT_psum"], 1)
                parts_T(KEY_BANKS)
                pe.wait_ge(kv1_sems["v_ready"], 1)
                pe.wait_ge(*PARTS1("ready", 4))

            batches(pe, before, heads, lambda b: project_out(S, b, w_in["L1_xattn_Wp"]), first=keys_and_values)

            S = FFN1
            pe.wait_ge(*CROSS1("x_ready", 1))
            pe.wait_ge(router_loaded[1], 16)
            router(S, MOE1)
            count_tokens(S, MOE1)
            spread_experts(S)
            expert_tiles(S, MOE1)

        @block.scalar
        def _(act):
            A = nc.scalar.activation

            def rows_in(S, b):
                act.wait_ge(*S("xT_psum", b))
                act.wait_ge(*S("xbo_ready", b))
                A(xb, x_res[:, bass.ds(b * 2, 2), :], ACT.Copy).then_inc(S["xb_ready"], 1)

            def rows_T(S, b):
                act.wait_ge(*S("xT_psum", b + 1))
                A(xT[:].rearrange("p c n -> p (c n)"), bank[X_BANK][:], ACT.Copy).then_inc(S["xT_ready"], 1)

            def query_out(S, b, bias):
                act.wait_ge(*S("q_psum", b + 1))
                for c in range(CHUNKS):
                    last = A(qT[:, c, :], bank[Q_BANK][:, c * 256:(c + 1) * 256], ACT.Identity,
                             bias=bias[:, c:c + 1], scale=SCALE)
                last.then_inc(S["q_ready"], 1)

            def group_out(S, b, g, done):
                act.wait_ge(*S("pv_psum", done))
                if g >= 2:
                    act.wait_ge(*S("back_psum", b * GROUPS + g - 1))
                A(oT4[g % 2][:], bank[PV_BANKS[g % 2]][:, 0:256], ACT.Copy).then_inc(S["ot_ready"], 1)

            def outputs_T(S, b, bias):
                act.wait_ge(*S("oT_psum", b + 1))
                for c in range(CHUNKS):
                    last = A(oT[:, c, :], bank[X_BANK][:, c * 256:(c + 1) * 256], ACT.Identity, bias=bias[:, c:c + 1])
                last.then_inc(S["oT_ready"], 1)

            act.wait_ge(x_loaded, 16)
            S = SELF0

            def before(b):
                rows_T(S, b)
                act.wait_ge(w_loaded[0], LOADS[0])
                act.wait_ge(const_ready, CONSTS)
                query_out(S, b, qbias[0])
                act.wait_ge(*S("v_psum", b + 1))
                for i in range(2):
                    last = A(v32[:, i, :, 0:HEAD_DIM],
                             bank[V_BANK][:, i * 256:(i + 1) * 256].rearrange("p (h d) -> p h d", d=HEAD_DIM), ACT.Copy)
                last.then_inc(S["v_ready"], 1)

            def heads(b, more):
                for h in range(HEADS + 3):
                    if h < HEADS:
                        act.wait_ge(*S("max_ready", b * HEADS + h + 1))
                        if h >= 3:
                            act.wait_ge(*S("pT_psum", b * HEADS + h - 2))
                        for i, c0, c1 in ((0, 0, 128), (1, 128, 384)):
                            last = A(probs[h % 3][:, c0:c1], bank[S_BANKS[h % 3]][:, c0:c1], ACT.Exp,
                                     bias=neg_max[:, h, i:i + 1])
                        last.then_inc(S["p_ready"], 1)
                    if more and h == 8:
                        rows_in(S, b + 1)
                    if h >= 6 and h % 4 == 2:
                        group_out(S, b, h // 4 - 1, b * HEADS + h - 2)

            rows_in(S, 0)
            batches(act, before, heads, lambda b: outputs_T(S, b, bias_col["L0_attn_b_attn"][:, 4:6]))

            act.wait_ge(w_loaded[1], LOADS[1])
            act.wait_ge(*SELF0("x_ready", 1))
            act.wait_ge(ctx_sems["T_psum"], 1)
            A(ctxT[:].rearrange("p c n -> p (c n)"), bank[X_BANK][:], ACT.Copy).then_inc(ctx_sems["T_ready"], 1)
            for a in range(2):
                last = A(ctxT2[:, :, :, a, :], bank[X_BANK][:].rearrange("p (c b k) -> p c b k", c=2, b=4), ACT.Copy)
            last.then_inc(ctx_sems["T_ready"], 1)
            act.wait_ge(qbias1_ready, 1)
            act.wait_ge(ctx_sems["k_psum"], 1)
            for c in range(CHUNKS):
                last = A(ckT[:, c, :], bank[K_BANK][:, c * 256:(c + 1) * 256], ACT.Identity,
                         bias=bias_col["L0_xattn_bk"][:, c:c + 1])
            last.then_inc(ctx_sems["k_ready"], 1)
            act.wait_ge(ctx_sems["v_psum"], 1)
            for bb in range(BATCH):
                last = A(cv[:, bb, :], bank[4 + bb // 2][:, bb % 2 * 256:bb % 2 * 256 + 256], ACT.Copy)
            last.then_inc(ctx_sems["v_ready"], 1)
            S = CROSS0

            def before(b):
                rows_T(S, b)
                query_out(S, b, qbias[1])

            def heads(b, more):
                for g in range(GROUPS + 3):
                    if g < GROUPS:
                        act.wait_ge(*S("shift_ready", b * GROUPS + g + 1))
                        A(probs[g % 3][:], probs[g % 3][:], ACT.Exp).then_inc(S["p_ready"], 1)
                    if 2 <= g < GROUPS + 2:
                        act.wait_ge(*S("pT_psum", b * GROUPS + g - 1))
                        if g >= 4:
                            act.wait_ge(*S("pv_psum", b * GROUPS + g - 3))
                        A(probsT[g % 2], bank[PT_BANKS[g % 2]][:], ACT.Copy).then_inc(S["pT_ready"], 1)
                    if more and g == 2:
                        act.wait_ge(*CROSS0("x_ready", 0))
                        rows_in(S, b + 1)
                    if g >= 3:
                        group_out(S, b, g - 3, b * GROUPS + g - 2)

            rows_in(S, 0)
            batches(act, before, heads, lambda b: outputs_T(S, b, bias_col["L0_xattn_bv"]))

            def route_exp(S, moe):
                act.wait_ge(*S("exp_in", 1))
                A(expw[:, :, 0:moe.experts], expw[:, :, 0:moe.experts], ACT.Exp).then_inc(S["exp_ready"], 1)

            def expert_tiles(S, moe):
                H = moe.hidden

                def turn(j, u, first=True, second=True, early=False):
                    if first:
                        act.wait_ge(*S("t_psum", j + 1))
                        if not early:
                            act.wait_ge(*S("gu_psum", j - 1))
                        A(xgT[u % 2].rearrange("p c n -> p (c n)"), bank[u % 2][:, 0:DIM], ACT.Copy)\
                            .then_inc(S["t_ready"], 1)
                    if second:
                        a = (u + 1) % 2
                        act.wait_ge(*S("gu_psum", j))
                        if not early:
                            act.wait_ge(*S("h_ready", j - 2))
                        A(silu_g[a][:, 0:H], bank[2 + a][:, 0:H], ACT.Silu).then_inc(S["act_ready"], 1)

                for j in range(4):
                    turn(j, j, second=j >= 1, early=j < 2)
                with act.Fori(1, moe.tiles // 4) as q:
                    for u in range(4):
                        turn(q * 4 + u, u)
                turn(moe.tiles, 0, first=False)

            def router_rows(S, prior):
                def rows(b):
                    act.wait_ge(*S("xT_psum", b))
                    A(xb, x_res[:, bass.ds(b * 2, 2), :], ACT.Copy).then_inc(S["xb_ready"], 1)

                def before(b):
                    act.wait_ge(*S("xT_psum", b + 1))
                    act.wait_ge(*S("logit_psum", b))
                    A(xT.rearrange("p c n -> p (c n)"), bank[X_BANK][:], ACT.Copy).then_inc(S["xT_ready"], 1)

                act.wait_ge(*prior("xbo_ready", BATCH))
                rows(0)
                def next_rows(b, more):
                    if more:
                        act.wait_ge(*prior("x_ready", 2))
                        rows(b + 1)

                batches(act, before, next_rows, lambda b: None)

            S = FFN0
            act.wait_ge(*CROSS0("x_ready", 1))
            router_rows(S, CROSS0)
            def shared_rows(b):
                act.wait_ge(*S("xT_s_psum", b))
                A(xb_s, x_res[:, bass.ds(b * 2, 2), :], ACT.Copy).then_inc(S["xb_s_ready"], 1)

            def before(b):
                act.wait_ge(*S("xT_s_psum", b + 1))
                act.wait_ge(*S("g_psum", b * 4))
                A(xT_s.rearrange("p c n -> p (c n)"), bank[SX_BANK][:], ACT.Copy).then_inc(S["xT_s_ready"], 1)

            def hidden(b, more):
                if more:
                    shared_rows(b + 1)
                for hc in range(4):
                    act.wait_ge(*S("g_psum", b * 4 + hc + 1))
                    act.wait_ge(*S("hid_ready", b * 4 + max(hc - 1, 0)))
                    A(silu_s[hc % 2], bank[4 + hc % 2][:, 0:256], ACT.Silu).then_inc(S["silu_ready"], 1)

            shared_rows(0)
            before(0)
            for b in range(BATCH):
                hidden(b, b < BATCH - 1)
                if b < BATCH - 1:
                    before(b + 1)
                if b == 0:
                    route_exp(S, MOE0)
            expert_tiles(S, MOE0)

            act.wait_ge(*FFN0("x_ready", 1))
            S = SELF1

            def before(b):
                rows_T(S, b)
                for n, (bk, psum, dst) in enumerate(((K_BANK, "k_psum", k_tok), (Q_BANK, "q_psum", q_tok),
                                                     (V_BANK, "v_psum", v_tok))):
                    act.wait_ge(*S(psum, b + 1))
                    act.wait_ge(*QKV1("qkv_ready", b * 3))
                    A(dst.rearrange("p i d -> p (i d)"), bank[bk][:], ACT.Copy, scale=SCALE if n == 1 else 1.0)\
                        .then_inc(QKV1["tok_ready"], 1)

            def heads(b, more):
                for h in range(HEADS + 3):
                    if h == 1:
                        act.wait_ge(*QKV1("vT_psum", b + 1))
                        for e in range(2):
                            last = A(v32.rearrange("p i (h e) d -> p (i h) e d", e=2)[:, :, e, 0:HEAD_DIM],
                                     bank[V_BANKS[e]][:].rearrange("p (h e d) -> p h e d", e=2, d=HEAD_DIM)[:, :, e, :],
                                     ACT.Copy)
                        last.then_inc(S["v_ready"], 1)
                    if h < HEADS:
                        act.wait_ge(*S("max_ready", b * HEADS + h + 1))
                        if h >= 3:
                            act.wait_ge(*S("pT_psum", b * HEADS + h - 2))
                        for i in range(2):
                            last = A(probs[h % 3][:, i * SEQ:(i + 1) * SEQ], bank[S_BANKS[h % 3]][:, i * SEQ:(i + 1) * SEQ],
                                     ACT.Exp, bias=neg_max[:, h, i:i + 1])
                        last.then_inc(S["p_ready"], 1)
                    if more and h == 8:
                        act.wait_ge(*FFN0("x_ready", 2))
                        rows_in(S, b + 1)
                    if h >= 6 and h % 4 == 2:
                        group_out(S, b, h // 4 - 1, b * HEADS + h - 2)

            rows_in(S, 0)
            batches(act, before, heads, lambda b: None)

            act.wait_ge(*SELF1("x_ready", 1))
            S = CROSS1

            def parts_out(dst, banks, lot):
                for n, bk in enumerate(banks):
                    act.wait_ge(*PARTS1("psum", lot * 4 + n + 1))
                    A(dst[:, 2 * n:2 * n + 2, :].rearrange("p h n -> p (h n)"), bank[bk][:], ACT.Copy)\
                        .then_inc(PARTS1["ready"], 1)

            def keys_and_values():
                act.wait_ge(kv1_sems["vT_psum"], 1)
                act.wait_ge(kv1_sems["zeroed"], 1)
                A(v32_b[:, :, :, 0:HEAD_DIM], bank[VT_BANK][:].rearrange("p (i h d) -> p i h d", i=2, h=HEADS), ACT.Copy)\
                    .then_inc(kv1_sems["v_ready"], 1)
                parts_out(k_parts, KEY_BANKS, 0)

            def heads(b, more):
                parts_out(q_parts, EXP_BANKS, b + 1)
                for h in range(HEADS + 3):
                    if 2 <= h < HEADS + 2 and not by_dve(h - 2):
                        act.wait_ge(*S("pT_psum", b * HEADS + h - 1))
                        if h >= 4:
                            act.wait_ge(*S("pT_ready", b * HEADS + h - 3))
                        A(p_shifted[h % 2], bank[PT_BANKS[h % 2]][:], ACT.Copy, scale=PROB_LEVELS, bias=ROUND)\
                            .then_inc(S["shift_ready"], 1)
                    if h < HEADS:
                        act.wait_ge(*S("max_ready", b * HEADS + h + 1))
                        if h >= 3:
                            act.wait_ge(*S("pT_psum", b * HEADS + h - 2))
                        for i in range(2):
                            last = A(probs[h % 3][:, i * SEQ:(i + 1) * SEQ], bank[S_BANKS[h % 3]][:, i * SEQ:(i + 1) * SEQ],
                                     ACT.Exp, bias=shift[:, h, i:i + 1], scale=q_scale[:, i, h:h + 1],
                                     accum_out=row_sum[:, h, i:i + 1])
                        last.then_inc(S["p_ready"], 1)
                    if more and h == 8:
                        act.wait_ge(*CROSS1("x_ready", 0))
                        rows_in(S, b + 1)
                    if h >= 6 and h % 4 == 2:
                        group_out(S, b, h // 4 - 1, b * HEADS + h - 2)

            def after(b):
                act.wait_ge(*S("oT_psum", b + 1))
                for c in range(CHUNKS):
                    last = A(oT[:, c, :], bank[X_BANK][:, c * 256:(c + 1) * 256], ACT.Copy, scale=v_scale[:, c:c + 1])
                last.then_inc(S["oT_ready"], 1)

            rows_in(S, 0)
            batches(act, lambda b: rows_T(S, b), heads, after, first=keys_and_values)

            S = FFN1
            act.wait_ge(*CROSS1("x_ready", 1))
            router_rows(S, CROSS1)
            route_exp(S, MOE1)
            expert_tiles(S, MOE1)

        @block.vector
        def _(dve):
            V = nc.vector

            def normalise_group(S, b, g, step, summed=False):
                dve.wait_ge(*S("back_psum", b * GROUPS + g + 1))
                o = bank[BACK_BANK][:, 0:256].rearrange("p (i m d) -> p i m d", i=2, m=4)
                inv = row_inv[:, g % 2]
                if summed:
                    step(V.reciprocal(inv, row_sum[:, 4 * g:4 * g + 4, :].rearrange("p m i -> p i m")))
                else:
                    step(V.reciprocal(inv, o[:, :, :, HEAD_DIM]))
                V.tensor_tensor(o_tok[:, :, g * 64:(g + 1) * 64].rearrange("p i (m d) -> p i m d", m=4),
                                o[:, :, :, 0:HEAD_DIM], inv.unsqueeze(3).to_broadcast([128, 2, 4, HEAD_DIM]), ALU.mult)\
                    .then_inc(S["o_ready"], 1)

            def norm_part(part, tiles, step, done=None):
                t0, t1 = tiles[0], tiles[-1] + 1
                v, bits, y, r = rs_v[:, t0:t1], rs_bits[:, t0:t1], rs_y[:, t0:t1], rs_t[:, t0:t1]
                if part == 0:
                    for i in tiles:
                        last = V.bn_stats(stats[:, i, :], y_acc[:, i, :])
                    step(last)
                elif part == 1:
                    V.memset(spacer[:], 0.0)
                    for i in tiles:
                        last = V.bn_aggr(mean_var[:, i, :], stats[:, i, :])
                    step(last)
                elif part == 2:
                    step(V.tensor_scalar(v, mean_var[:, t0:t1, 1], EPS, None, ALU.add))
                    step(V.tensor_scalar(bits, v.bitcast(i32), 1, None, ALU.logical_shift_right))
                    step(V.tensor_scalar(y.bitcast(i32), bits, -1.0, RSQRT_SEED, ALU.mult, ALU.add))
                elif part < 6:
                    step(V.tensor_tensor(r, y, y, ALU.mult))
                    step(V.tensor_tensor(r, r, v, ALU.mult))
                    step(V.tensor_scalar(r, r, -0.5, 1.5, ALU.mult, ALU.add))
                    step(V.tensor_tensor(y, y, r, ALU.mult))
                else:
                    for i in tiles:
                        last = V.tensor_scalar(x_res[:, i, :], y_acc[:, i, :], mean_var[:, i, 0:1], rs_y[:, i:i + 1],
                                               ALU.subtract, ALU.mult)
                    if done is None:
                        step(last)
                    else:
                        last.then_inc(done, 1)

            def normalise(tiles, step, done=None):
                for part in range(7):
                    norm_part(part, tiles, step, done)

            EARLY, LATE = tuple(range(TILES - 2)), (TILES - 2, TILES - 1)

            def early_norm(S, h, step):
                if h == 2:
                    dve.wait_ge(*S("y_ready", BATCH - 1))
                if 2 <= h < 9:
                    norm_part(h - 2, EARLY, step, S["x_ready"])

            def late_norm(S, stage):
                dve.wait_ge(*S("y_ready", BATCH))
                normalise(LATE, Steps(dve, steps["ln"], stage, 17), S["x_ready"])

            def add_rows(S, b):
                dve.wait_ge(*S("proj_psum", b + 1))
                dve.wait_ge(*S("xbo_ready", b + 1))
                V.tensor_tensor(y_acc[:, bass.ds(b * 2, 2), :], bank[PROJ_BANK][:].rearrange("p (i d) -> p i d", i=2),
                                xbo, ALU.add).then_inc(S["y_ready"], 1)

            dve.wait_ge(const_loaded, 32)
            V.tensor_copy(ident_b[:], ident).then_inc(const_ready, 1)
            V.tensor_copy(ident_h[:], ident).then_inc(const_ready, 1)
            V.tensor_copy(causal_b[:], const[:, C_CAUSAL:C_CAUSAL + 128]).then_inc(const_ready, 1)
            V.tensor_copy(tri_b[:], const[:, C_TRI:C_TRI + 128])
            V.tensor_copy(causal_h[:].rearrange("p i k -> p (i k)"), causal_f)
            V.memset(ones_b[:], 1.0)
            V.memset(ones_f[:], 1.0)
            V.memset(v32, 0.0).then_inc(zeroed, 1)
            dve.wait_ge(zeroed, 1)
            V.memset(v32[:, :, :, HEAD_DIM], 1.0).then_inc(const_ready, 1)
            V.memset(zeros[:], 0.0).then_inc(zeroed, 1)
            dve.wait_ge(w_loaded[0], LOADS[0])
            V.tensor_scalar(qbias[0][:], bias_col["L0_attn_b_attn"][:, 0:2], SCALE, None, ALU.mult).then_inc(const_ready, 1)

            S = SELF0

            def before(b):
                dve.wait_ge(*S("k_psum", b + 1))
                dve.wait_ge(*S("km_ready", b * CHUNKS))
                for c in range(CHUNKS):
                    last = V.tensor_scalar(kT[:, c, :], bank[K_BANK][:, c * 256:(c + 1) * 256],
                                           bias_col["L0_attn_b_attn"][:, 2 + c:3 + c], None, ALU.add)
                last.then_inc(S["k_ready"], 1)

            def heads(b, more):
                step = Steps(dve, steps["self0_norm"], b, GROUPS)
                early = Steps(dve, steps["early_ln"], 0, 17)
                for h in range(HEADS + 5):
                    if not more:
                        early_norm(S, h, early)
                    if h < HEADS:
                        dve.wait_ge(*S("s_psum", b * HEADS + h + 1))
                        s = bank[S_BANKS[h % 3]]
                        V.tensor_reduce(neg_max[:, h, 0:1], s[:, 0:128], AX.X, ALU.max, negate=True)
                        V.tensor_reduce(neg_max[:, h, 1:2], s[:, 128:384], AX.X, ALU.max, negate=True)\
                            .then_inc(S["max_ready"], 1)
                    if 2 <= h < HEADS + 2:
                        dve.wait_ge(*S("pT_psum", b * HEADS + h - 1))
                        if h >= 4:
                            dve.wait_ge(*S("pv_psum", b * HEADS + h - 3))
                        V.tensor_copy(probsT[h % 2][:, 0:384], bank[PT_BANKS[h % 2]][:, 0:384]).then_inc(S["pT_ready"], 1)
                    if h >= 8 and h % 4 == 0:
                        normalise_group(S, b, h // 4 - 2, step)
                step.done()

            batches(dve, before, heads, lambda b: add_rows(S, b))
            late_norm(S, 0)

            dve.wait_ge(w_loaded[1], LOADS[1])
            V.tensor_scalar(qbias[1][:], bias_col["L0_xattn_bq"], SCALE, None, ALU.mult).then_inc(qbias1_ready, 1)
            V.memset(v32[:, 0], 0.0).then_inc(ctx_sems["zeroed"], 1)
            dve.wait_ge(ctx_sems["zeroed"], 1)
            for a in range(2):
                last = V.memset(v32[64 * a:64 * a + 64, 0, a::2, HEAD_DIM], 1.0)
            last.then_inc(ctx_sems["zeroed"], 1)
            dve.wait_ge(ctx_sems["zeroed"], 2)
            dve.wait_ge(ctx_sems["v_ready"], 1)
            S = CROSS0

            def before(b):
                for a in range(2):
                    pp = slice(64 * a, 64 * a + 64)
                    last = V.tensor_copy(v32[pp, 0, a::2, 0:HEAD_DIM],
                                         cv[pp, bass.ds(b, 1), :].rearrange("p o (h a d) -> p (o h) a d", a=2, d=HEAD_DIM)[:, :, a, :])
                last.then_inc(S["v_ready"], 1)

            def heads(b, more):
                step = Steps(dve, steps["cross0_heads"], b, 2 * GROUPS)
                early = Steps(dve, steps["early_ln"], 1, 17)
                for i in range(GROUPS + 4):
                    if not more:
                        early_norm(S, i + 2, early)
                    if i < GROUPS:
                        dve.wait_ge(*S("s_psum", b * GROUPS + i + 1))
                        if i == 3:
                            dve.wait_ge(*S("pT_psum", b * GROUPS + 1))
                        s = bank[S_BANKS[i % 3]][:].rearrange("p (i m k) -> p i m k", i=2, m=4)
                        m = neg_max[:, 4 * i:4 * i + 4, :].rearrange("p m i -> p i m")
                        step(V.tensor_reduce(m, s, AX.X, ALU.max, negate=True))
                        V.tensor_tensor(probs[i % 3][:].rearrange("p (i m k) -> p i m k", i=2, m=4), s,
                                        m.unsqueeze(3).to_broadcast([128, 2, 4, CTX]), ALU.add)\
                            .then_inc(S["shift_ready"], 1)
                    if i >= 4:
                        normalise_group(S, b, i - 4, step)
                step.done()

            batches(dve, before, heads, lambda b: add_rows(S, b))
            late_norm(S, 1)

            def route(S, moe, step, beside=lambda n: None):
                E, K = moe.experts, moe.picks
                TK = TILES * K
                lg, bi, ew = logits[:, :, 0:E], biased[:, :, 0:E], expw[:, :, 0:E]
                oh, pr = onehot[:, 0:TK, 0:E], product[:, 0:TK, 0:E]
                by_tile = lambda x: x.rearrange("p (i k) e -> p i k e", k=K)
                each_pick = lambda x: x.unsqueeze(2).to_broadcast([128, TILES, K, E])
                if moe is MOE0:
                    step(V.tensor_tensor(bi, lg, router_bias[:, 0:E].unsqueeze(1).to_broadcast([128, TILES, E]), ALU.add))
                else:
                    step(V.tensor_copy(bi, lg))
                for i in range(TILES):
                    last = V.max(top8[:, i, :], bi[:, i, :])
                step(last)
                for i in range(TILES):
                    last = V.max_index(top8_i[:, i, :], top8[:, i, :], bi[:, i, :])
                step(last)
                beside(0)
                step(V.tensor_copy(top_f[:, 0:TK].rearrange("p (i k) -> p i k", k=K), top8_i[:, :, 0:K]))
                step(V.tensor_tensor(oh, iota_e[:, 0:E].unsqueeze(1).to_broadcast([128, TK, E]),
                                     top_f[:, 0:TK].unsqueeze(2).to_broadcast([128, TK, E]), ALU.is_equal))
                with nc.allow_low_precision("the mask is 0 or 1"):
                    V.tensor_reduce(mask_b[:, :, 0:E], oh.rearrange("p (i k) e -> p i e k", k=K), AX.X, ALU.add)\
                        .then_inc(S["mask_ready"], 1)
                beside(1)
                step(V.tensor_reduce(row_t[0], lg, AX.X, ALU.max))
                V.tensor_tensor(ew, lg, row_t[0].unsqueeze(2).to_broadcast([128, TILES, E]), ALU.subtract)\
                    .then_inc(S["exp_in"], 1)
                dve.wait_ge(*S("exp_ready", 1))
                step(V.tensor_tensor(by_tile(pr), by_tile(oh), each_pick(ew), ALU.mult))
                step(V.tensor_reduce(picked[:, :, 0:K], by_tile(pr), AX.X, ALU.add))
                step(V.tensor_reduce(row_t[1], picked[:, :, 0:K], AX.X, ALU.add))
                step(V.reciprocal(row_t[2], row_t[1]))
                step(V.tensor_tensor(pick_w[:, :, 0:K], picked[:, :, 0:K],
                                     row_t[2].unsqueeze(2).to_broadcast([128, TILES, K]), ALU.mult))
                beside(2)
                dve.wait_ge(*S("rank_psum", 1))
                cnt, tiles, upto, first, _ = [c[:, 0:E] for c in counts]
                ci, ti = [c[:, 0:E] for c in counts_i]
                step(V.tensor_scalar(ci, bank[1][:, 0:E], float(TILE - 1), None, ALU.add))
                step(V.tensor_scalar(ti, ci, TILE.bit_length() - 1, None, ALU.logical_shift_right))
                step(V.tensor_copy(tiles, ti))
                step(V.tensor_tensor_scan(upto, ones_f[:, 0:E], tiles, 0.0, ALU.mult, ALU.add))
                step(V.tensor_tensor(first, upto, tiles, ALU.subtract))
                step(V.tensor_scalar(first, first, float(TILE), None, ALU.mult))
                sb_ = slot_base[:, :, 0:E]
                step(V.tensor_tensor(sb_, bank[0][:, 0:TILES * E].rearrange("p (i e) -> p i e", i=TILES),
                                     first.unsqueeze(1).to_broadcast([128, TILES, E]), ALU.add))
                step(V.tensor_tensor(by_tile(pr), by_tile(oh), each_pick(sb_), ALU.mult))
                step(V.tensor_reduce(pos_f[:, 0:TK], pr, AX.X, ALU.add))
                step(V.tensor_copy(pos[:, 0:TK], pos_f[:, 0:TK]))
                dve.sem_inc(S["placed"], 1)
                step(V.tensor_scalar(counts[4][:, 0:E], upto, const[:, C_ROW:C_ROW + 1], None, ALU.is_le))
                step(V.tensor_reduce(e_col[0], counts[4][:, 0:E], AX.X, ALU.add))
                step(V.tensor_scalar(e_col[1], e_col[0], float(E - 1), None, ALU.min))
                V.tensor_scalar(e_diag, ident, e_col[1], None, ALU.mult).then_inc(S["e_ready"], 1)
                beside(3)
                dve.wait_ge(*S("e_psum", 1))
                step(V.tensor_copy(tile_expert[:, 0, :], bank[2][:, 0:128]))
                step(V.tensor_scalar(tile_expert[:, 1, :], tile_expert[:, 0, :], 1, None, ALU.logical_shift_right))
                step(V.tensor_scalar(e_par, tile_expert[:, 0, :], 1, None, ALU.bitwise_and))
                step(V.tensor_scalar(tile_half[:], e_par, const[:, C_HALF:C_HALF + 1], None, ALU.is_equal))
                n_turns = moe.tiles // 4
                step(V.tensor_copy(turn_experts[:, 1:n_turns, 0:4],
                                   tile_expert[:, 0, 3:3 + 4 * (n_turns - 1)].rearrange("p (q u) -> p q u", u=4)))
                step(V.tensor_copy(turn_experts[:, 1:n_turns, 4:8],
                                   tile_expert[:, 1 if moe is MOE0 else 0, 1:1 + 4 * (n_turns - 1)].rearrange("p (q u) -> p q u", u=4)))
                dve.sem_inc(S["routed"], 1)

            def expert_tiles(S, moe):
                H = moe.hidden
                small = moe is MOE0

                def turn(j, u, second=True, third=True, fourth=True, early=0, stored=None):
                    if second:
                        a = (u + 1) % 2
                        dve.wait_ge(*S("act_ready", j))
                        if early == 0 or early > 3:
                            dve.wait_ge(*S("hT_psum", j - 2))
                        if small:
                            V.tensor_tensor(hid[a][:, 0:128].rearrange("p (a n) -> p a n", a=2),
                                            silu_g[a][:, 0:H].unsqueeze(1).to_broadcast([128, 2, H]),
                                            bank[2 + a][:, H:2 * H].unsqueeze(1).to_broadcast([128, 2, H]), ALU.mult)\
                                .then_inc(S["h_ready"], 1)
                        else:
                            V.tensor_tensor(hid[a], silu_g[a], bank[4 + a][:], ALU.mult).then_inc(S["h_ready"], 1)
                    if third:
                        dve.wait_ge(*S("hT_psum", j - 1))
                        if early == 0 or early > 4:
                            dve.wait_ge(*S("y_psum", j - 3))
                        if small:
                            V.tensor_scalar(hidT[u % 2][:, 0:128], bank[moe.hT_banks[u % 2]][:, 0:128], tile_half[:, bass.ds(j - 2, 1)],
                                            None, ALU.mult).then_inc(S["hT_ready"], 1)
                        else:
                            V.tensor_copy(hidT[u % 2], bank[moe.hT_banks[0]][:]).then_inc(S["hT_ready"], 1)
                    if fourth:
                        v = (u + 1) % 4
                        dve.wait_ge(*S("y_psum", j - 2))
                        if early == 0:
                            dve.wait_ge(*S("stored", (j - 3) // 4 * 16 if stored is None else stored, v))
                        V.tensor_copy(y_tile[v], bank[moe.y_banks[(u + 1) % 2]][:, 0:DIM]).then_inc(S["y_copied"], 1)

                for j in range(1, 4):
                    turn(j, j, third=j >= 2, fourth=j >= 3, early=j)
                for j in range(4, 8):
                    turn(j, j % 4, early=j if j < 7 else 0)
                with dve.Fori(2, moe.tiles // 4) as q:
                    for u in range(4):
                        turn(q * 4 + u, u, stored=q * 16 - 16 if u < 3 else q * 16)
                for u in range(3):
                    turn(moe.tiles + u, u, second=u == 0, third=u <= 1)

            def combine(S, moe, step, first, beside=lambda: None):
                for n in range(TILES * moe.picks):
                    i, k = n // moe.picks, n % moe.picks
                    if (i, k) == (TILES - 2, 0):
                        beside()
                    dve.wait_ge(*S("fetched", 16 * (n // 8 + 1), n % 8))
                    ins = V.scalar_tensor_tensor(y_acc[:, i, :], y_pick[n % 8], pick_w[:, i, k:k + 1], y_acc[:, i, :],
                                                 ALU.mult, ALU.add)
                    ins.then_inc(S["summed"], 1)
                    dve.wait_ge(*S("summed", n + 1))
                    if n % (2 * moe.picks) == 2 * moe.picks - 1:
                        normalise((i - 1, i), step, S["x_ready"] if i in (first, TILES - 1) else None)

            def collect_logits(S, moe):
                with dve.Fori(0, BATCH) as b:
                    dve.wait_ge(*S("logit_psum", b + 1))
                    V.tensor_copy(logits[:, bass.ds(b * 2, 2), 0:moe.experts],
                                  bank[K_BANK][:, 0:128].rearrange("p (i e) -> p i e", i=2)[:, :, 0:moe.experts])\
                        .then_inc(S["logit_ready"], 1)
                dve.wait_ge(*S("logit_ready", BATCH))

            S = FFN0
            collect_logits(S, MOE0)
            dve.wait_ge(router_loaded[0], 32)
            step = Steps(dve, steps["ffn0"], 0, None)

            def hidden(b, hcs=range(4)):
                for hc in hcs:
                    dve.wait_ge(*S("silu_ready", b * 4 + hc + 1))
                    if hc == 0:
                        dve.wait_ge(*S("sum_psum", b))
                    V.tensor_tensor(hidden_s[:, hc, :], silu_s[hc % 2], bank[4 + hc % 2][:, 256:512], ALU.mult)\
                        .then_inc(S["hid_ready"], 1)

            def summed(b):
                dve.wait_ge(*S("sum_psum", b + 1))
                for i in range(2):
                    last = V.tensor_tensor(y_acc[:, 2 * b + i, :], bank[6 + i][:, 0:256], x_res[:, 2 * b + i, :], ALU.add)
                last.then_inc(S["y_init"], 1)

            parts = (lambda: hidden(0, (0, 1)), lambda: hidden(0, (2, 3)), lambda: summed(0), lambda: hidden(1))
            route(S, MOE0, step, lambda n: parts[n]())
            summed(1)
            for b in (2, 3):
                hidden(b)
                summed(b)
            expert_tiles(S, MOE0)
            dve.wait_ge(*S("y_init", BATCH))

            def blocks_T(src, dst):
                for st in range(2):
                    last = V.transpose(dst[st].rearrange("p a j i -> p j a i"),
                                       src[:, st, :].rearrange("p (j d) -> p j d", d=HEAD_DIM).unsqueeze(2)
                                       .to_broadcast([128, HEADS, 2, HEAD_DIM]))
                return last

            def keys_and_queries_T(b, step):
                dve.wait_ge(*QKV1("tok_ready", b * 3 + 1))
                dve.wait_ge(*SELF1("km_ready", b * CHUNKS))
                step(blocks_T(k_tok, dup_k))
                dve.sem_inc(QKV1["qkv_ready"], 1)
                dve.sem_inc(SELF1["k_ready"], 1)
                dve.wait_ge(*QKV1("tok_ready", b * 3 + 2))
                step(blocks_T(q_tok, dup))
                dve.sem_inc(QKV1["qkv_ready"], 1)

            def values_T(b, step):
                dve.wait_ge(*QKV1("tok_ready", b * 3 + 3))
                step(blocks_T(v_tok, dup_v))
                dve.sem_inc(QKV1["qkv_ready"], 1)
                step.done()

            first_in = Steps(dve, steps["self1_in"], 0, 3)

            def self1_in():
                V.memset(v32, 0.0).then_inc(ctx_sems["zeroed"], 1)
                dve.wait_ge(ctx_sems["zeroed"], 3)
                V.memset(v32[:, :, :, HEAD_DIM], 1.0).then_inc(ctx_sems["zeroed"], 1)
                dve.wait_ge(ctx_sems["zeroed"], 4)
                keys_and_queries_T(0, first_in)

            combine(S, MOE0, step, 1, self1_in)

            def by_head(src, dst, step):
                step(blocks_T(src, dup))
                for st in range(2):
                    last = V.tensor_scalar(dst(st), dup[st][:, 0], parity[:, 0:1], None, ALU.mult)
                step(last)
                for st in range(2):
                    last = V.scalar_tensor_tensor(dst(st), dup[st][:, 1], parity[:, 1:2], dst(st), ALU.mult, ALU.add)
                step(last)

            def full_heads(S, b, step, quantised, more):
                early = Steps(dve, steps["early_ln"], 3 if quantised else 2, 17)
                for h in range(HEADS + 5):
                    if not more:
                        early_norm(S, h, early)
                    if h < HEADS:
                        dve.wait_ge(*S("s_psum", b * HEADS + h + 1))
                        ins = V.tensor_reduce(neg_max[:, h, :], bank[S_BANKS[h % 3]][:].rearrange("p (i k) -> p i k", i=2),
                                              AX.X, ALU.max, negate=True)
                        if quantised:
                            step(ins)
                            ins = V.tensor_tensor(shift[:, h, :], neg_max[:, h, :], q_scale[:, :, h], ALU.mult)
                        ins.then_inc(S["max_ready"], 1)
                    if 2 <= h < HEADS + 2:
                        if quantised and not by_dve(h - 2):
                            dve.wait_ge(*S("shift_ready", b * shifted_by_act(HEADS - 1) + shifted_by_act(h - 2)))
                        else:
                            dve.wait_ge(*S("pT_psum", b * HEADS + h - 1))
                        if h >= 4:
                            dve.wait_ge(*S("pv_psum", b * HEADS + h - 3))
                        if quantised and by_dve(h - 2):
                            step(V.tensor_scalar(p_shifted[h % 2], bank[PT_BANKS[h % 2]][:], PROB_LEVELS, ROUND,
                                                 ALU.mult, ALU.add))
                        if quantised:
                            with nc.allow_low_precision("whole numbers up to 255 are exact"):
                                V.tensor_scalar(probsT_b[h % 2], p_shifted[h % 2], ROUND, None, ALU.subtract)\
                                    .then_inc(S["pT_ready"], 1)
                        else:
                            V.tensor_copy(probsT[h % 2], bank[PT_BANKS[h % 2]][:]).then_inc(S["pT_ready"], 1)
                    if h >= 8 and h % 4 == 0:
                        normalise_group(S, b, h // 4 - 2, step, summed=quantised)

            S = SELF1
            by_pos = lambda a: (lambda st: a[:, st, :].rearrange("p (j i) -> p j i", i=16))

            def before(b):
                step = Steps(dve, steps["self1_in"], b, 3)
                keys_and_queries_T(b, step)
                values_T(b, step)

            def heads(b, more):
                step = Steps(dve, steps["self1_norm"], b, GROUPS)
                full_heads(S, b, step, False, more)
                step.done()
                dve.wait_ge(*S("o_ready", (b + 1) * GROUPS))
                step = Steps(dve, steps["self1_out"], b, 3)
                by_head(o_tok, by_pos(oT), step)
                dve.sem_inc(S["oT_ready"], 1)
                step.done()

            heads_of = lambda x: x.rearrange("p i (h d) -> p i h d", h=HEADS)

            def quantise(x, s, step):
                step(V.tensor_reduce(s, heads_of(x), AX.X, ALU.max, apply_absolute_value=True))
                step(V.tensor_scalar(s, s, 1 / LEVELS, 1e-8, ALU.mult, ALU.max))
                step(V.reciprocal(inv_scale, s))
                step(V.tensor_tensor(heads_of(x), heads_of(x), inv_scale.unsqueeze(3).to_broadcast([128, 2, HEADS, HEAD_DIM]),
                                     ALU.mult))
                step(V.tensor_scalar(x, x, ROUND, ROUND + LEVELS, ALU.add, ALU.min))

            def context_kv():
                step = Steps(dve, steps["kv1"], 0, None)
                V.memset(v32_b, 0.0).then_inc(kv1_sems["zeroed"], 1)
                dve.wait_ge(w_loaded[3], LOADS[3])
                dve.wait_ge(kv1_sems["k_psum"], 1)
                step(V.tensor_tensor(k_int, bank[K_BANK][:].rearrange("p (i d) -> p i d", i=2),
                                     bias_row["L1_xattn_bk_row"][:, 0:DIM].unsqueeze(1).to_broadcast([128, 2, DIM]), ALU.add))
                quantise(k_int, k_scale, step)
                step(V.tensor_scalar(k_int, k_int, ROUND - LEVELS, ROUND, ALU.max, ALU.subtract))
                step(V.tensor_tensor(heads_of(k_int), heads_of(k_int), k_scale.unsqueeze(3)
                                     .to_broadcast([128, 2, HEADS, HEAD_DIM]), ALU.mult))
                rows = k_int.rearrange("p i (h d) -> p (i h) d", h=HEADS)
                with nc.allow_low_precision("the parts add up to the whole float32"):
                    step(V.tensor_copy(expanded[:, :, 0, :], rows))
                    step(V.tensor_tensor(rows, rows, expanded[:, :, 0, :], ALU.subtract))
                    step(V.tensor_copy(expanded[:, :, 1, :], rows))
                    step(V.tensor_tensor(rows, rows, expanded[:, :, 1, :], ALU.subtract))
                    step(V.tensor_copy(expanded[:, :, 2, :], rows))
                    step(V.memset(expanded[:, :, 3, :], 0.0))
                dve.sem_inc(kv1_sems["k_ready"], 1)
                dve.wait_ge(kv1_sems["v_psum"], 1)
                for c in range(CHUNKS):
                    last = V.tensor_scalar(vq[:, c, :], bank[V_BANK][:, c * 256:(c + 1) * 256],
                                           bias_col["L1_xattn_bkv"][:, 2 + c:3 + c], None, ALU.add)
                step(last)
                step(V.tensor_reduce(v_scale, vq, AX.X, ALU.max, apply_absolute_value=True))
                step(V.tensor_scalar(v_scale, v_scale, 1 / LEVELS, 1e-8, ALU.mult, ALU.max))
                step(V.reciprocal(v_inv, v_scale))
                for c in range(CHUNKS):
                    last = V.tensor_scalar(vq[:, c, :], vq[:, c, :], v_inv[:, c:c + 1], ROUND, ALU.mult, ALU.add)
                step(last)
                step(V.tensor_scalar(vq, vq, ROUND + LEVELS, ROUND - LEVELS, ALU.min, ALU.max))
                step(V.tensor_scalar(vq, vq, ROUND, None, ALU.subtract))
                dve.sem_inc(kv1_sems["vq_ready"], 1)
                step(V.tensor_scalar(v_scale, v_scale, 1 / PROB_LEVELS, None, ALU.mult))
                step(V.tensor_scalar(bias_row["L1_xattn_bq"], bias_row["L1_xattn_bq"], SCALE, None, ALU.mult))

            batches(dve, before, heads, lambda b: add_rows(S, b), last=context_kv,
                    start=lambda b: values_T(b, first_in))
            late_norm(S, 2)

            S = CROSS1

            def before(b):
                step = Steps(dve, steps["cross1_in"], b, 7)
                dve.wait_ge(*S("q_psum", b + 1))
                step(V.scalar_tensor_tensor(q_int, bank[Q_BANK][:].rearrange("p (i d) -> p i d", i=2), SCALE,
                                            bias_row["L1_xattn_bq"].unsqueeze(1).to_broadcast([128, 2, DIM]),
                                            ALU.mult, ALU.add))
                quantise(q_int, q_scale, step)
                dve.wait_ge(*PARTS1("psum", b * 4 + 4))
                with nc.allow_low_precision("whole numbers up to 127 are exact"):
                    step(V.tensor_scalar(expanded, q_int.rearrange("p i (h d) -> p (i h) d", h=HEADS).unsqueeze(2)
                                         .to_broadcast([128, 2 * HEADS, 4, HEAD_DIM]), ROUND - LEVELS, ROUND,
                                         ALU.max, ALU.subtract))
                dve.sem_inc(S["k_ready"], 1)
                step.done()

            def heads(b, more):
                step = Steps(dve, steps["cross1_heads"], b, HEADS + GROUPS + HEADS // 4)
                full_heads(S, b, step, True, more)
                step.done()

            batches(dve, before, heads, lambda b: add_rows(S, b))
            late_norm(S, 3)

            S = FFN1
            collect_logits(S, MOE1)
            V.tensor_copy(y_acc[:], x_res[:]).then_inc(S["y_init"], 1)
            step = Steps(dve, steps["ffn1"], 0, None)
            route(S, MOE1, step)
            expert_tiles(S, MOE1)
            dve.wait_ge(*S("y_init", 1))
            combine(S, MOE1, step, TILES - 3)

        @block.gpsimd
        def _(pool):
            P = nc.gpsimd
            for signals in (SELF0, FFN0, QKV1, PARTS1):
                for n, s in signals.sems.items():
                    if n not in signals.by_dma:
                        pool.sem_inc(s, 1)

            def residual_rows(S, b, bias):
                pool.wait_ge(*S("xb_ready", b + 1))
                pool.wait_ge(*S("y_ready", b))
                P.tensor_tensor(xbo[:], xb[:], bias[:].unsqueeze(1).to_broadcast([128, 2, DIM]), ALU.add)\
                    .then_inc(S["xbo_ready"], 1)

            def masked_keys(S, b, src, n):
                for c in range(CHUNKS):
                    P.tensor_tensor(kTm[:, c, :, 0:n], src(c).to_broadcast([128, 4, n]),
                                    head_mask.unsqueeze(2).to_broadcast([128, 4, n]), ALU.mult)\
                        .then_inc(S["km_ready"], 1)

            pool.wait_ge(const_loaded, 32)
            pool.wait_ge(w_loaded[0], LOADS[0])
            S = SELF0
            with pool.Fori(0, BATCH) as b:
                pool.wait_ge(*S("k_ready", b + 1))
                masked_keys(S, b, lambda c: kT[:, c:c + 1, :], SEQ)
                residual_rows(S, b, bias_row["L0_attn_b_proj"])
            pool.wait_ge(w_loaded[1], LOADS[1])
            pool.wait_ge(ctx_sems["k_ready"], 1)
            S = CROSS0
            with pool.Fori(0, BATCH) as b:
                pool.wait_ge(*S("s_psum", b * GROUPS))
                masked_keys(S, b, lambda c: ckT[:, c:c + 1, bass.ds(b * CTX, CTX)], CTX)
                residual_rows(S, b, bias_row["L0_xattn_bo"])

            def send_rows(S, moe):
                pool.wait_ge(*S("placed", 1))
                pool.wait_ge(zero_filled, 16 * (MOE0.tiles + MOE1.tiles) // 8)
                for n in range(TILES * moe.picks):
                    P.indirect_dma_start(out=sorted_x[moe.stage],
                                         out_offset=bass.IndirectOffsetOnAxis(ap=pos[:, n:n + 1], axis=0),
                                         in_=x_res[:, n // moe.picks, :], in_offset=None).then_inc(S["sent"], 16)

            def fetch_outputs(S, moe):
                for v in range(4):
                    pool.wait_ge(*S("stored", 16 * moe.tiles // 4, v))
                for n in range(TILES * moe.picks):
                    if n >= 8:
                        pool.wait_ge(*S("summed", n - 7))
                    P.indirect_dma_start(out=y_pick[n % 8], out_offset=None, in_=sorted_y[moe.stage],
                                         in_offset=bass.IndirectOffsetOnAxis(ap=pos[:, n:n + 1], axis=0))\
                        .then_inc(S["fetched"][n % 8], 16)

            send_rows(FFN0, MOE0)
            fetch_outputs(FFN0, MOE0)
            S = SELF1
            with pool.Fori(0, BATCH) as b:
                pool.wait_ge(*S("k_ready", b + 1))
                for st in range(2):
                    for a in range(2):
                        last = P.tensor_tensor(
                            kTm[:, st, 2 * a:2 * a + 2, :].rearrange("p e (j i) -> p e j i", i=16),
                            dup_k[st],
                            head_mask[:, 2 * a:2 * a + 2].unsqueeze(2).unsqueeze(3).to_broadcast([128, 2, 16, 16]), ALU.mult)
                    last.then_inc(S["km_ready"], 1)
                residual_rows(S, b, zeros[:])
            S = CROSS1
            pool.wait_ge(w_loaded[3], LOADS[3])
            with pool.Fori(0, BATCH) as b:
                residual_rows(S, b, bias_row["L1_xattn_bp"])
            send_rows(FFN1, MOE1)
            fetch_outputs(FFN1, MOE1)


_TRANSPOSED = ("L0_xattn_Wq", "L0_xattn_Wk", "L0_xattn_Wv", "L0_xattn_Wo")


def _constants(np):
    c = np.zeros((128, C_COLS), np.float32)
    p = np.arange(128)
    c[:, C_IDENT:C_IDENT + 128] = np.eye(128)
    c[:, C_CAUSAL:C_CAUSAL + 128] = np.where(p[None, :] <= p[:, None], 0.0, -1e30)
    c[:, C_TRI:C_TRI + 128] = p[:, None] < p[None, :]
    s = np.arange(256)
    s = s % 16 * 16 + s // 16
    c[:, C_CAUSAL1:C_COLS] = np.where(s[None, :] <= s[:, None], 1.0, -10000.0).reshape(2, 128, 256)\
        .transpose(1, 0, 2).reshape(128, 512)
    c[:, C_HALF] = p // 64
    c[:, C_ROW] = p
    c[:, C_IOTA:C_IOTA + 64] = np.arange(64)
    c[:, C_HEADMASK:C_HEADMASK + 4] = (p[:, None] % 64 // 16 == np.arange(4)[None, :])
    c[:, C_PARITY:C_PARITY + 2] = (p[:, None] // 16 % 2 == np.arange(2)[None, :])
    return c


def _program(nc, inputs):
    import numpy as np

    arrays, tensors = {}, {}
    host = {n: np.asarray(a) for n, a in inputs.items() if "decoder_" not in n}
    host["x"] = host["x"].reshape(-1, DIM)
    host["ctx_2048"] = host["ctx_2048"].reshape(-1, DIM)
    for n in _TRANSPOSED:
        host[n] = host[n].T
    swg, swu, wg, wu = [host.pop(f"L0_ffn_{n}") for n in ("swg", "swu", "wg", "wu")]
    host["L0_ffn_swg"] = swg.transpose(1, 0, 2).reshape(DIM, SHARED_HIDDEN)
    host["L0_ffn_swu"] = swu.transpose(1, 0, 2).reshape(DIM, SHARED_HIDDEN)
    host["L0_ffn_swd"] = host["L0_ffn_swd"].reshape(SHARED_HIDDEN, DIM)
    gu = np.concatenate([wg, wu], axis=2)
    host["expert_in0"] = gu.reshape(64, CHUNKS, 128, 128).transpose(2, 0, 1, 3).reshape(128, -1)
    host["expert_out0"] = host.pop("L0_ffn_wd").reshape(32, 128, DIM).transpose(1, 0, 2).reshape(128, -1)
    gu = np.concatenate([host.pop("L1_ffn_w0"), host.pop("L1_ffn_w1")], axis=2)
    host["expert_in1"] = gu.reshape(8, CHUNKS, 128, 1024).transpose(2, 0, 1, 3).reshape(128, -1)
    host["expert_out1"] = host.pop("L1_ffn_wo").reshape(8, 4, 128, DIM).transpose(2, 0, 1, 3).reshape(128, -1)
    host["L1_xattn_bk_row"] = host["L1_xattn_bkv"]
    for n in BIAS_COL:
        host[n] = host[n].reshape(-1, 128).T
    host["const"] = _constants(np)
    for n, a in host.items():
        a = np.ascontiguousarray(a)
        arrays[f"in_{n}"] = a
        tensors[n] = nc.dram_tensor(f"in_{n}", a.shape, mybir.dt.from_np(a.dtype), kind="ExternalInput").ap()
    out = nc.dram_tensor("out", (BATCH * SEQ, DIM), mybir.dt.float32, kind="ExternalOutput").ap()
    decoder_kernel(nc, tensors, out)
    return arrays


def kernel(**inputs):
    import concourse.bacc as bacc
    from concourse.bass_utils import run_bass_kernel_spmd

    nc = bacc.Bacc("TRN2", target_bir_lowering=False, num_devices=1)
    arrays = _program(nc, inputs)
    r = run_bass_kernel_spmd(nc, [arrays], core_ids=[0])
    return r.results[0]["out"].reshape(BATCH, SEQ, DIM)
```
